# Optimizing a Trainium2 kernel written in Bass

```python
import numpy as np
import jax
import jax.numpy as jnp

def _softmax(x, axis=-1):
    return jax.nn.softmax(x, axis=axis)

def _gelu(x):
    return jax.nn.gelu(x, approximate=True)

def _silu(x):
    return jax.nn.silu(x)

def _sigmoid(x):
    return jax.nn.sigmoid(x)

def _layernorm(x, axis=-1, eps=1e-05):
    m = jnp.mean(x, axis=axis, keepdims=True)
    v = jnp.var(x, axis=axis, keepdims=True)
    return (x - m) / jnp.sqrt(v + eps)

def _scatter_add(tgt, idx, src, axis=0):
    return tgt.at[idx].add(src)

def _segment_sum(src, seg, n):
    return jax.ops.segment_sum(src, seg, n)
kernel_name = 'mk_gnn_preln_d4_gnn_r8_fb009f'

def setup_inputs(seed: int=0):
    np.random.seed(seed)
    _w = jnp.asarray

    def _rec_inputs():
        import jax
        import jax.numpy as jnp
        _gk = jax.random.key(seed)
        x = -6.415e-05 + 1 * jax.random.normal(jax.random.fold_in(_gk, 1), (1250, 512), jnp.float32)
        src = jax.random.randint(jax.random.fold_in(_gk, 2), (40000,), 0, 1250, jnp.int32)
        dst = jax.random.randint(jax.random.fold_in(_gk, 3), (40000,), 0, 1250, jnp.int32)
        _o = jnp.argsort(dst, stable=True)
        src = src[_o]
        dst = dst[_o]
        return (x, src, dst)
    x, src, dst = _rec_inputs()

    def _L0_gnn_setup():
        import jax, jax.numpy as jnp
        import numpy as np
        N_NODES = 2500
        N_EDGES = 40000
        D = 512
        L = 3
        key = jax.random.key(seed)
        ks = jax.random.split(key, 6)
        x = jax.random.normal(ks[0], (N_NODES, D), dtype=jnp.float32)
        Ws_self = jax.random.normal(ks[1], (L, D, D), dtype=jnp.float32) * 0.05
        Ws_neigh = jax.random.normal(ks[2], (L, D, D), dtype=jnp.float32) * 0.05
        bs = jax.random.normal(ks[3], (L, D), dtype=jnp.float32) * 0.05
        src = jax.random.randint(ks[4], (N_EDGES,), 0, N_NODES, dtype=jnp.int64)
        dst = jax.random.randint(ks[5], (N_EDGES,), 0, N_NODES, dtype=jnp.int64)
        return {'x': x, 'Ws_self': Ws_self, 'Ws_neigh': Ws_neigh, 'bs': bs, 'src': src, 'dst': dst}
    _L0_gnn_all = _L0_gnn_setup()
    _L0_gnn_in = {k: v for k, v in _L0_gnn_all.items() if k in ('Ws_self', 'Ws_neigh', 'bs')}
    del _L0_gnn_all

    def _L1_gnn_setup():
        import jax, jax.numpy as jnp
        import numpy as np
        N_NODES = 6250
        N_EDGES = 100000
        D = 512
        N_LAYERS = 3
        EPS = 1e-12
        key = jax.random.key(seed)
        ks = jax.random.split(key, 6)
        x = jax.random.normal(ks[0], (N_NODES, D), dtype=jnp.float32)
        src = jax.random.randint(ks[1], (N_EDGES,), 0, N_NODES, dtype=jnp.int64)
        dst = jax.random.randint(ks[2], (N_EDGES,), 0, N_NODES, dtype=jnp.int64)
        scale = 1.0 / np.sqrt(D)
        W_self = jax.random.normal(ks[3], (N_LAYERS, D, D), dtype=jnp.float32) * scale
        W_neigh = jax.random.normal(ks[4], (N_LAYERS, D, D), dtype=jnp.float32) * scale
        b = jax.random.normal(ks[5], (N_LAYERS, D), dtype=jnp.float32) * 0.01
        return {'x': x, 'src': src, 'dst': dst, 'W_self': W_self, 'W_neigh': W_neigh, 'b': b}
    _L1_gnn_all = _L1_gnn_setup()
    _L1_gnn_in = {k: v for k, v in _L1_gnn_all.items() if k in ('W_self', 'W_neigh', 'b')}
    del _L1_gnn_all

    def _L2_gnn_setup():
        import jax, jax.numpy as jnp
        import numpy as np
        N, E, H, D_IN, D_PRIME = (6250, 100000, 8, 512, 64)

        def _segment_softmax(scores, seg, num_segments):
            smax = jax.ops.segment_max(scores, seg, num_segments=num_segments)
            ex = jnp.exp(scores - smax[seg])
            denom = jax.ops.segment_sum(ex, seg, num_segments=num_segments)
            return ex / denom[seg]
        key = jax.random.key(seed)
        ks = jax.random.split(key, 6)
        x = jax.random.normal(ks[0], (N, D_IN), dtype=jnp.float32)
        edge_index = jax.random.randint(ks[1], (2, E), 0, N)
        Ws = jax.random.normal(ks[2], (H, D_IN, D_PRIME), dtype=jnp.float32) * 0.05
        Wb = jax.random.normal(ks[3], (H, D_PRIME), dtype=jnp.float32) * 0.05
        a_w = jax.random.normal(ks[4], (H, 2 * D_PRIME), dtype=jnp.float32) * 0.05
        a_b = jax.random.normal(ks[5], (H,), dtype=jnp.float32) * 0.05
        return dict(x=x, edge_index=edge_index, Ws=Ws, Wb=Wb, a_w=a_w, a_b=a_b)
    _L2_gnn_all = _L2_gnn_setup()
    _L2_gnn_in = {k: v for k, v in _L2_gnn_all.items() if k in ('Ws', 'Wb', 'a_w', 'a_b')}
    del _L2_gnn_all

    def _L3_gnn_setup():
        import jax, jax.numpy as jnp
        import numpy as np
        N_NODES = 6250
        N_EDGES = 100000
        D_IN = 512
        D_OUT = 512
        key = jax.random.key(seed)
        k1, k2, k3, k4, k5 = jax.random.split(key, 5)
        local_feats = jax.random.normal(k1, (N_NODES, D_IN), dtype=jnp.float32)
        src = jax.random.randint(k2, (N_EDGES,), 0, N_NODES, dtype=jnp.int64)
        dst = jax.random.randint(k3, (N_EDGES,), 0, N_NODES, dtype=jnp.int64)
        lim = (6.0 / (D_IN + D_OUT)) ** 0.5
        W_self = jax.random.uniform(k4, (D_OUT, D_IN), minval=-lim, maxval=lim, dtype=jnp.float32)
        W_neigh = jax.random.uniform(k5, (D_OUT, D_IN), minval=-lim, maxval=lim, dtype=jnp.float32)
        b = jnp.zeros((D_OUT,), dtype=jnp.float32)
        return {'local_feats': local_feats, 'src': src, 'dst': dst, 'layer': 0, 'W_self': W_self, 'W_neigh': W_neigh, 'b': b}
    _L3_gnn_all = _L3_gnn_setup()
    _L3_gnn_in = {k: v for k, v in _L3_gnn_all.items() if k in ('W_self', 'W_neigh', 'b')}
    del _L3_gnn_all
    return {'x': x, 'src': src, 'dst': dst, 'L0_gnn_Ws_self': _L0_gnn_in['Ws_self'], 'L0_gnn_Ws_neigh': _L0_gnn_in['Ws_neigh'], 'L0_gnn_bs': _L0_gnn_in['bs'], 'L1_gnn_W_self': _L1_gnn_in['W_self'], 'L1_gnn_W_neigh': _L1_gnn_in['W_neigh'], 'L1_gnn_b': _L1_gnn_in['b'], 'L2_gnn_Ws': _L2_gnn_in['Ws'], 'L2_gnn_Wb': _L2_gnn_in['Wb'], 'L2_gnn_a_w': _L2_gnn_in['a_w'], 'L2_gnn_a_b': _L2_gnn_in['a_b'], 'L3_gnn_W_self': _L3_gnn_in['W_self'], 'L3_gnn_W_neigh': _L3_gnn_in['W_neigh'], 'L3_gnn_b': _L3_gnn_in['b']}

def reference(x, src, dst, L0_gnn_Ws_self, L0_gnn_Ws_neigh, L0_gnn_bs, L1_gnn_W_self, L1_gnn_W_neigh, L1_gnn_b, L2_gnn_Ws, L2_gnn_Wb, L2_gnn_a_w, L2_gnn_a_b, L3_gnn_W_self, L3_gnn_W_neigh, L3_gnn_b):
    import jax
    import jax.numpy as jnp

    def _L0_gnn_ref(x, Ws_self, Ws_neigh, bs, src, dst):
        import jax, jax.numpy as jnp
        import numpy as np
        N_NODES = 2500
        N_EDGES = 40000
        D = 512
        L = 3
        n = x.shape[0]
        deg = jax.ops.segment_sum(jnp.ones_like(dst, dtype=x.dtype), dst, num_segments=n)
        inv_deg = (1.0 / jnp.clip(deg, 1.0))[:, None]
        h = x
        n_layers = Ws_self.shape[0]
        for l in range(n_layers):
            neigh = jax.ops.segment_sum(h[src], dst, num_segments=n) * inv_deg
            h = h @ Ws_self[l] + neigh @ Ws_neigh[l] + bs[l]
            if l != n_layers - 1:
                h = jax.nn.relu(h)
        return h

    def _L1_gnn_ref(x, src, dst, W_self, W_neigh, b):
        import jax, jax.numpy as jnp
        import numpy as np
        N_NODES = 6250
        N_EDGES = 100000
        D = 512
        N_LAYERS = 3
        EPS = 1e-12
        n = x.shape[0]
        deg = jax.ops.segment_sum(jnp.ones_like(dst, dtype=x.dtype), dst, num_segments=n)
        deg = jnp.maximum(deg, 1.0)[:, None]
        h = x
        for l in range(N_LAYERS):
            h_neigh = jax.ops.segment_sum(h[src], dst, num_segments=n) / deg
            rst = h @ W_self[l] + h_neigh @ W_neigh[l] + b[l]
            rst = jax.nn.relu(rst)
            nrm = jnp.sqrt(jnp.sum(rst * rst, axis=-1, keepdims=True))
            h = rst / jnp.maximum(nrm, EPS)
        return h

    def _L2_gnn_ref(x, edge_index, Ws, Wb, a_w, a_b):
        import jax, jax.numpy as jnp
        import numpy as np
        N, E, H, D_IN, D_PRIME = (6250, 100000, 8, 512, 64)

        def _segment_softmax(scores, seg, num_segments):
            smax = jax.ops.segment_max(scores, seg, num_segments=num_segments)
            ex = jnp.exp(scores - smax[seg])
            denom = jax.ops.segment_sum(ex, seg, num_segments=num_segments)
            return ex / denom[seg]
        v_src, v_tgt = (edge_index[0], edge_index[1])
        n = x.shape[0]
        outs = []
        for h in range(Ws.shape[0]):
            Wx = x @ Ws[h] + Wb[h]
            d = Wx.shape[-1]
            s = Wx[v_tgt] @ a_w[h, :d] + Wx[v_src] @ a_w[h, d:] + a_b[h]
            s = jax.nn.leaky_relu(s, negative_slope=0.2)
            alpha = _segment_softmax(s, v_tgt, n)
            outs.append(jax.ops.segment_sum(alpha[:, None] * Wx[v_src], v_tgt, num_segments=n))
        return jnp.stack(outs, axis=1).reshape(n, -1)

    def _L3_gnn_ref(local_feats, src, dst, layer, W_self, W_neigh, b):
        import jax, jax.numpy as jnp
        import numpy as np
        N_NODES = 6250
        N_EDGES = 100000
        D_IN = 512
        D_OUT = 512
        'DistSAGEConv forward: mean neighbor aggregation + fc_self + fc_neigh + bias + ReLU.\n            `layer` only selects which hop in the distributed impl; aggregation math is identical.\n            '
        n = local_feats.shape[0]
        msg = local_feats[src]
        agg = jax.ops.segment_sum(msg, dst, num_segments=n)
        deg = jax.ops.segment_sum(jnp.ones((src.shape[0],), local_feats.dtype), dst, num_segments=n)
        h_neigh = agg / jnp.maximum(deg, 1.0)[:, None]
        rst = local_feats @ W_self.T + h_neigh @ W_neigh.T + b
        return jax.nn.relu(rst)
    edge_index = jnp.stack([src, dst])
    h = jnp.maximum(_layernorm(x, axis=-1), 0.0)
    x = x + _L0_gnn_ref(h, L0_gnn_Ws_self, L0_gnn_Ws_neigh, L0_gnn_bs, src, dst)
    h = jnp.maximum(_layernorm(x, axis=-1), 0.0)
    x = x + _L1_gnn_ref(h, src, dst, L1_gnn_W_self, L1_gnn_W_neigh, L1_gnn_b)
    h = jnp.maximum(_layernorm(x, axis=-1), 0.0)
    x = x + _L2_gnn_ref(h, edge_index, L2_gnn_Ws, L2_gnn_Wb, L2_gnn_a_w, L2_gnn_a_b)
    h = jnp.maximum(_layernorm(x, axis=-1), 0.0)
    x = x + _L3_gnn_ref(h, src, dst, 0, L3_gnn_W_self, L3_gnn_W_neigh, L3_gnn_b)
    return x

_drawn_inputs = setup_inputs


def setup_inputs(seed=0):
    import zlib

    import numpy as np

    out = dict(_drawn_inputs(seed))
    spreads = {'L3_gnn_b': (0.0, 0.1)}
    factors = {'L1_gnn_b': 8.0,
     'L2_gnn_a_w': 5.738,
     'L2_gnn_a_b': 64.0,
     'L1_gnn_W_self': 4.19,
     'L1_gnn_W_neigh': 4.26}
    for name, (base, spread) in spreads.items():
        noise = np.random.default_rng([zlib.crc32(name.encode()), seed]).standard_normal(out[name].shape)
        drawn = base * np.exp(spread * noise) if base else spread * noise
        out[name] = jnp.asarray(drawn.astype(out[name].dtype))
    for name, factor in factors.items():
        out[name] = (out[name] * factor).astype(out[name].dtype)
    return out
```

```python
import concourse.bass as bass
from concourse import mybir
from concourse.alu_op_type import AluOpType as ALU
from contextlib import ExitStack

F32 = mybir.dt.float32
BF16 = mybir.dt.bfloat16
F16 = mybir.dt.float16
I32 = mybir.dt.int32
U8 = mybir.dt.uint8
ACT = mybir.ActivationFunctionType
AX = mybir.AxisListType.X

N, D, E = 1250, 512, 40000
P = 125
T = N // P
KT = D // 128
HEADS, DH = 8, 64
EC = E // P
CH = 34
CAP = CH * 128
HALF = CH // 2
R3 = 417
LN_EPS, NORM_EPS = 1e-5, 1e-12
NEVER = -3e38
SLOPE = 0.2
WIDE = 40.0
RATIO_MAX = 50.0
MAX = bass.bass_isa.ReduceOp.max
THIRDS = [(0, 417), (417, 834), (834, N)]
COLS = [(0, 512), (512, 1024), (1024, N)]

STAGES = range(9)
GAT_E = 7
HAS_RST = [e != 0 for e in STAGES]
MAKES_H = [e != 8 for e in STAGES]
MAKES_HP = [e not in (6, 8) for e in STAGES]
RELU = [e in (4, 5, 6, 8) for e in STAGES]
L2NORM = [e in (4, 5, 6) for e in STAGES]
LAYERNORM = [e in (0, 3, 6, 7) for e in STAGES]


def first(e, table):
    return T * sum(table[:e])


def averaging(e):
    return e - 1 if e < 8 else 6


def steps(e):
    return (e == 3) + 5 * L2NORM[e] + (e == 6) + 7 * LAYERNORM[e]


LN_BASE = [T * sum(steps(i) for i in range(e)) for e in STAGES]


class Chain:

    def __init__(self, eng, sem):
        self.eng, self.sem, self.n = eng, sem, 0

    def link(self, ins):
        self.n = self.n + 1
        ins.then_inc(self.sem, 1)
        self.eng.wait_ge(self.sem, self.n)


def gnn_kernel(nc, x, src, dst, weights, biases, attn, attn_b, out):
    with ExitStack() as ctx:
        def sb(name, shape, dt):
            return ctx.enter_context(nc.sbuf_tensor(name, shape, dt))

        def sem(name):
            return ctx.enter_context(nc.semaphore(name))

        X = sb("X", [128, T, D], F32)
        AT = sb("AT", [128, T, N], BF16)
        AH = sb("AH", [128, T, N], BF16)
        MK = sb("MK", [128, T, N], BF16)
        INV = sb("INV", [128, N], F32)
        BB = sb("BB", [128, D], F32)
        iota = sb("iota", [128, N], F16)
        bounds = sb("bounds", [128, T], F32)
        ident = sb("ident", [128, 128], F32)
        ident16 = sb("ident16", [128, 128], BF16)
        ones = sb("ones", [128, 128], F32)
        ones16 = sb("ones16", [128, 128], BF16)
        zeros16 = sb("zeros16", [128, 128], BF16)
        small = sb("small", [128, 2, 16], F32)
        stat = sb("stat", [128, 2, 6], F32)
        cnt = sb("cnt", [128, T], F32)
        starts = sb("starts", [1, T], I32)
        over = sb("over", [128, T], F32)
        flagf = sb("flagf", [128, 4], F32)
        flag = sb("flag", [1, 1], I32)
        tds = sb("tds", [128, 2, T, HEADS], F32)
        tsl = sb("tsl", [128, T, HEADS], F32)
        smax = sb("smax", [128, T, HEADS], F32)
        ab = sb("ab", [128, 3, T, HEADS], F32)
        abias = sb("abias", [128, HEADS], F32)
        ext = sb("ext", [128, 2, HEADS], F32)
        extall = sb("extall", [128, 2, HEADS], F32)
        flag8 = sb("flag8", [128, HEADS], F32)
        wflag = sb("wflag", [1, 1], I32)
        fac = sb("fac", [128, 5, T, HEADS], F32)
        WV = sb("WV", [128, 6 * N], F32)
        W = WV[:, 0:4096].rearrange("p (s k n) -> p s k n", s=2, k=KT)
        Vb = WV[:, 4096:5120].rearrange("p (u n) -> p u n", u=2)
        Hb = WV[:, 5120:6144].rearrange("p (u n) -> p u n", u=2)
        Rb = WV[:, 6144:7168].rearrange("p (u n) -> p u n", u=2)
        HN = sb("HN", [128, 12740], F32)
        HP = HN[:, 0:7680].bitcast(BF16).rearrange("p (t s n) -> p t s n", t=T, s=3)
        NT = HN[:, 7680:12680].rearrange("p (k n) -> p k n", k=KT)
        HT = sb("HT", [128, KT, N], F32)

        ring = HN[:, 0:HALF * 544].bitcast(BF16).rearrange("p (u c n) -> p u c n", u=2, c=HALF)
        scr = HT[:, :, :].rearrange("p k n -> p (k n)")
        ew = scr[:, 0:2 * T * CH].bitcast(I32).rearrange("p (s t c) -> p s t c", s=2, t=T)
        es = scr[:, 700:700 + 3 * T * CH].rearrange("p (s t c) -> p s t c", s=3, t=T)
        cur = scr[:, 1750:1750 + 3 * CH].rearrange("p (s c) -> p s c", s=3)
        tmpe = scr[:, 1860:1860 + 2 * T * CH].rearrange("p (s n) -> p s n", s=2)
        eall = scr[:, 2600:2600 + 2 * EC].bitcast(I32).rearrange("p (s n) -> p s n", s=2)
        eallf = scr[:, 3300:3300 + 2 * EC].rearrange("p (s n) -> p s n", s=2)
        DM = scr[:, 3980:3980 + 626].bitcast(BF16)
        less = WV[:, 4096:4096 + 1600].bitcast(BF16).rearrange("p (t n) -> p t n", t=T)
        cint = WV[:, 5700:5700 + R3 + 1].bitcast(I32)
        junk8 = WV[:, 6130:6130 + 210].bitcast(BF16)
        gint = HN[:, 9300:9300 + N].bitcast(I32)
        goh = HN[:, 10600:10600 + 700].bitcast(BF16)
        gdm = HN[:, 11320:11320 + 1252].bitcast(BF16).rearrange("p (w n) -> p w n", w=2)

        WX = HN[:, 0:T * HEADS * 128].rearrange("p (t h n) -> p t h n", t=T, h=HEADS)
        rows = HN[:, 10240:10240 + 2 * N].rearrange("p (s n) -> p s n", s=2)
        slots = WV[:, 0:6 * N].rearrange("p (s n) -> p s n", s=6)
        attn_s = HN[:, 10240:10240 + 2 * D].rearrange("p (s n) -> p s n", s=2)

        agg = ctx.enter_context(nc.psum_tensor("agg", [128, 2, 1536], F32))
        rst = ctx.enter_context(nc.psum_tensor("rst", [128, 2, 512], F32))
        rhop = [rst[:, i, :].rearrange("p (t n) -> p t n", t=4)[:, :, 0:P] for i in range(2)]
        hps = [agg[:, 1, 512 * (1 + u):512 * (1 + u) + KT * P].rearrange("p (k n) -> p k n", k=KT) for u in range(2)]
        rowv = agg[:, :, 0:128 * T].rearrange("p s (t n) -> p s t n", t=T)[:, :, :, 0:P]
        aps = agg[:, :, 512:1024].bitcast(BF16)[:, :, 0:5 * 126].rearrange("p s (k n) -> p s k n", k=5)[:, :, :, 0:P]

        s_const = sem("constants_made")
        s_idx = sem("edge_lists_loaded")
        s_x = sem("x_loaded")
        s_w = sem("weights_loaded")
        s_ew = sem("edge_windows_loaded")
        s_cnt = sem("edges_below_bounds_counted")
        s_startps = sem("window_starts_summed")
        s_starts = sem("window_starts_ready")
        s_ohr = sem("one_hots_ready")
        s_ohu = sem("one_hots_used")
        s_cint = sem("packed_counts_read")
        s_dm = sem("counts_unpacked")
        s_mk = sem("mask_made")
        s_tp = sem("counts_transposed")
        s_at = sem("counts_stored")
        s_deg = sem("degrees_summed")
        s_flag = sem("flag_ready")
        s_inv = sem("inverse_degrees_ready")
        g_ready = sem("general_one_hots_ready")
        g_used = sem("general_one_hots_used")
        g_tile = sem("general_tile_counted")
        g_dm = sem("general_counts_unpacked")
        g_tp = sem("general_counts_transposed")
        g_ev = sem("general_counts_stored")
        s_wide = sem("wide_vector_step_done")
        s_dve = sem("vector_step_done")
        s_cur = sem("tile_scalars_copied")
        s_nm = sem("normalising_step_done")
        g_dve = sem("general_vector_step_done")
        s_pool = sem("pool_step_done")
        s_ln = sem("statistics_step_done")
        s_agg = sem("neighbour_sums_ready")
        s_nt = sem("neighbour_means_ready")
        s_rst = sem("layer_tile_ready")
        s_v = sem("layer_tile_read")
        s_relu = sem("rectified")
        s_sum = sem("squares_summed")
        s_sq = sem("norms_ready")
        s_root = sem("deviations_ready")
        s_pre = sem("normalised_before_relu")
        s_h = sem("features_ready")
        s_hi = sem("high_parts_ready")
        s_rem = sem("remainders_ready")
        s_mid = sem("middle_parts_ready")
        s_hp = sem("feature_parts_ready")
        s_tr = sem("features_transposed")
        s_ht = sem("transposed_features_stored")
        s_wx = sem("projection_ready")
        s_wxv = sem("projection_stored")
        s_one = sem("ones_beside_projections")
        s_sc = sem("scores_ready")
        s_tsr = sem("source_score_rows_in_psum")
        s_mx = sem("maxima_done")
        s_ab = sem("score_terms_ready")
        s_row = sem("score_rows_in_psum")
        s_ev = sem("score_rows_stored")
        s_ext = sem("partition_extremes_ready")
        s_all = sem("score_extremes_ready")
        s_dif = sem("exponents_of_factors_ready")
        s_fac = sem("factors_ready")
        s_rho = sem("ratio_rows_in_psum")
        s_re = sem("ratio_rows_stored")
        s_r = sem("excess_ready")
        s_lin = sem("flat_branch_ready")
        s_q = sem("exponents_ready")
        s_e = sem("exponentials_ready")
        s_p = sem("edge_weights_ready")
        s_pu = sem("edge_weights_used")
        s_out = sem("output_rows_ready")
        s_st = sem("output_stored")

        loads = [0 if e == 0 else 5 if e == GAT_E else 3 for e in STAGES]
        w_after = [16 * sum(loads[:e + 1]) for e in STAGES]

        block = ctx.enter_context(nc.Block())

        @block.sync
        def _(sp):
            sp.dma_start(eall[0:P, 0, :], dst.rearrange("(p c) -> p c", p=P)).then_inc(s_idx, 16)
            sp.dma_start(eall[0:P, 1, :], src.rearrange("(p c) -> p c", p=P)).then_inc(s_idx, 16)
            sp.dma_start(X[0:P, :, :], x.rearrange("(t p) n -> p t n", p=P)).then_inc(s_x, 16)

            sp.wait_ge(s_starts, 1)
            for t in range(T):
                at = sp.value_load(starts[0:1, t:t + 1], min_val=0, max_val=E - CAP)
                for i, a in enumerate((dst, src)):
                    sp.dma_start(ew[:, i, t, :], a[bass.ds(at, CAP)].rearrange("(p c) -> p c", p=128)).then_inc(s_ew, 16)

            n = 0
            for e in STAGES[1:]:
                if e > 1:
                    sp.wait_ge(s_v, first(e, HAS_RST))
                for s in range(1 if e == GAT_E else 2):
                    sp.dma_start(W[:, s, :, :], weights[n].rearrange("p (k n) -> p k n", k=KT)).then_inc(s_w, 16)
                    n += 1
                sp.dma_start(BB[0:P, :], biases[e - 1:e, :].broadcast_to([P, D])).then_inc(s_w, 16)
                if e == GAT_E:
                    for s in range(2):
                        sp.dma_start(attn_s[0:P, s, :], attn[s:s + 1, :].broadcast_to([P, D])).then_inc(s_w, 16)
                    sp.dma_start(abias[0:P, :], attn_b[0:1, :].broadcast_to([P, HEADS])).then_inc(s_w, 16)

            outv = out.rearrange("(t p) n -> p t n", p=P)
            for m in range(T):
                sp.wait_ge(s_out, m + 1)
                sp.dma_start(outv[:, m, :], X[0:P, m, :]).then_inc(s_st, 16)
            sp.wait_ge(s_st, 16 * T)

        @block.gpsimd
        def _(pool):
            chain = Chain(pool, s_pool)
            nc.gpsimd.iota(iota[:, :], [[1, N]], base=0, channel_multiplier=0, allow_small_or_imprecise_dtypes=True)
            nc.gpsimd.iota(bounds[:, :], [[P, T]], base=0, channel_multiplier=0, allow_small_or_imprecise_dtypes=True)
            nc.gpsimd.memset(ones[:, :], 1.0)
            nc.gpsimd.memset(zeros16[:, :], 0.0)
            nc.gpsimd.memset(ones16[:, :], 1.0)
            nc.gpsimd.memset(ext[:, :, :], NEVER)
            chain.link(nc.gpsimd.memset(ident[:, :], 0.0))
            chain.link(nc.gpsimd.affine_select(out=ident[:, :], in_=ident[:, :], compare_op=ALU.not_equal, fill=1.0,
                                               base=0, pattern=[[-1, 128]], channel_multiplier=1))
            nc.gpsimd.tensor_copy(ident16[:, :], ident[:, :]).then_inc(s_const, 1)

            for t in range(T):
                pool.wait_ge(s_dm, t + 1)
                nc.gpsimd.tensor_scalar(MK[0:P, t, :], DM[0:P, 0:N], 0.0, NEVER,
                                        ALU.is_equal, ALU.mult).then_inc(s_mk, 1)

            for e in STAGES:
                if e == GAT_E:
                    pool.wait_ge(s_rst, first(GAT_E, HAS_RST))
                    nc.gpsimd.memset(WX[0:P, :, :, DH:2 * DH], 1.0).then_inc(s_one, 1)
                    pool.wait_ge(s_ext, 1)
                    nc.gpsimd.partition_all_reduce(extall[:, :, :].rearrange("p s h -> p (s h)"),
                                                   ext[:, :, :].rearrange("p s h -> p (s h)"), 128, MAX).then_inc(s_all, 1)
                if not MAKES_HP[e]:
                    continue
                with pool.Fori(0, T // 2) as i:
                    for u in range(2):
                        m = 2 * i + u
                        pool.wait_ge(s_mid, first(e, MAKES_HP) + m + 1)
                        nc.gpsimd.tensor_tensor(HP[0:P, m, 2, :], Rb[0:P, u, :], HP[0:P, m, 1, :],
                                                ALU.subtract).then_inc(s_hp, 1)

        @block.scalar
        def _(act):
            def store_counts(t):
                act.wait_ge(s_tp, t + 1)
                for j in range(2):
                    ins = nc.scalar.copy(AT[0:P, 5 * j:5 * j + 5, bass.ds(P * t, P)], aps[0:P, j])
                ins.then_inc(s_at, 1)

            def unpack(t, u, earlier):
                act.wait_ge(s_ohu, 2 * t + 2)
                if earlier:
                    act.wait_ge(s_dm, t)
                nc.scalar.copy(cint[0:P, 0:R3], agg[0:P, u, 0:R3]).then_inc(s_cint, 1)
                act.wait_ge(s_cint, t + 1)
                if earlier:
                    store_counts(t - 1)
                    act.wait_ge(s_mk, t)
                b = cint[0:P, 0:R3].bitcast(U8).rearrange("p (n b) -> p n b", b=4)
                for q in range(3):
                    w = min(R3, N - R3 * q)
                    nc.scalar.copy(DM[0:P, R3 * q:R3 * q + w], b[:, 0:w, q])
                nc.scalar.activation(junk8[0:P, 0:R3], b[:, :, 3], ACT.Copy,
                                     accum_out=over[0:P, bass.ds(t, 1)]).then_inc(s_dm, 1)

            act.wait_ge(s_const, 1)
            unpack(0, 0, False)
            unpack(1, 1, True)
            with act.Fori(1, T // 2) as i:
                for u in range(2):
                    unpack(2 * i + u, u, True)
            store_counts(T - 1)

            def tile(e, m, u):
                hp = first(e, MAKES_HP) + m
                hh = first(e, MAKES_H) + m
                reused = e > 0 or m >= 2
                if RELU[e]:
                    act.wait_ge(s_v, first(e, HAS_RST) + m + 1)
                    if MAKES_H[e] and reused:
                        act.wait_ge(s_tr, hh - 1)
                    nc.scalar.activation(Hb[0:P, u, :], Vb[0:P, u, :], ACT.Relu).then_inc(s_relu, 1)
                if L2NORM[e]:
                    act.wait_ge(s_relu, first(e, RELU) + m + 1)
                    nc.scalar.activation(Vb[0:P, u, :], Hb[0:P, u, :], ACT.Square,
                                         accum_out=small[0:P, u, 0:1]).then_inc(s_sum, 1)
                    act.wait_ge(s_sum, first(e, L2NORM) + m + 1)
                    nc.scalar.activation(small[0:P, u, 1:2], small[0:P, u, 0:1], ACT.Sqrt).then_inc(s_sq, 1)
                if LAYERNORM[e]:
                    act.wait_ge(s_ln, LN_BASE[e] + steps(e) * (m + 1) - 4)
                    nc.scalar.activation(small[0:P, u, 6:7], small[0:P, u, 5:6], ACT.Sqrt).then_inc(s_root, 1)
                if LAYERNORM[e] or e in (1, 2):
                    if LAYERNORM[e]:
                        act.wait_ge(s_pre, first(e, LAYERNORM) + m + 1)
                    else:
                        act.wait_ge(s_v, first(e, HAS_RST) + m + 1)
                    if reused:
                        act.wait_ge(s_tr, hh - 1)
                    nc.scalar.activation(Hb[0:P, u, :], Vb[0:P, u, :], ACT.Relu).then_inc(s_h, 1)
                if MAKES_HP[e]:
                    act.wait_ge(s_h, hh + 1)
                    nc.scalar.copy(HP[0:P, m, 0, :], Hb[0:P, u, :]).then_inc(s_hi, 1)
                    act.wait_ge(s_rem, hp + 1)
                    nc.scalar.copy(HP[0:P, m, 1, :], Rb[0:P, u, :]).then_inc(s_mid, 1)
                if MAKES_H[e]:
                    act.wait_ge(s_tr, hh + 1)
                    nc.scalar.copy(HT[:, :, bass.ds(P * m, P)], hps[u]).then_inc(s_ht, 1)

            def flat(h, k):
                j = T * h + k
                if j >= 4:
                    act.wait_ge(s_p, j - 3)
                nc.scalar.activation(slots[0:P, j % 4, :], rows[0:P, 1, :], ACT.Identity,
                                     bias=tsl[0:P, k, h:h + 1]).then_inc(s_lin, 1)

            def exponential(j):
                act.wait_ge(s_q, j + 1)
                nc.scalar.activation(slots[0:P, j % 4, :], slots[0:P, j % 4, :], ACT.Exp).then_inc(s_e, 1)

            def attention():
                def store_row(h, i):
                    a, b = 4 * P * i, min(4 * P * i + 4 * P, N)
                    act.wait_ge(s_rho, 3 * h + i + 1)
                    if h >= 2:
                        act.wait_ge(s_r, T * (h - 1))
                    nc.scalar.copy(rows[0:P, h % 2, a:b].rearrange("p (t n) -> p t n", n=P),
                                   rhop[i % 2][0:P, 0:(b - a) // P]).then_inc(s_re, 1)

                for i in range(3):
                    store_row(0, i)
                for h in range(HEADS):
                    act.wait_ge(s_re, 3 * h + 3)
                    for k in range(T):
                        j = T * h + k
                        if h + 1 < HEADS and k in (5, 8):
                            for i in ((0, 1) if k == 5 else (2,)):
                                store_row(h + 1, i)
                        if j >= 4:
                            act.wait_ge(s_p, j - 3)
                        nc.scalar.activation(slots[0:P, j % 4, :], rows[0:P, h % 2, :], ACT.Relu, bias=fac[0:P, 3, k, h:h + 1],
                                             scale=fac[0:P, 1, k, h:h + 1]).then_inc(s_r, 1)

            def factors():
                act.wait_ge(s_dif, 1)
                nc.scalar.activation(fac[0:P, 1], fac[0:P, 0], ACT.Exp, scale=SLOPE)
                nc.scalar.activation(fac[0:P, 2], fac[0:P, 2], ACT.Exp)
                nc.scalar.activation(fac[0:P, 4], fac[0:P, 0], ACT.Exp).then_inc(s_fac, 1)
                act.wait_ge(s_fac, 1)
                nc.scalar.mul(fac[0:P, 3], fac[0:P, 4], -1.0).then_inc(s_fac, 1)
                act.wait_ge(s_fac, 2)

            def wide_attention():
                act.wait_ge(s_ab, 1)
                for h in range(HEADS):
                    for s in range(2):
                        act.wait_ge(s_row, 2 * h + s + 1)
                        if s == 0 and h > 0:
                            act.wait_ge(s_q, T * h)
                        nc.scalar.copy(rows[:, s, :].rearrange("p (t n) -> p t n", t=T), rowv[:, 0]).then_inc(s_ev, 1)
                    act.wait_ge(s_ev, 2 * h + 2)
                    for k in range(T):
                        flat(h, k)
                        if k > 0:
                            exponential(T * h + k - 1)
                    exponential(T * h + T - 1)

            for e in STAGES:
                if e == GAT_E:
                    factors()
                    wide = act.value_load(wflag[0:1, 0:1], min_val=0, max_val=1)
                    with act.If(wide != 0):
                        wide_attention()
                    with act.Else():
                        attention()
                if e == 0:
                    act.wait_ge(s_mk, T)
                    for m in range(T):
                        tile(e, m, m % 2)
                else:
                    with act.Fori(0, T // 2) as i:
                        for u in range(2):
                            tile(e, 2 * i + u, u)

        @block.vector
        def _(dve):
            chain = Chain(dve, s_dve)
            link = chain.link

            dve.wait_ge(s_const, 1)
            dve.wait_ge(s_idx, 32)
            link(nc.vector.tensor_copy(eallf[0:P], eall[0:P]))
            link(nc.vector.tensor_tensor(less[0:P], eallf[0:P, 0:1, :].broadcast_to([P, T, EC]),
                                         bounds[0:P, :].unsqueeze(2).broadcast_to([P, T, EC]), ALU.is_lt))
            nc.vector.reduce_sum(cnt[0:P, :], less[0:P], AX).then_inc(s_cnt, 1)
            dve.wait_ge(s_startps, 1)
            nc.vector.tensor_scalar(starts[0:1, :], rst[0:1, 0, 0:T], float(E - CAP), None, ALU.min).then_inc(s_starts, 1)

            dve.wait_ge(s_ew, 32 * T)
            flat_n = T * CH
            d_in, s_in = (ew[:, i].rearrange("p t c -> p (t c)") for i in range(2))
            link(nc.vector.tensor_tensor(es[:, 0], ew[:, 0], bounds[:, :].unsqueeze(2).broadcast_to([128, T, CH]),
                                         ALU.subtract))
            link(nc.vector.tensor_scalar(tmpe[:, 0, :], s_in, float(R3), float(R3), ALU.is_ge, ALU.mult))
            link(nc.vector.tensor_scalar(tmpe[:, 1, :], s_in, float(2 * R3), float(R3), ALU.is_ge, ALU.mult))
            link(nc.vector.tensor_tensor(tmpe[:, 0, :], tmpe[:, 0, :], tmpe[:, 1, :], ALU.add))
            link(nc.vector.tensor_tensor(es[:, 1].rearrange("p t c -> p (t c)"), s_in, tmpe[:, 0, :], ALU.subtract))
            link(nc.vector.tensor_scalar(tmpe[:, 0, :], s_in, float(R3), 255.0, ALU.is_ge, ALU.mult))
            link(nc.vector.tensor_scalar(tmpe[:, 1, :], s_in, float(2 * R3), 65280.0, ALU.is_ge, ALU.mult))
            link(nc.vector.scalar_tensor_tensor(out=es[:, 2].rearrange("p t c -> p (t c)"), in0=tmpe[:, 0, :],
                                                scalar=1.0, in1=tmpe[:, 1, :], op0=ALU.add, op1=ALU.add))

            def one_hots(t, earlier):
                if earlier:
                    dve.wait_ge(s_ohr, 2 * t)
                nc.vector.tensor_copy(cur[:, :, :], es[:, :, t, :]).then_inc(s_cur, 1)
                dve.wait_ge(s_cur, t + 1)
                for v in range(2):
                    if earlier:
                        dve.wait_ge(s_ohu, 2 * t + v - 1)
                    for c in range(HALF):
                        n = HALF * v + c
                        nc.vector.tensor_scalar(ring[:, v, c, 0:P], iota[:, 0:P], cur[:, 0, n:n + 1], None, ALU.is_equal)
                        ins = nc.vector.tensor_scalar(ring[:, v, c, 126:126 + R3], iota[:, 0:R3], cur[:, 1, n:n + 1],
                                                      cur[:, 2, n:n + 1], ALU.is_equal, ALU.mult)
                    ins.then_inc(s_ohr, 1)

            one_hots(0, False)
            with dve.Fori(1, T) as t:
                one_hots(t, True)

            dve.wait_ge(s_deg, 1)
            nc.vector.reduce_sum(flagf[:, 0:1], agg[:, 0, 0:N], AX)
            link(nc.vector.reduce_sum(flagf[:, 1:2], rst[:, 0, 0:T], AX))
            link(nc.vector.tensor_scalar(flagf[:, 2:3], flagf[:, 0:1], float(E), None, ALU.not_equal))
            link(nc.vector.tensor_tensor(flagf[:, 3:4], flagf[:, 2:3], flagf[:, 1:2], ALU.add))
            link(nc.vector.tensor_scalar(flag[0:1, :], flagf[0:1, 3:4], 1.0, None, ALU.min))
            nc.vector.tensor_copy(flagf[:, 0:1], flagf[:, 3:4]).then_inc(s_flag, 1)
            general = dve.value_load(flag[0:1, 0:1], min_val=0, max_val=1)

            with dve.If(general != 0):
                dve.wait_ge(s_mk, T)
                with dve.Fori(0, T) as t:
                    with dve.Fori(0, EC) as c:
                        nc.vector.tensor_scalar(goh[0:P, 0:P], iota[0:P, 0:P], eallf[0:P, 0, bass.ds(c, 1)], None, ALU.is_equal)
                        nc.vector.tensor_scalar(goh[0:P, 126:126 + N], iota[0:P, :], eallf[0:P, 1, bass.ds(c, 1)], None,
                                                ALU.is_equal).then_inc(g_ready, 1)
                        dve.wait_ge(g_used, EC * t + c + 1)
                    dve.wait_ge(g_tile, t + 1)
                    nc.vector.tensor_copy(gint[0:P, :], agg[0:P, 0, 0:N])
                    nc.vector.tensor_scalar(MK[0:P, t, :], agg[0:P, 0, 0:N], 0.0, NEVER, ALU.is_equal, ALU.mult)
                    nc.vector.tensor_scalar(eallf[0:P, 0, :], eallf[0:P, 0, :], -float(P), None, ALU.add).then_inc(g_dve, 1)
                    dve.wait_ge(g_dve, t + 1)
                    b = gint[0:P, :].bitcast(U8).rearrange("p (n b) -> p n b", b=4)
                    nc.vector.tensor_copy(gdm[0:P, 0, 0:N], b[:, :, 0])
                    nc.vector.tensor_scalar(gdm[0:P, 1, 0:N], b[:, :, 1], 256.0, None, ALU.mult).then_inc(g_dm, 1)
                    for w in range(2):
                        dve.wait_ge(g_tp, 2 * t + w + 1)
                        to = AT if w == 0 else AH
                        for j in range(2):
                            ins = nc.vector.tensor_copy(to[0:P, 5 * j:5 * j + 5, bass.ds(P * t, P)], aps[0:P, j])
                        ins.then_inc(g_ev, 1)
                dve.wait_ge(s_deg, 2)

            link(nc.vector.tensor_scalar(INV[:, :], agg[:, 0, 0:N], 1.0, None, ALU.max))
            nc.vector.reciprocal(INV[:, :], INV[:, :]).then_inc(s_inv, 1)
            dve.wait_ge(s_inv, 1)

            class Steps:

                def __init__(self, base):
                    self.n = base

                def link(self, ins):
                    self.n = self.n + 1
                    ins.then_inc(s_ln, 1)
                    dve.wait_ge(s_ln, self.n)

            def invert_root(st, v, root, q, least):
                st.link(nc.vector.reciprocal(q, root))
                st.link(nc.vector.tensor_scalar(q, v, q, root, ALU.mult, ALU.add))
                st.link(nc.vector.tensor_scalar(root, q, 0.5, least, ALU.mult, ALU.max))
                st.link(nc.vector.reciprocal(root, root))

            def tile(e, m, u):
                st = Steps(LN_BASE[e] + steps(e) * m)
                start = st.n
                hp = first(e, MAKES_HP) + m
                hh = first(e, MAKES_H) + m
                if e > 0 and MAKES_H[e] or e == 0 and m >= 2:
                    dve.wait_ge(s_h, hh - 1)
                if HAS_RST[e]:
                    n = first(e, HAS_RST) + m + 1
                    dve.wait_ge(s_rst, n)
                    if e == GAT_E:
                        ins = nc.vector.tensor_tensor(X[0:P, m, :], rst[0:P, u, :], X[0:P, m, :], ALU.add)
                    else:
                        ins = nc.vector.tensor_tensor(Vb[0:P, u, :], rst[0:P, u, :], BB[0:P, :], ALU.add)
                    ins.then_inc(s_v, 1)
                    dve.wait_ge(s_v, n)
                if e == 3:
                    st.link(nc.vector.tensor_tensor(X[0:P, m, :], X[0:P, m, :], Vb[0:P, u, :], ALU.add))
                if L2NORM[e]:
                    dve.wait_ge(s_sq, first(e, L2NORM) + m + 1)
                    sq, root, q = (small[0:P, u, i:i + 1] for i in range(3))
                    st.link(nc.vector.tensor_scalar(root, root, NORM_EPS, None, ALU.max))
                    invert_root(st, sq, root, q, NORM_EPS)
                    if e == 6:
                        st.link(nc.vector.scalar_tensor_tensor(out=X[0:P, m, :], in0=Hb[0:P, u, :], scalar=small[0:P, u, 1:2],
                                                               in1=X[0:P, m, :], op0=ALU.mult, op1=ALU.add))
                    else:
                        nc.vector.tensor_scalar(Hb[0:P, u, :], Hb[0:P, u, :], small[0:P, u, 1:2], None,
                                                ALU.mult).then_inc(s_h, 1)
                if e == 8:
                    dve.wait_ge(s_relu, first(e, RELU) + m + 1)
                    nc.vector.tensor_tensor(X[0:P, m, :], X[0:P, m, :], Hb[0:P, u, :], ALU.add).then_inc(s_out, 1)
                if LAYERNORM[e]:
                    st.link(nc.vector.bn_stats(stat[0:P, u, :], X[0:P, m, :]))
                    st.link(nc.vector.bn_aggr(small[0:P, u, 4:6], stat[0:P, u, :]))
                    mean, var, root, q = (small[0:P, u, i:i + 1] for i in range(4, 8))
                    st.link(nc.vector.tensor_scalar(var, var, LN_EPS, None, ALU.add))
                    dve.wait_ge(s_root, first(e, LAYERNORM) + m + 1)
                    invert_root(st, var, root, q, NORM_EPS)
                    nc.vector.tensor_scalar(Vb[0:P, u, :], X[0:P, m, :], mean, root,
                                            ALU.subtract, ALU.mult).then_inc(s_pre, 1)
                if MAKES_HP[e]:
                    if e > 0 or m >= 2:
                        dve.wait_ge(s_hp, hp - 1)
                    dve.wait_ge(s_hi, hp + 1)
                    nc.vector.tensor_tensor(Rb[0:P, u, :], Hb[0:P, u, :], HP[0:P, m, 0, :], ALU.subtract).then_inc(s_rem, 1)
                return st.n

            def means(e):
                for f in range(KT):
                    for i, (lo, hi) in enumerate(THIRDS):
                        dve.wait_ge(s_agg, 3 * KT * averaging(e) + 3 * f + i + 1)
                        nc.vector.tensor_tensor(NT[:, f, lo:hi], agg[:, 0, 512 * i:512 * i + hi - lo], INV[:, lo:hi],
                                                ALU.mult).then_inc(s_nt, 1)

            def scores():
                for m in range(T):
                    dve.wait_ge(s_wx, m + 1)
                    nc.vector.tensor_tensor(WX[0:P, m, :, 0:DH], rst[0:P, m % 2, :].rearrange("p (h n) -> p h n", h=HEADS),
                                            BB[0:P, :].rearrange("p (h n) -> p h n", h=HEADS), ALU.add).then_inc(s_wxv, 1)
                    dve.wait_ge(s_wxv, m + 1)
                    for s in range(2):
                        link(nc.vector.tensor_tensor(Vb[0:P, s, :].rearrange("p (h n) -> p h n", h=HEADS), WX[0:P, m, :, 0:DH],
                                                     attn_s[0:P, s, :].rearrange("p (h n) -> p h n", h=HEADS), ALU.mult))
                        link(nc.vector.reduce_sum(tds[0:P, s, m, :], Vb[0:P, s, :].rearrange("p (h n) -> p h n", h=HEADS), AX))
                td, ts = tds[0:P, 0], tds[0:P, 1]
                link(nc.vector.tensor_tensor(td, td, abias[0:P, :].unsqueeze(1).broadcast_to([P, T, HEADS]), ALU.add))
                nc.vector.tensor_scalar(tsl[0:P], ts, SLOPE, None, ALU.mult).then_inc(s_sc, 1)
                link(nc.vector.tensor_scalar(fac[0:P, 0], ts, -1.0, None, ALU.mult))
                nc.vector.tensor_reduce(ext[0:P, 0, :], ts.rearrange("p t h -> p h t"), AX, ALU.max)
                nc.vector.tensor_reduce(ext[0:P, 1, :], fac[0:P, 0].rearrange("p t h -> p h t"), AX, ALU.max).then_inc(s_ext, 1)
                dve.wait_ge(s_all, 1)
                most = extall[0:P, 0:1, :].broadcast_to([P, T, HEADS])
                link(nc.vector.tensor_tensor(flag8[:, :], extall[:, 0, :], extall[:, 1, :], ALU.add))
                link(nc.vector.tensor_reduce(flagf[:, 0:1], flag8[:, :], AX, ALU.max))
                link(nc.vector.tensor_scalar(wflag[0:1, :], flagf[0:1, 0:1], WIDE, None, ALU.is_ge))
                link(nc.vector.tensor_tensor(fac[0:P, 2], td, most, ALU.add))
                link(nc.vector.tensor_scalar(fac[0:P, 2], fac[0:P, 2], SLOPE - 1.0, RATIO_MAX, ALU.mult, ALU.min))
                nc.vector.tensor_tensor(fac[0:P, 0], ts, most, ALU.subtract).then_inc(s_dif, 1)
                dve.wait_ge(s_dif, 1)

            def maxima():
                td, ts = tds[0:P, 0], tds[0:P, 1]
                for h in range(HEADS):
                    dve.wait_ge(s_tsr, h + 1)
                    for t in range(T):
                        if T * h + t >= 2:
                            dve.wait_ge(s_mx, T * h + t - 1)
                        nc.vector.tensor_tensor_reduce(
                            slots[0:P, t % 2, :].rearrange("p (t n) -> p t n", t=T), MK[0:P, t, :].rearrange("p (t n) -> p t n", t=T),
                            rowv[0:P, h % 2], 1.0, NEVER, ALU.add, ALU.max, smax[0:P, t, h:h + 1]).then_inc(s_mx, 1)
                dve.wait_ge(s_mx, T * HEADS)
                z, lz = ab[0:P, 0], ab[0:P, 2]
                wch = Chain(dve, s_wide)
                link = wch.link
                link(nc.vector.tensor_scalar(z, smax[0:P], NEVER / 2, None, ALU.is_ge))
                link(nc.vector.tensor_tensor(smax[0:P], smax[0:P], z, ALU.mult))
                link(nc.vector.tensor_tensor(z, td, smax[0:P], ALU.add))
                link(nc.vector.scalar_tensor_tensor(out=lz, in0=z, scalar=SLOPE, in1=z, op0=ALU.mult, op1=ALU.max))
                link(nc.vector.tensor_tensor(ab[0:P, 0], td, lz, ALU.subtract))
                nc.vector.scalar_tensor_tensor(out=ab[0:P, 1], in0=td, scalar=SLOPE, in1=lz, op0=ALU.mult,
                                               op1=ALU.subtract).then_inc(s_ab, 1)

            def edge_weights_factored(high):
                gch = Chain(dve, g_dve)
                gch.n = T
                for j in range(HEADS * T):
                    h, k = divmod(j, T)
                    dve.wait_ge(s_r, j + 1)
                    if j >= 2:
                        dve.wait_ge(s_pu, j - 1)
                    to, s, u1 = slots[0:P, 4 + j % 2, :], slots[0:P, j % 4, :], fac[0:P, 4, k, h:h + 1]
                    ins = nc.vector.scalar_tensor_tensor(out=to, in0=s, scalar=u1, in1=AT[0:P, k, :],
                                                         op0=ALU.add, op1=ALU.mult)
                    if high:
                        gch.link(ins)
                        gch.link(nc.vector.scalar_tensor_tensor(out=s, in0=s, scalar=u1, in1=AH[0:P, k, :],
                                                                op0=ALU.add, op1=ALU.mult))
                        ins = nc.vector.tensor_tensor(to, to, s, ALU.add)
                    ins.then_inc(s_p, 1)
                    if j % T == 2 and h > 0:
                        normalise(h - 1, (h - 1) % 2)
                normalise(HEADS - 1, (HEADS - 1) % 2)

            def normalise(h, o):
                dve.wait_ge(s_pu, T * (h + 1))
                for i, (a, b) in enumerate(COLS):
                    rec = BB[0:DH, 0:b - a]
                    nc.vector.tensor_scalar(rec, agg[DH:2 * DH, o, a:b], 1e-30, None, ALU.max).then_inc(s_nm, 1)
                    dve.wait_ge(s_nm, 9 * h + 3 * i + 1)
                    nc.vector.reciprocal(rec, rec).then_inc(s_nm, 1)
                    dve.wait_ge(s_nm, 9 * h + 3 * i + 2)
                    nc.vector.tensor_tensor(HT[DH * (h % 2):DH * (h % 2) + DH, h // 2, a:b], agg[0:DH, o, a:b], rec,
                                            ALU.mult).then_inc(s_nm, 1)
                    dve.wait_ge(s_nm, 9 * h + 3 * i + 3)

            def attention(high):
                gch = Chain(dve, g_dve)
                gch.n = T

                def exponent(j):
                    h, k = divmod(j, T)
                    if k == 0:
                        dve.wait_ge(s_ev, 2 * h + 2)
                    dve.wait_ge(s_lin, j + 1)
                    s = slots[0:P, j % 4, :]
                    nc.vector.scalar_tensor_tensor(out=s, in0=rows[0:P, 0, :], scalar=tds[0:P, 1, k, h:h + 1], in1=s,
                                                   op0=ALU.add, op1=ALU.max).then_inc(s_q, 1)

                def edge_weights(j):
                    h, k = divmod(j, T)
                    dve.wait_ge(s_e, j + 1)
                    if j >= 2:
                        dve.wait_ge(s_pu, j - 1)
                    to, s = slots[0:P, 4 + j % 2, :], slots[0:P, j % 4, :]
                    ins = nc.vector.scalar_tensor_tensor(out=to, in0=s, scalar=1.0, in1=AT[0:P, k, :],
                                                         op0=ALU.min, op1=ALU.mult)
                    if high:
                        gch.link(ins)
                        gch.link(nc.vector.scalar_tensor_tensor(out=s, in0=s, scalar=1.0, in1=AH[0:P, k, :],
                                                                op0=ALU.min, op1=ALU.mult))
                        ins = nc.vector.tensor_tensor(to, to, s, ALU.add)
                    ins.then_inc(s_p, 1)

                for j in range(HEADS * T):
                    exponent(j)
                    if j > 0:
                        edge_weights(j - 1)
                    if j % T == 1 and j > T:
                        normalise(j // T - 1, 1)
                edge_weights(HEADS * T - 1)
                normalise(HEADS - 1, 1)

            for e in STAGES:
                if e == 0:
                    dve.wait_ge(s_x, 16)
                elif e == GAT_E:
                    scores()
                    wide = dve.value_load(wflag[0:1, 0:1], min_val=0, max_val=1)
                    with dve.If(wide != 0):
                        maxima()
                        with dve.If(general != 0):
                            attention(True)
                        with dve.Else():
                            attention(False)
                    with dve.Else():
                        dve.wait_ge(s_fac, 2)
                        with dve.If(general != 0):
                            edge_weights_factored(True)
                        with dve.Else():
                            edge_weights_factored(False)
                else:
                    means(e)
                if LAYERNORM[e]:
                    for m in range(T):
                        tile(e, m, m % 2)
                    continue
                with dve.Fori(0, T // 2) as i:
                    for u in range(2):
                        tile(e, 2 * i + u, u)

        @block.tensor
        def _(pe):
            pe.wait_ge(s_const, 1)
            pe.wait_ge(s_cnt, 1)
            nc.tensor.matmul(rst[0:1, 0, 0:T], ones[0:P, 0:1], cnt[0:P, :], start=True, stop=True).then_inc(s_startps, 1)

            def count(t, u, earlier):
                if earlier:
                    pe.wait_ge(s_cint, t - 1)
                for v in range(2):
                    pe.wait_ge(s_ohr, 2 * t + v + 1)
                    for c in range(HALF):
                        ins = nc.tensor.matmul(agg[0:P, u, 0:R3], ring[:, v, c, 0:P], ring[:, v, c, 126:126 + R3],
                                               start=(v == 0 and c == 0), stop=(v == 1 and c == HALF - 1))
                    ins.then_inc(s_ohu, 1)

            def transpose_counts(t, earlier):
                pe.wait_ge(s_dm, t + 1)
                if earlier:
                    pe.wait_ge(s_at, t)
                for k in range(T):
                    ins = nc.tensor.transpose(aps[0:P, k // 5, k % 5], DM[0:P, P * k:P * k + P], ident16[0:P, 0:P])
                ins.then_inc(s_tp, 1)

            count(0, 0, False)
            count(1, 1, False)
            transpose_counts(0, False)
            with pe.Fori(1, T // 2) as i:
                for u in range(2):
                    t = 2 * i + u
                    count(t, u, True)
                    transpose_counts(t - 1, True)
            transpose_counts(T - 1, True)

            def sum_degrees(parts):
                for a, b in COLS:
                    for w, c in enumerate(parts):
                        for k in range(T):
                            ins = nc.tensor.matmul(agg[:, 0, a:b], ones16[0:P, :], c[0:P, k, a:b],
                                                   start=(w == 0 and k == 0), stop=(w == len(parts) - 1 and k == T - 1))
                return ins

            pe.wait_ge(s_at, T)
            nc.tensor.matmul(rst[:, 0, 0:T], ones[0:P, :], over[0:P, :], start=True, stop=True)
            sum_degrees([AT]).then_inc(s_deg, 1)
            pe.wait_ge(s_flag, 1)
            general = pe.value_load(flag[0:1, 0:1], min_val=0, max_val=1)

            with pe.If(general != 0):
                with pe.Fori(0, T) as t:
                    for a, b in COLS:
                        nc.tensor.matmul(agg[0:P, 0, a:b], zeros16[0:P, 0:P], iota[0:P, a:b], start=True, stop=False)
                    with pe.Fori(0, EC) as c:
                        pe.wait_ge(g_ready, EC * t + c + 1)
                        for a, b in COLS:
                            ins = nc.tensor.matmul(agg[0:P, 0, a:b], goh[0:P, 0:P], goh[0:P, 126 + a:126 + b],
                                                   start=False, stop=False)
                        ins.then_inc(g_used, 1)
                    for a, b in COLS:
                        ins = nc.tensor.matmul(agg[0:P, 0, a:b], zeros16[0:P, 0:P], iota[0:P, a:b], start=False, stop=True)
                    ins.then_inc(g_tile, 1)
                    pe.wait_ge(g_dm, t + 1)
                    for w in range(2):
                        for k in range(T):
                            ins = nc.tensor.transpose(aps[0:P, k // 5, k % 5], gdm[0:P, w, P * k:P * k + P], ident16[0:P, 0:P])
                        ins.then_inc(g_tp, 1)
                        pe.wait_ge(g_ev, 2 * t + w + 1)
                sum_degrees([AT, AH]).then_inc(s_deg, 1)
            pe.wait_ge(s_inv, 1)

            def transpose_features(e, m):
                hh = first(e, MAKES_H) + m
                pe.wait_ge(s_h, hh + 1)
                if hh >= 2:
                    pe.wait_ge(s_ht, hh - 1)
                for f in range(KT):
                    ins = nc.tensor.transpose(hps[m % 2][:, f], Hb[0:P, m % 2, 128 * f:128 * f + 128], ident[0:P, 0:P])
                ins.then_inc(s_tr, 1)

            def sum_neighbours(e):
                a = averaging(e)

                def products(f, k, i, counts, start, stop):
                    lo, hi = THIRDS[i]
                    for s in range(3):
                        ins = nc.tensor.matmul(agg[:, 0, 512 * i:512 * i + hi - lo], HP[0:P, k, s, bass.ds(128 * f, 128)],
                                               counts[0:P, k, lo:hi], start=(start and s == 0), stop=(stop and s == 2))
                    return ins

                def block_of_features(f, opening):
                    for i in range(3):
                        if opening and i == 0:
                            pe.wait_ge(s_hp, T * a + 1)
                        if not opening:
                            pe.wait_ge(s_nt, 3 * (KT * a + f - 1) + i + 1)
                        products(f, 0, i, AT, True, False)
                        for k in range(1, T):
                            if opening and i == 0:
                                pe.wait_ge(s_hp, T * a + k + 1)
                            if k == T - 1:
                                with pe.If(general != 0):
                                    for kh in range(T):
                                        products(f, kh, i, AH, False, False)
                            ins = products(f, k, i, AT, False, k == T - 1)
                        ins.then_inc(s_agg, 1)

                block_of_features(0, True)
                transpose_features(e - 1, T - 1)
                with pe.Fori(1, KT) as f:
                    block_of_features(f, False)

            def layer_tile(e, m):
                n = first(e, HAS_RST) + m
                if n >= 2:
                    pe.wait_ge(s_v, n - 1)
                cols = slice(P * m, P * m + P)
                for s, feats in enumerate((HT, NT)):
                    for k in range(KT):
                        ins = nc.tensor.matmul(rst[0:P, m % 2, :], feats[:, k, cols], W[:, s, k, :],
                                               start=(s == 0 and k == 0), stop=(s == 1 and k == KT - 1))
                ins.then_inc(s_rst, 1)

            def project():
                transpose_features(6, T - 1)
                pe.wait_ge(s_w, w_after[GAT_E])
                pe.wait_ge(s_ht, T * GAT_E)
                pe.wait_ge(s_v, first(GAT_E, HAS_RST))
                for m in range(T):
                    if m >= 2:
                        pe.wait_ge(s_wxv, m - 1)
                    for k in range(KT):
                        ins = nc.tensor.matmul(rst[0:P, m % 2, :], HT[:, k, P * m:P * m + P], W[:, 0, k, :],
                                               start=(k == 0), stop=(k == KT - 1))
                    ins.then_inc(s_wx, 1)

            def source_rows():
                pe.wait_ge(s_sc, 1)
                for h in range(HEADS):
                    if h >= 2:
                        pe.wait_ge(s_mx, T * (h - 1))
                    for t in range(T):
                        ins = nc.tensor.transpose(rowv[:, h % 2, t], tds[0:P, 1, t, h:h + 1].broadcast_to([P, 128]), ident[0:P, 0:P])
                    ins.then_inc(s_tsr, 1)

            def sum_head(h, k, o, start, stop):
                j = T * h + k
                pe.wait_ge(s_p, j + 1)
                for a, b in COLS:
                    ins = nc.tensor.matmul(agg[:, o, a:b], WX[0:P, k, h, :], slots[0:P, 4 + j % 2, a:b],
                                           start=(k == 0), stop=(k == T - 1))
                ins.then_inc(s_pu, 1)

            def attend():
                def ratio_row(h, i):
                    if 3 * h + i >= 2:
                        pe.wait_ge(s_re, 3 * h + i - 1)
                    for t in range(4 * i, min(4 * i + 4, T)):
                        ins = nc.tensor.transpose(rhop[i % 2][:, t - 4 * i], fac[0:P, 2, t, h:h + 1].broadcast_to([P, 128]), ident[0:P, 0:P])
                    ins.then_inc(s_rho, 1)

                pe.wait_ge(s_fac, 2)
                pe.wait_ge(s_one, 1)
                for i in range(3):
                    ratio_row(0, i)
                for h in range(HEADS):
                    if h > 1:
                        pe.wait_ge(s_nm, 9 * (h - 1))
                    for k in range(T):
                        sum_head(h, k, h % 2, k == 0, k == T - 1)
                        if h + 1 < HEADS and k in (1, 6):
                            for i in ((0, 1) if k == 1 else (2,)):
                                ratio_row(h + 1, i)

            def attend_wide():
                def score_rows(h, s):
                    if 2 * h + s > 0:
                        pe.wait_ge(s_ev, 2 * h + s)
                    for t in range(T):
                        ins = nc.tensor.transpose(rowv[:, 0, t], ab[0:P, s, t, h:h + 1].broadcast_to([P, 128]), ident[0:P, 0:P])
                    ins.then_inc(s_row, 1)

                pe.wait_ge(s_ab, 1)
                pe.wait_ge(s_one, 1)
                score_rows(0, 0)
                score_rows(0, 1)
                for h in range(HEADS):
                    if h > 0:
                        pe.wait_ge(s_nm, 9 * h)
                    for k in range(T):
                        if k == T - 1 and h + 1 < HEADS:
                            score_rows(h + 1, 1)
                        sum_head(h, k, 1, k == 0, k == T - 1)
                        if k == 5 and h + 1 < HEADS:
                            score_rows(h + 1, 0)

            def turn_attended():
                pe.wait_ge(s_nm, 9 * HEADS)
                for m in range(T):
                    n = first(GAT_E, HAS_RST) + m
                    if m >= 2:
                        pe.wait_ge(s_v, n - 1)
                    for f in range(KT):
                        ins = nc.tensor.transpose(rst[0:P, m % 2, 128 * f:128 * f + 128], HT[:, f, P * m:P * m + P], ident[:, :])
                    ins.then_inc(s_rst, 1)
                    if m > 0:
                        transpose_features(GAT_E, m - 1)

            for m in range(T - 1):
                transpose_features(0, m)
            for e in STAGES[1:]:
                if e == GAT_E:
                    project()
                    pe.wait_ge(s_dif, 1)
                    wide = pe.value_load(wflag[0:1, 0:1], min_val=0, max_val=1)
                    with pe.If(wide != 0):
                        source_rows()
                        attend_wide()
                    with pe.Else():
                        attend()
                    turn_attended()
                    continue
                sum_neighbours(e)
                pe.wait_ge(s_w, w_after[e])
                pe.wait_ge(s_ht, T * e)
                pe.wait_ge(s_nt, 3 * KT * (averaging(e) + 1))
                for m in range(T):
                    layer_tile(e, m)
                    if m > 0 and MAKES_H[e]:
                        transpose_features(e, m - 1)


def kernel(x, src, dst, L0_gnn_Ws_self, L0_gnn_Ws_neigh, L0_gnn_bs, L1_gnn_W_self, L1_gnn_W_neigh, L1_gnn_b,
           L2_gnn_Ws, L2_gnn_Wb, L2_gnn_a_w, L2_gnn_a_b, L3_gnn_W_self, L3_gnn_W_neigh, L3_gnn_b):
    import numpy as np
    import concourse.bacc as bacc
    from concourse.bass_utils import run_bass_kernel_spmd

    def rows_first(w):
        return np.asarray(w).reshape(KT, 128, D).transpose(1, 0, 2).reshape(128, KT * D)

    mats = []
    for selfs, neighs in ((L0_gnn_Ws_self, L0_gnn_Ws_neigh), (L1_gnn_W_self, L1_gnn_W_neigh)):
        for l in range(3):
            mats += [rows_first(selfs[l]), rows_first(neighs[l])]
    mats.append(rows_first(np.asarray(L2_gnn_Ws).transpose(1, 0, 2).reshape(D, D)))
    mats += [rows_first(np.asarray(L3_gnn_W_self).T), rows_first(np.asarray(L3_gnn_W_neigh).T)]
    a_w = np.asarray(L2_gnn_a_w)
    arrays = {
        "x": np.ascontiguousarray(x),
        "src": np.ascontiguousarray(src),
        "dst": np.ascontiguousarray(dst),
        "weights": np.ascontiguousarray(np.stack(mats)),
        "biases": np.concatenate([np.asarray(L0_gnn_bs), np.asarray(L1_gnn_b), np.asarray(L2_gnn_Wb).reshape(1, D),
                                  np.asarray(L3_gnn_b).reshape(1, D)]),
        "attn": np.stack([np.ascontiguousarray(a_w[:, :DH]).reshape(D), np.ascontiguousarray(a_w[:, DH:]).reshape(D)]),
        "attn_b": np.ascontiguousarray(L2_gnn_a_b).reshape(1, HEADS),
    }
    nc = bacc.Bacc("TRN2", target_bir_lowering=False, num_devices=1)
    args = [nc.dram_tensor(k, a.shape, mybir.dt.from_np(a.dtype), kind="ExternalInput").ap() for k, a in arrays.items()]
    out = nc.dram_tensor("out", (N, D), F32, kind="ExternalOutput").ap()
    gnn_kernel(nc, *args, out)
    r = run_bass_kernel_spmd(nc, [arrays], core_ids=[0])
    return r.results[0]["out"]
```

```python
import concourse.bass as bass
from concourse import mybir
from concourse.alu_op_type import AluOpType as ALU
from contextlib import ExitStack

F32 = mybir.dt.float32
BF16 = mybir.dt.bfloat16
F16 = mybir.dt.float16
I32 = mybir.dt.int32
U8 = mybir.dt.uint8
ACT = mybir.ActivationFunctionType
AX = mybir.AxisListType.X
MAX = bass.bass_isa.ReduceOp.max

N, D, E = 1250, 512, 40000
P = 125
T = N // P
KT = D // 128
HEADS, DH = 8, 64
EC = E // P
GROUPS = [10, 8, 8, 8]
GMAX = max(GROUPS)
CH = sum(GROUPS)
CAP = CH * 128
R3 = 417
LN_EPS, NORM_EPS = 1e-5, 1e-12
NEVER = -3e38
SLOPE = 0.2
WIDE = 40.0
RATIO_MAX = 50.0
COLS = [(0, 512), (512, 1024), (1024, N)]
THIRDS = [(0, 417), (417, 834), (834, N)]
HALVES = [(0, 7), (7, T)]

LN_SCALE, UNIT_SCALE = 1024.0, 32768.0
LN_NORM2 = 520.0
EXPONENT = 0x7F800000

STAGES = range(9)
GAT_E = 7
HAS_RST = [e not in (0, GAT_E) for e in STAGES]
L2NORM = [e in (4, 5, 6) for e in STAGES]
LAYERNORM = [e in (0, 3, 6, 7) for e in STAGES]
DYNAMIC = [e in (1, 2) for e in STAGES]
OUT_SCALE = [LN_SCALE if LAYERNORM[e] else UNIT_SCALE for e in STAGES]


def first(e, table):
    return T * sum(table[:e])


def averaging(e):
    return e - 1 if e < 8 else 6


def steps(e):
    return (e == 3) + 5 * L2NORM[e] + (e == 6) + 7 * LAYERNORM[e]


LN_BASE = [T * sum(steps(i) for i in range(e)) for e in STAGES]


class Chain:

    def __init__(self, eng, sem, n=0):
        self.eng, self.sem, self.n = eng, sem, n

    def link(self, ins):
        self.n = self.n + 1
        ins.then_inc(self.sem, 1)
        self.eng.wait_ge(self.sem, self.n)


def gnn_kernel(nc, x, src, dst, weights, biases, attn, attn_b, out):
    with ExitStack() as ctx:
        def sb(name, shape, dt):
            return ctx.enter_context(nc.sbuf_tensor(name, shape, dt))

        def sem(name):
            return ctx.enter_context(nc.semaphore(name))

        X = sb("X", [128, T, D], F32)
        AT = sb("AT", [128, T, N], BF16)
        AH = sb("AH", [128, T, N], BF16)
        INV = sb("INV", [128, N], F32)
        BB = sb("BB", [128, D], F32)
        RW = sb("RW", [128, 2, KT * D], F32)
        iota = sb("iota", [128, N], F16)
        iotac = sb("iotac", [128, P, GMAX], F16)
        bounds = sb("bounds", [128, T], F32)
        ident = sb("ident", [128, 128], F32)
        ident16 = sb("ident16", [128, 128], BF16)
        identh = sb("identh", [128, 128], F16)
        ones = sb("ones", [128, 128], F32)
        zeros16 = sb("zeros16", [128, 128], BF16)
        small = sb("small", [128, 2, 16], F32)
        stat = sb("stat", [128, 2, 6], F32)
        cnt = sb("cnt", [128, T], F32)
        starts = sb("starts", [1, T], I32)
        deg3 = sb("deg3", [128, 3, T], F32)
        degov = sb("degov", [128, 2, T], F32)
        invc = sb("invc", [128, T], F32)
        flagf = sb("flagf", [128, 4], F32)
        flag = sb("flag", [1, 1], I32)
        norms = sb("norms", [128, 3], F32)
        roots = sb("roots", [128, 2, 2], F32)
        bound4 = sb("bound4", [128, 3], F32)
        scale_w = sb("scale_w", [128, 9], F32)
        scale_o = sb("scale_o", [128, 9], F32)
        unscale = sb("unscale", [128, 9], F32)
        tds = sb("tds", [128, 2, T, HEADS], F32)
        tsl = sb("tsl", [128, T, HEADS], F32)
        smax = sb("smax", [128, T, HEADS], F32)
        ab = sb("ab", [128, 3, T, HEADS], F32)
        abias = sb("abias", [128, HEADS], F32)
        ext = sb("ext", [128, 2, HEADS], F32)
        extall = sb("extall", [128, 2, HEADS], F32)
        flag8 = sb("flag8", [128, HEADS], F32)
        wflag = sb("wflag", [1, 1], I32)
        fac = sb("fac", [128, 5, T, HEADS], F32)
        den = sb("den", [128, T], F32)
        WV = sb("WV", [128, 6 * N], F32)
        W16 = WV[:, 0:4096].bitcast(F16).rearrange("p (s w k n) -> p s w k n", s=2, w=2, k=KT)
        Vb = WV[:, 4096:5120].rearrange("p (u n) -> p u n", u=2)
        Rb = WV[:, 5120:6144].rearrange("p (u n) -> p u n", u=2)
        NB = WV[:, 6144:6144 + 2 * R3].rearrange("p (u n) -> p u n", u=2)
        HN = sb("HN", [128, 10624], F32)
        HP = HN[:, 0:5120].bitcast(F16).rearrange("p (t w n) -> p t w n", t=T, w=2)
        NT = HN[:, 5120:10120].bitcast(F16).rearrange("p (w k n) -> p w k n", w=2, k=KT)
        HTf = sb("HT", [128, KT * N], F32)
        HT = HTf[:, :].bitcast(F16).rearrange("p (w k n) -> p w k n", w=2, k=KT)

        ringd = HN[:, 5120:5120 + P * GMAX].bitcast(BF16).rearrange("p (u n c) -> p u n c", u=2, c=GMAX)
        rings = HN[:, 6400:6400 + 2 * GMAX * 209].bitcast(BF16).rearrange("p (u c n) -> p u c n", u=2, c=GMAX)
        ew = INV[:, 0:2 * T * CH].bitcast(I32).rearrange("p (s t c) -> p s t c", s=2, t=T)
        es = WV[:, 0:2 * T * CH].rearrange("p (s t c) -> p s t c", s=2, t=T)
        esn = WV[:, 680:680 + T * CH].rearrange("p (t c) -> p t c", t=T)
        esm = WV[:, 1020:1020 + T * CH].rearrange("p (t c) -> p t c", t=T)
        esd = WV[:, 1360:1360 + T * CH // 2].bitcast(F16).rearrange("p (t c) -> p t c", t=T)
        eall = WV[:, 1800:1800 + 2 * EC].bitcast(I32).rearrange("p (s n) -> p s n", s=2)
        eallf = WV[:, 2440:2440 + 2 * EC].rearrange("p (s n) -> p s n", s=2)
        DM = WV[:, 3080:3080 + 626].bitcast(BF16)
        cint = WV[:, 7000:7000 + R3].bitcast(I32)
        less = WV[:, 4096:4096 + 1600].bitcast(BF16).rearrange("p (t n) -> p t n", t=T)
        tmpe = WV[:, 6144:6144 + 2 * T * CH].rearrange("p (s n) -> p s n", s=2)
        junk8 = WV[:, 3706:3706 + 210].bitcast(BF16)
        gint = HN[:, 6400:6400 + N].bitcast(I32)
        goh = HN[:, 8500:8500 + 700].bitcast(BF16)
        gdm = HN[:, 5120:5120 + 1252].bitcast(BF16).rearrange("p (w n) -> p w n", w=2)

        WX = HN[:, 0:T * HEADS * 65].rearrange("p (t h n) -> p t h n", t=T, h=HEADS)
        rows = HN[:, 5200:5200 + 2 * N].rearrange("p (s n) -> p s n", s=2)
        NU = HN[:, 7700:7700 + N]
        attn_s = HN[:, 8950:8950 + 2 * D].rearrange("p (s n) -> p s n", s=2)
        slots = WV[:, 0:6 * N].rearrange("p (s n) -> p s n", s=6)
        share = BB[:, 0:7 * DH].rearrange("p (t n) -> p t n", n=DH)

        agg = ctx.enter_context(nc.psum_tensor("agg", [128, 2, 1536], F32))
        rst = ctx.enter_context(nc.psum_tensor("rst", [128, 2, 512], F32))
        hps = [agg[:, 1, 512 * (1 + u):512 * (2 + u)].bitcast(F16)[:, 0:8 * 126]
               .rearrange("p (w k n) -> p w k n", w=2, k=KT)[:, :, :, 0:P] for u in range(2)]
        rowv = agg[:, :, 0:128 * T].rearrange("p s (t n) -> p s t n", t=T)[:, :, :, 0:P]
        aps = rst[:, :, :].bitcast(BF16)[:, :, 0:5 * 126].rearrange("p s (k n) -> p s k n", k=5)[:, :, :, 0:P]
        rhop = [rst[:, i, :].rearrange("p (t n) -> p t n", t=4)[:, :, 0:P] for i in range(2)]
        nups = [rst[:, 1 - i, 0:65 * 7].rearrange("p (t n) -> p t n", n=65) for i in range(2)]

        s_const = sem("constants_made")
        s_idx = sem("edge_lists_loaded")
        s_x = sem("x_loaded")
        s_w = sem("weights_loaded")
        s_b = sem("bias_loaded")
        s_ew = sem("edge_windows_loaded")
        s_cnt = sem("edges_below_bounds_counted")
        s_startps = sem("window_starts_summed")
        s_starts = sem("window_starts_ready")
        s_esc = sem("edge_scalars_ready")
        s_ohr = sem("one_hots_ready")
        s_oha = sem("scalar_engines_one_hots_ready")
        s_sqd = sem("squared_distances_ready")
        s_ohu = sem("one_hots_used")
        s_cint = sem("packed_counts_read")
        s_dm = sem("counts_unpacked")
        s_tp = sem("counts_transposed")
        s_at = sem("counts_stored")
        s_deg = sem("degrees_ready")
        s_degs = sem("edges_summed")
        s_flag = sem("flag_ready")
        s_invc = sem("inverse_degrees_ready")
        s_invr = sem("inverse_degree_rows_in_psum")
        s_inv = sem("inverse_degree_rows_ready")
        g_ready = sem("general_one_hots_ready")
        g_used = sem("general_one_hots_used")
        g_tile = sem("general_tile_counted")
        g_dm = sem("general_counts_unpacked")
        g_tp = sem("general_counts_transposed")
        g_ev = sem("general_counts_stored")
        g_dve = sem("general_vector_step_done")
        s_dve = sem("vector_step_done")
        s_wide = sem("wide_vector_step_done")
        s_pool = sem("pool_step_done")
        s_ln = sem("statistics_step_done")
        s_norm = sem("squares_of_weights_summed")
        s_normps = sem("squared_norms_ready")
        s_sq2 = sem("squared_norms_stored")
        s_roots = sem("norms_ready")
        s_scale = sem("scales_ready")
        s_whi = sem("weights_high_parts_ready")
        s_wlo = sem("weights_low_parts_ready")
        s_agg = sem("neighbour_sums_ready")
        s_mean = sem("neighbour_means_ready")
        s_nhi = sem("means_high_parts_ready")
        s_nt = sem("means_parts_ready")
        s_rst = sem("layer_tile_ready")
        s_v = sem("layer_tile_read")
        s_relu = sem("rectified")
        s_sum = sem("squares_summed")
        s_sq = sem("row_norms_ready")
        s_root = sem("deviations_ready")
        s_pre = sem("normalised_before_relu")
        s_hi = sem("high_parts_ready")
        s_hp = sem("feature_parts_ready")
        s_tr = sem("features_transposed")
        s_ht = sem("transposed_features_stored")
        s_wx = sem("projection_ready")
        s_wxv = sem("projection_stored")
        s_one = sem("ones_beside_projections")
        s_sc = sem("scores_ready")
        s_tsr = sem("source_score_rows_in_psum")
        s_ct = sem("counts_turned")
        s_mk = sem("mask_made")
        s_mx = sem("maxima_done")
        s_ab = sem("score_terms_ready")
        s_row = sem("score_rows_in_psum")
        s_ev = sem("score_rows_stored")
        s_ext = sem("partition_extremes_ready")
        s_all = sem("score_extremes_ready")
        s_dif = sem("exponents_of_factors_ready")
        s_fac = sem("factors_ready")
        s_rho = sem("ratio_rows_in_psum")
        s_re = sem("ratio_rows_stored")
        s_r = sem("excess_ready")
        s_lin = sem("flat_branch_ready")
        s_q = sem("exponents_ready")
        s_e = sem("exponentials_ready")
        s_p = sem("edge_weights_ready")
        s_pu = sem("edge_weights_used")
        s_nu = sem("head_sums_stored")
        s_nut = sem("head_sums_transposed")
        s_xh = sem("head_added")
        s_fin = sem("head_step_done")
        s_out = sem("output_rows_ready")
        s_st = sem("output_stored")

        b_after = [16 * sum(0 if i == 0 else 4 if i == GAT_E else 1 for i in range(e + 1)) for e in STAGES]
        w_after = [16 * sum(0 if i == 0 else 1 if i == GAT_E else 2 for i in range(e + 1)) for e in STAGES]
        mats = [0 if e == 0 else 1 if e == GAT_E else 2 for e in STAGES]
        chunks = [sum(GROUPS[:g]) for g in range(5)]

        block = ctx.enter_context(nc.Block())

        @block.sync
        def _(sp):
            sp.dma_start(eall[0:P, 0, :], dst.rearrange("(p c) -> p c", p=P)).then_inc(s_idx, 16)
            sp.dma_start(eall[0:P, 1, :], src.rearrange("(p c) -> p c", p=P)).then_inc(s_idx, 16)
            xv = x.rearrange("(t p) n -> p t n", p=P)
            sp.dma_start(X[0:P, :, :], xv).then_inc(s_x, 16)

            sp.wait_ge(s_starts, 1)
            for t in range(T):
                at = sp.value_load(starts[0:1, t:t + 1], min_val=0, max_val=E - CAP)
                for i, a in enumerate((dst, src)):
                    sp.dma_start(ew[:, i, t, :], a[bass.ds(at, CAP)].rearrange("(p c) -> p c", p=128)).then_inc(s_ew, 16)

            n = 0
            for e in STAGES[1:]:
                if e > 1:
                    sp.wait_ge(s_wlo, sum(mats[:e]))
                for s in range(mats[e]):
                    sp.dma_start(RW[:, s, :], weights[n]).then_inc(s_w, 16)
                    n += 1
                if e > 1:
                    sp.wait_ge(s_hp, T * e)
                sp.dma_start(BB[0:P, :], biases[e - 1:e, :].broadcast_to([P, D])).then_inc(s_b, 16)
                if e == GAT_E:
                    for s in range(2):
                        sp.dma_start(attn_s[0:P, s, :], attn[s:s + 1, :].broadcast_to([P, D])).then_inc(s_b, 16)
                    sp.dma_start(abias[0:P, :], attn_b[0:1, :].broadcast_to([P, HEADS])).then_inc(s_b, 16)

            outv = out.rearrange("(t p) n -> p t n", p=P)
            for m in range(T):
                sp.wait_ge(s_out, m + 1)
                sp.dma_start(outv[:, m, :], X[0:P, m, :]).then_inc(s_st, 16)
            sp.wait_ge(s_st, 16 * T)

        @block.gpsimd
        def _(pool):
            chain = Chain(pool, s_pool)
            nc.gpsimd.iota(bounds[:, :], [[P, T]], base=0, channel_multiplier=0, allow_small_or_imprecise_dtypes=True)
            nc.gpsimd.memset(ones[:, :], 1.0)
            nc.gpsimd.iota(iota[:, :], [[1, N]], base=0, channel_multiplier=0, allow_small_or_imprecise_dtypes=True)
            nc.gpsimd.iota(iotac[:, :, :], [[1, P], [0, GMAX]], base=0, channel_multiplier=0,
                           allow_small_or_imprecise_dtypes=True).then_inc(s_const, 1)
            nc.gpsimd.memset(zeros16[:, :], 0.0)
            nc.gpsimd.memset(ext[:, :, :], NEVER)
            nc.gpsimd.memset(roots[:, :, :], 1.0)
            nc.gpsimd.memset(bound4[:, 0:1], 4.0 * LN_NORM2)
            chain.link(nc.gpsimd.memset(ident[:, :], 0.0))
            chain.link(nc.gpsimd.affine_select(out=ident[:, :], in_=ident[:, :], compare_op=ALU.not_equal, fill=1.0,
                                               base=0, pattern=[[-1, 128]], channel_multiplier=1))
            nc.gpsimd.tensor_copy(ident16[:, :], ident[:, :])
            nc.gpsimd.tensor_copy(identh[:, :], ident[:, :]).then_inc(s_const, 1)

            pool.wait_ge(s_tr, T * GAT_E)
            nc.gpsimd.memset(WX[0:P, :, :, DH:DH + 1], 1.0).then_inc(s_one, 1)
            pool.wait_ge(s_ext, 1)
            nc.gpsimd.partition_all_reduce(extall[:, :, :].rearrange("p s h -> p (s h)"),
                                           ext[:, :, :].rearrange("p s h -> p (s h)"), 128, MAX).then_inc(s_all, 1)

        @block.scalar
        def _(act):
            def store_counts(t):
                act.wait_ge(s_tp, t + 1)
                for j in range(2):
                    ins = nc.scalar.copy(AT[0:P, 5 * j:5 * j + 5, P * t:P * t + P], aps[0:P, j])
                ins.then_inc(s_at, 1)

            def unpack(t):
                act.wait_ge(s_ohu, 4 * t + 4)
                nc.scalar.copy(cint[0:P, 0:R3], agg[0:P, t % 2, 0:R3]).then_inc(s_cint, 1)
                act.wait_ge(s_cint, t + 1)
                if t > 0:
                    store_counts(t - 1)
                b = cint[0:P, 0:R3].bitcast(U8).rearrange("p (n b) -> p n b", b=4)
                for q in range(3):
                    w = min(R3, N - R3 * q)
                    nc.scalar.activation(DM[0:P, R3 * q:R3 * q + w], b[:, 0:w, q], ACT.Copy,
                                         accum_out=deg3[0:P, q, t:t + 1])
                nc.scalar.activation(junk8[0:P, 0:R3], b[:, :, 3], ACT.Copy,
                                     accum_out=degov[0:P, 1, t:t + 1]).then_inc(s_dm, 1)
                act.wait_ge(s_dm, t + 1)

            def tile(e, m, u):
                n = T * e + m
                if L2NORM[e]:
                    act.wait_ge(s_v, first(e, HAS_RST) + m + 1)
                    nc.scalar.activation(Rb[0:P, u, :], Vb[0:P, u, :], ACT.Relu).then_inc(s_relu, 1)
                    act.wait_ge(s_relu, first(e, L2NORM) + m + 1)
                    nc.scalar.activation(Vb[0:P, u, :], Rb[0:P, u, :], ACT.Square,
                                         accum_out=small[0:P, u, 0:1]).then_inc(s_sum, 1)
                    act.wait_ge(s_sum, first(e, L2NORM) + m + 1)
                    nc.scalar.activation(small[0:P, u, 1:2], small[0:P, u, 0:1], ACT.Sqrt).then_inc(s_sq, 1)
                if LAYERNORM[e]:
                    act.wait_ge(s_ln, LN_BASE[e] + steps(e) * (m + 1) - 4)
                    nc.scalar.activation(small[0:P, u, 6:7], small[0:P, u, 5:6], ACT.Sqrt).then_inc(s_root, 1)
                    act.wait_ge(s_pre, first(e, LAYERNORM) + m + 1)
                    nc.scalar.activation(HP[0:P, m, 0, :], Vb[0:P, u, :], ACT.Relu).then_inc(s_hi, 1)
                elif L2NORM[e]:
                    act.wait_ge(s_ln, LN_BASE[e] + steps(e) * (m + 1))
                    nc.scalar.mul(HP[0:P, m, 0, :], Rb[0:P, u, :], small[0:P, u, 1:2]).then_inc(s_hi, 1)
                else:
                    act.wait_ge(s_v, first(e, HAS_RST) + m + 1)
                    nc.scalar.activation(HP[0:P, m, 0, :], Vb[0:P, u, :], ACT.Relu).then_inc(s_hi, 1)

            def store_features(e, m, u):
                act.wait_ge(s_tr, T * e + m + 1)
                nc.scalar.copy(HT[:, :, :, bass.ds(P * m, P)], hps[u]).then_inc(s_ht, 1)

            act.wait_ge(s_const, 2)
            for t in range(T):
                tile(0, t, t % 2)
                if t > 0:
                    store_features(0, t - 1, (t - 1) % 2)
                unpack(t)
            store_counts(T - 1)
            store_features(0, T - 1, 1)

            def sum_squares(e):
                act.wait_ge(s_w, w_after[e])
                if e > 1:
                    act.wait_ge(s_hp, T * e)
                else:
                    act.wait_ge(s_inv, 1)
                for s in range(mats[e]):
                    ins = nc.scalar.activation(W16[:, s, 0, :, :].rearrange("p k n -> p (k n)"), RW[:, s, :], ACT.Square,
                                               scale=2.0 ** -20, accum_out=norms[:, s:s + 1])
                if DYNAMIC[e]:
                    act.wait_ge(s_b, b_after[e])
                    ins = nc.scalar.activation(W16[0:P, 0, 1, 0, :], BB[0:P, :], ACT.Square, accum_out=norms[0:P, 2:3])
                ins.then_inc(s_norm, 1)

            def take_roots(e):
                act.wait_ge(s_sq2, e)
                c = 2 if DYNAMIC[e] else 1
                nc.scalar.activation(roots[:, 1, 0:c], roots[:, 0, 0:c], ACT.Sqrt).then_inc(s_roots, 1)

            def high_weights(e, s):
                if s == 0:
                    act.wait_ge(s_scale, e)
                nc.scalar.mul(W16[:, s, 0, :, :].rearrange("p k n -> p (k n)"), RW[:, s, :],
                              scale_w[:, e:e + 1]).then_inc(s_whi, 1)

            def high_means(e, i):
                n = 3 * KT * averaging(e) + i
                f, (lo, hi) = i // 3, THIRDS[i % 3]
                act.wait_ge(s_mean, n + 1)
                nc.scalar.copy(NT[:, 0, f, lo:hi], NB[:, i % 2, 0:hi - lo]).then_inc(s_nhi, 1)

            def factors():
                act.wait_ge(s_dif, 1)
                nc.scalar.activation(fac[0:P, 1], fac[0:P, 0], ACT.Exp, scale=SLOPE)
                nc.scalar.activation(fac[0:P, 2], fac[0:P, 2], ACT.Exp)
                nc.scalar.activation(fac[0:P, 4], fac[0:P, 0], ACT.Exp).then_inc(s_fac, 1)
                act.wait_ge(s_fac, 1)
                nc.scalar.mul(fac[0:P, 3], fac[0:P, 4], -1.0).then_inc(s_fac, 1)
                act.wait_ge(s_fac, 2)

            def store_sums(h, o):
                act.wait_ge(s_pu, T * (h + 1))
                if h > 0:
                    act.wait_ge(s_nut, 2 * h)
                nc.scalar.copy(NU[0:DH + 1, :], agg[0:DH + 1, o, 0:N]).then_inc(s_nu, 1)

            def attention():
                def store_row(h, i):
                    a, b = 4 * P * i, min(4 * P * i + 4 * P, N)
                    act.wait_ge(s_rho, 3 * h + i + 1)
                    if h >= 2:
                        act.wait_ge(s_r, T * (h - 1))
                    nc.scalar.copy(rows[0:P, h % 2, a:b].rearrange("p (t n) -> p t n", n=P),
                                   rhop[i % 2][0:P, 0:(b - a) // P]).then_inc(s_re, 1)

                for i in range(3):
                    store_row(0, i)
                for h in range(HEADS):
                    act.wait_ge(s_re, 3 * h + 3)
                    for k in range(T):
                        j = T * h + k
                        if h > 0 and k == 4:
                            store_sums(h - 1, (h - 1) % 2)
                        if h + 1 < HEADS and k in (5, 7):
                            for i in ((0, 1) if k == 5 else (2,)):
                                store_row(h + 1, i)
                        if j >= 4:
                            act.wait_ge(s_p, j - 3)
                        nc.scalar.activation(slots[0:P, j % 4, :], rows[0:P, h % 2, :], ACT.Relu, bias=fac[0:P, 3, k, h:h + 1],
                                             scale=fac[0:P, 1, k, h:h + 1]).then_inc(s_r, 1)
                store_sums(HEADS - 1, 1)

            def wide_attention():
                def flat(h, k):
                    j = T * h + k
                    if j >= 4:
                        act.wait_ge(s_p, j - 3)
                    nc.scalar.activation(slots[0:P, j % 4, :], rows[0:P, 1, :], ACT.Identity,
                                         bias=tsl[0:P, k, h:h + 1]).then_inc(s_lin, 1)

                def exponential(j):
                    act.wait_ge(s_q, j + 1)
                    nc.scalar.activation(slots[0:P, j % 4, :], slots[0:P, j % 4, :], ACT.Exp).then_inc(s_e, 1)

                act.wait_ge(s_ab, 1)
                for h in range(HEADS):
                    for s in range(2):
                        act.wait_ge(s_row, 2 * h + s + 1)
                        if s == 0 and h > 0:
                            act.wait_ge(s_q, T * h)
                        nc.scalar.copy(rows[:, s, :].rearrange("p (t n) -> p t n", t=T), rowv[:, 0]).then_inc(s_ev, 1)
                    act.wait_ge(s_ev, 2 * h + 2)
                    for k in range(T):
                        flat(h, k)
                        if k > 0:
                            exponential(T * h + k - 1)
                    exponential(T * h + T - 1)
                    store_sums(h, 1)

            for e in STAGES[1:]:
                sum_squares(e)
                if e == GAT_E:
                    take_roots(e)
                    high_weights(e, 0)
                    factors()
                    wide = act.value_load(wflag[0:1, 0:1], min_val=0, max_val=1)
                    with act.If(wide != 0):
                        wide_attention()
                    with act.Else():
                        attention()
                else:
                    for i in range(3 * KT):
                        high_means(e, i)
                        if i == 1:
                            take_roots(e)
                        if i in (2, 4):
                            high_weights(e, i // 2 - 1)
                if e < 8:
                    with act.Fori(0, T // 2) as i:
                        for u in range(2):
                            tile(e, 2 * i + u, u)
                            store_features(e, 2 * i + u, u)

        @block.vector
        def _(dve):
            chain = Chain(dve, s_dve)
            link = chain.link

            dve.wait_ge(s_const, 1)
            dve.wait_ge(s_idx, 32)
            link(nc.vector.tensor_copy(eallf[0:P], eall[0:P]))
            link(nc.vector.tensor_tensor(less[0:P], eallf[0:P, 0:1, :].broadcast_to([P, T, EC]),
                                         bounds[0:P, :].unsqueeze(2).broadcast_to([P, T, EC]), ALU.is_lt))
            nc.vector.reduce_sum(cnt[0:P, :], less[0:P], AX).then_inc(s_cnt, 1)
            dve.wait_ge(s_startps, 1)
            nc.vector.tensor_scalar(starts[0:1, :], rst[0:1, 0, 0:T], float(E - CAP), None, ALU.min).then_inc(s_starts, 1)

            class Steps:

                def __init__(self, base):
                    self.n = base

                def link(self, ins):
                    self.n = self.n + 1
                    ins.then_inc(s_ln, 1)
                    dve.wait_ge(s_ln, self.n)

            def invert_root(st, v, root, q, least, scale):
                st.link(nc.vector.reciprocal(q, root))
                st.link(nc.vector.tensor_scalar(q, v, q, root, ALU.mult, ALU.add))
                st.link(nc.vector.tensor_scalar(root, q, 0.5 / scale, least / scale, ALU.mult, ALU.max))
                st.link(nc.vector.reciprocal(root, root))

            def tile_begin(e, m, u):
                st = Steps(LN_BASE[e] + steps(e) * m)
                n = T * e + m
                if e in (0, GAT_E):
                    pass
                elif e == 8:
                    if m >= 2:
                        dve.wait_ge(s_out, m - 1)
                if HAS_RST[e]:
                    if e < 8:
                        dve.wait_ge(s_hp, n - 1)
                    r = first(e, HAS_RST) + m + 1
                    dve.wait_ge(s_rst, r)
                    nc.vector.scalar_tensor_tensor(out=Vb[0:P, u, :], in0=rst[0:P, u, :], scalar=unscale[0:P, e:e + 1],
                                                   in1=BB[0:P, :], op0=ALU.mult, op1=ALU.add).then_inc(s_v, 1)
                    dve.wait_ge(s_v, r)
                if e == 3:
                    st.link(nc.vector.tensor_tensor(X[0:P, m, :], X[0:P, m, :], Vb[0:P, u, :], ALU.add))
                if L2NORM[e]:
                    dve.wait_ge(s_sq, first(e, L2NORM) + m + 1)
                    sq, root, q = (small[0:P, u, i:i + 1] for i in range(3))
                    st.link(nc.vector.tensor_scalar(root, root, NORM_EPS, None, ALU.max))
                    invert_root(st, sq, root, q, NORM_EPS, 1.0 if e == 6 else UNIT_SCALE)
                    if e == 6:
                        st.link(nc.vector.scalar_tensor_tensor(out=X[0:P, m, :], in0=Rb[0:P, u, :], scalar=root,
                                                               in1=X[0:P, m, :], op0=ALU.mult, op1=ALU.add))
                if e == 8:
                    nc.vector.scalar_tensor_tensor(out=X[0:P, m, :], in0=Vb[0:P, u, :], scalar=0.0, in1=X[0:P, m, :],
                                                   op0=ALU.max, op1=ALU.add).then_inc(s_out, 1)
                if LAYERNORM[e]:
                    st.link(nc.vector.bn_stats(stat[0:P, u, :], X[0:P, m, :]))
                    st.link(nc.vector.bn_aggr(small[0:P, u, 4:6], stat[0:P, u, :]))
                    mean, var, root, q = (small[0:P, u, i:i + 1] for i in range(4, 8))
                    st.link(nc.vector.tensor_scalar(var, var, LN_EPS, None, ALU.add))
                    dve.wait_ge(s_root, first(e, LAYERNORM) + m + 1)
                    invert_root(st, var, root, q, NORM_EPS, LN_SCALE)
                    if n >= 2:
                        dve.wait_ge(s_hp, n - 1)
                    nc.vector.tensor_scalar(Vb[0:P, u, :], X[0:P, m, :], mean, root,
                                            ALU.subtract, ALU.mult).then_inc(s_pre, 1)

            def tile_end(e, m, u):
                n = T * e + m
                dve.wait_ge(s_hi, n + 1)
                if e in (4, 5):
                    f, scalar, op = Rb, small[0:P, u, 1:2], ALU.mult
                else:
                    f, scalar, op = Vb, 0.0, ALU.max
                    if LAYERNORM[e]:
                        dve.wait_ge(s_pre, first(e, LAYERNORM) + m + 1)
                nc.vector.scalar_tensor_tensor(out=HP[0:P, m, 1, :], in0=f[0:P, u, :], scalar=scalar, in1=HP[0:P, m, 0, :],
                                               op0=op, op1=ALU.subtract).then_inc(s_hp, 1)

            dve.wait_ge(s_ew, 32 * T)
            s_in = ew[:, 1].rearrange("p t c -> p (t c)")
            es_r, es_v = (es[:, i].rearrange("p t c -> p (t c)") for i in range(2))
            link(nc.vector.tensor_tensor(esd[:, :, :], ew[:, 0], bounds[:, :].unsqueeze(2).broadcast_to([128, T, CH]),
                                         ALU.subtract))
            link(nc.vector.tensor_scalar(tmpe[:, 0, :], s_in, float(R3), float(R3), ALU.is_ge, ALU.mult))
            link(nc.vector.tensor_scalar(tmpe[:, 1, :], s_in, float(2 * R3), float(R3), ALU.is_ge, ALU.mult))
            link(nc.vector.tensor_tensor(tmpe[:, 0, :], tmpe[:, 0, :], tmpe[:, 1, :], ALU.add))
            link(nc.vector.tensor_tensor(es_r, s_in, tmpe[:, 0, :], ALU.subtract))
            link(nc.vector.tensor_scalar(tmpe[:, 0, :], s_in, float(R3), 255.0, ALU.is_ge, ALU.mult))
            link(nc.vector.tensor_scalar(tmpe[:, 1, :], s_in, float(2 * R3), 65280.0, ALU.is_ge, ALU.mult))
            link(nc.vector.scalar_tensor_tensor(out=es_v, in0=tmpe[:, 0, :], scalar=1.0, in1=tmpe[:, 1, :],
                                                op0=ALU.add, op1=ALU.add))

            def one_hots(t, g):
                if 4 * t + g >= 2:
                    dve.wait_ge(s_ohu, 4 * t + g - 1)
                c0, n = chunks[g], GROUPS[g]
                nc.vector.tensor_tensor(ringd[:, g % 2, :, 0:n], iotac[:, :, 0:n],
                                        esd[:, t:t + 1, c0:c0 + n].broadcast_to([128, P, n]), ALU.is_equal)
                for c in range(n):
                    ins = nc.vector.tensor_scalar(rings[:, g % 2, c, 0:R3], iota[:, 0:R3], es[:, 0, t, c0 + c:c0 + c + 1],
                                                  es[:, 1, t, c0 + c:c0 + c + 1], ALU.is_equal, ALU.mult)
                ins.then_inc(s_ohr, 1)

            dve.wait_ge(s_x, 16)
            for t in range(T):
                one_hots(t, 0)
                tile_begin(0, t, t % 2)
                one_hots(t, 1)
                tile_end(0, t, t % 2)
                one_hots(t, 2)
                one_hots(t, 3)

            dve.wait_ge(s_dm, T)
            nc.vector.reduce_sum(degov[0:P, 0, :], deg3[0:P].rearrange("p q t -> p t q"), AX).then_inc(s_deg, 1)
            dve.wait_ge(s_degs, 1)
            nc.vector.reduce_sum(flagf[:, 0:1], rst[:, 0, 0:T], AX)
            link(nc.vector.reduce_sum(flagf[:, 1:2], rst[:, 0, T:2 * T], AX))
            link(nc.vector.tensor_scalar(flagf[:, 2:3], flagf[:, 0:1], float(E), None, ALU.not_equal))
            link(nc.vector.tensor_tensor(flagf[:, 3:4], flagf[:, 2:3], flagf[:, 1:2], ALU.add))
            link(nc.vector.tensor_scalar(flag[0:1, :], flagf[0:1, 3:4], 1.0, None, ALU.min))
            nc.vector.tensor_copy(flagf[:, 0:1], flagf[:, 3:4]).then_inc(s_flag, 1)
            general = dve.value_load(flag[0:1, 0:1], min_val=0, max_val=1)

            with dve.If(general != 0):
                dve.wait_ge(s_at, T)
                with dve.Fori(0, T) as t:
                    with dve.Fori(0, EC) as c:
                        nc.vector.tensor_scalar(goh[0:P, 0:P], iota[0:P, 0:P], eallf[0:P, 0, bass.ds(c, 1)], None, ALU.is_equal)
                        nc.vector.tensor_scalar(goh[0:P, 126:126 + N], iota[0:P, :], eallf[0:P, 1, bass.ds(c, 1)], None,
                                                ALU.is_equal).then_inc(g_ready, 1)
                        dve.wait_ge(g_used, EC * t + c + 1)
                    dve.wait_ge(g_tile, t + 1)
                    nc.vector.tensor_copy(gint[0:P, :], agg[0:P, 0, 0:N])
                    nc.vector.reduce_sum(degov[0:P, 0, bass.ds(t, 1)], agg[0:P, 0, 0:N], AX)
                    nc.vector.tensor_scalar(eallf[0:P, 0, :], eallf[0:P, 0, :], -float(P), None, ALU.add).then_inc(g_dve, 1)
                    dve.wait_ge(g_dve, t + 1)
                    b = gint[0:P, :].bitcast(U8).rearrange("p (n b) -> p n b", b=4)
                    nc.vector.tensor_copy(gdm[0:P, 0, 0:N], b[:, :, 0])
                    nc.vector.tensor_scalar(gdm[0:P, 1, 0:N], b[:, :, 1], 256.0, None, ALU.mult).then_inc(g_dm, 1)
                    for w in range(2):
                        dve.wait_ge(g_tp, 2 * t + w + 1)
                        to = AT if w == 0 else AH
                        for j in range(2):
                            ins = nc.vector.tensor_copy(to[0:P, 5 * j:5 * j + 5, bass.ds(P * t, P)], aps[0:P, j])
                        ins.then_inc(g_ev, 1)

            link(nc.vector.tensor_scalar(invc[0:P, :], degov[0:P, 0, :], 1.0, None, ALU.max))
            nc.vector.reciprocal(invc[0:P, :], invc[0:P, :]).then_inc(s_invc, 1)
            dve.wait_ge(s_invr, 1)
            nc.vector.tensor_copy(INV[:, :].rearrange("p (t n) -> p t n", t=T), rowv[:, 0]).then_inc(s_inv, 1)
            dve.wait_ge(s_inv, 1)

            def mean(e, i):
                n = 3 * KT * averaging(e) + i
                f, (lo, hi) = i // 3, THIRDS[i % 3]
                w = hi - lo
                dve.wait_ge(s_agg, n + 1)
                if n >= 2:
                    dve.wait_ge(s_nt, n - 1)
                nc.vector.tensor_tensor(NB[:, i % 2, 0:w], agg[:, 0, 512 * (i % 3):512 * (i % 3) + w], INV[:, lo:hi],
                                        ALU.mult).then_inc(s_mean, 1)

            def low_mean(e, i):
                n = 3 * KT * averaging(e) + i
                f, (lo, hi) = i // 3, THIRDS[i % 3]
                dve.wait_ge(s_nhi, n + 1)
                dve.wait_ge(s_mean, n + 1)
                nc.vector.tensor_tensor(NT[:, 1, f, lo:hi], NB[:, i % 2, 0:hi - lo], NT[:, 0, f, lo:hi],
                                        ALU.subtract).then_inc(s_nt, 1)

            def square_norms(e):
                dve.wait_ge(s_normps, e)
                f = roots[:, 0, 0:1]
                if mats[e] == 2:
                    link(nc.vector.tensor_copy(flagf[:, 0:2], rst[:, 0, 0:2]))
                    ins = nc.vector.tensor_scalar(f, flagf[:, 0:1], flagf[:, 1:2], 1e-24, ALU.add, ALU.max)
                else:
                    ins = nc.vector.tensor_scalar(f, rst[:, 0, 0:1], 1e-24, None, ALU.max)
                if DYNAMIC[e]:
                    link(ins)
                    link(nc.vector.tensor_scalar(flagf[0:P, 2:3], norms[0:P, 2:3], 2.0, None, ALU.mult))
                    link(nc.vector.tensor_scalar(flagf[0:P, 3:4], f[0:P], bound4[0:P, e - 1:e], 2.0 ** 40, ALU.mult, ALU.mult))
                    link(nc.vector.tensor_tensor(roots[0:P, 0, 1:2], flagf[0:P, 3:4], flagf[0:P, 2:3], ALU.add))
                    ins = nc.vector.tensor_scalar(bound4[0:P, e:e + 1], roots[0:P, 0, 1:2], 4.0, None, ALU.mult)
                ins.then_inc(s_sq2, 1)

            def set_scales(e):
                dve.wait_ge(s_roots, e)
                bits = roots[:, 1, :].bitcast(I32)
                c = 2 if DYNAMIC[e] else 1
                link(nc.vector.tensor_scalar(bits[:, 0:c], bits[:, 0:c], EXPONENT, EXPONENT, ALU.bitwise_and, ALU.bitwise_xor))
                link(nc.vector.tensor_scalar(scale_w[:, e:e + 1], roots[:, 1, 0:1], 2.0 ** (13 - 20), None, ALU.mult))
                if DYNAMIC[e]:
                    link(nc.vector.tensor_scalar(scale_o[0:P, e:e + 1], roots[0:P, 1, 1:2], 2.0 ** 13, None, ALU.mult))
                    link(nc.vector.tensor_scalar(BB[0:P, :], BB[0:P, :], scale_o[0:P, e:e + 1], None, ALU.mult))
                before = scale_o[0:P, e - 1:e] if DYNAMIC[e - 1] else OUT_SCALE[e - 1]
                u = unscale[0:P, e:e + 1]
                link(nc.vector.tensor_scalar(u, scale_w[0:P, e:e + 1], before, None, ALU.mult))
                ui = u.bitcast(I32)
                link(nc.vector.tensor_scalar(ui, ui, EXPONENT, EXPONENT, ALU.bitwise_and, ALU.bitwise_xor))
                after = scale_o[0:P, e:e + 1] if DYNAMIC[e] else 1.0
                link(nc.vector.tensor_scalar(u, u, 0.5, after, ALU.mult, ALU.mult))
                nc.vector.tensor_copy(flagf[:, 0:1], scale_w[:, e:e + 1]).then_inc(s_scale, 1)

            def low_weights(e, s):
                dve.wait_ge(s_whi, sum(mats[:e]) + s + 1)
                nc.vector.scalar_tensor_tensor(out=W16[:, s, 1, :, :].rearrange("p k n -> p (k n)"), in0=RW[:, s, :],
                                               scalar=scale_w[:, e:e + 1], in1=W16[:, s, 0, :, :].rearrange("p k n -> p (k n)"),
                                               op0=ALU.mult, op1=ALU.subtract).then_inc(s_wlo, 1)

            def scores():
                dve.wait_ge(s_b, b_after[GAT_E])
                for m in range(T):
                    dve.wait_ge(s_wx, m + 1)
                    nc.vector.scalar_tensor_tensor(out=WX[0:P, m, :, 0:DH], in0=rst[0:P, m % 2, :].rearrange("p (h n) -> p h n", h=HEADS),
                                                   scalar=unscale[0:P, GAT_E:GAT_E + 1],
                                                   in1=BB[0:P, :].rearrange("p (h n) -> p h n", h=HEADS),
                                                   op0=ALU.mult, op1=ALU.add).then_inc(s_wxv, 1)
                    dve.wait_ge(s_wxv, m + 1)
                    for s in range(2):
                        v = Rb if s == 0 else Vb
                        link(nc.vector.tensor_tensor(v[0:P, m % 2, :].rearrange("p (h n) -> p h n", h=HEADS), WX[0:P, m, :, 0:DH],
                                                     attn_s[0:P, s, :].rearrange("p (h n) -> p h n", h=HEADS), ALU.mult))
                        link(nc.vector.reduce_sum(tds[0:P, s, m, :], v[0:P, m % 2, :].rearrange("p (h n) -> p h n", h=HEADS), AX))
                td, ts = tds[0:P, 0], tds[0:P, 1]
                link(nc.vector.tensor_tensor(td, td, abias[0:P, :].unsqueeze(1).broadcast_to([P, T, HEADS]), ALU.add))
                nc.vector.tensor_scalar(tsl[0:P], ts, SLOPE, None, ALU.mult).then_inc(s_sc, 1)
                link(nc.vector.tensor_scalar(fac[0:P, 0], ts, -1.0, None, ALU.mult))
                nc.vector.tensor_reduce(ext[0:P, 0, :], ts.rearrange("p t h -> p h t"), AX, ALU.max)
                nc.vector.tensor_reduce(ext[0:P, 1, :], fac[0:P, 0].rearrange("p t h -> p h t"), AX, ALU.max).then_inc(s_ext, 1)
                dve.wait_ge(s_all, 1)
                most = extall[0:P, 0:1, :].broadcast_to([P, T, HEADS])
                link(nc.vector.tensor_tensor(flag8[:, :], extall[:, 0, :], extall[:, 1, :], ALU.add))
                link(nc.vector.tensor_reduce(flagf[:, 0:1], flag8[:, :], AX, ALU.max))
                link(nc.vector.tensor_scalar(wflag[0:1, :], flagf[0:1, 0:1], WIDE, None, ALU.is_ge))
                link(nc.vector.tensor_tensor(fac[0:P, 2], td, most, ALU.add))
                link(nc.vector.tensor_scalar(fac[0:P, 2], fac[0:P, 2], SLOPE - 1.0, RATIO_MAX, ALU.mult, ALU.min))
                nc.vector.tensor_tensor(fac[0:P, 0], ts, most, ALU.subtract).then_inc(s_dif, 1)
                dve.wait_ge(s_dif, 1)

            def maxima(high, wl):
                td = tds[0:P, 0]
                mask = slots[0:P, 2, 0:625].bitcast(BF16).rearrange("p (t n) -> p t n", t=T)
                mask2 = slots[0:P, 3, 0:625].bitcast(BF16).rearrange("p (t n) -> p t n", t=T)
                turns = 2 if high else 1
                for h in range(HEADS):
                    dve.wait_ge(s_tsr, h + 1)
                    for t in range(T):
                        for w in range(turns):
                            dve.wait_ge(s_ct, turns * (T * h + t) + w + 1)
                            for j in range(2):
                                ins = nc.vector.tensor_scalar((mask2 if w else mask)[:, 5 * j:5 * j + 5], aps[0:P, j], 0.0, NEVER,
                                                              ALU.is_equal, ALU.mult)
                            ins.then_inc(s_mk, 1)
                            dve.wait_ge(s_mk, turns * (T * h + t) + w + 1)
                        if high:
                            wl(nc.vector.tensor_tensor(mask, mask, mask2, ALU.max))
                        nc.vector.tensor_tensor_reduce(slots[0:P, 0, :].rearrange("p (t n) -> p t n", t=T), mask, rowv[0:P, h % 2],
                                                       1.0, NEVER, ALU.add, ALU.max, smax[0:P, t, h:h + 1]).then_inc(s_mx, 1)
                        dve.wait_ge(s_mx, T * h + t + 1)
                z, lz = ab[0:P, 0], ab[0:P, 2]
                wl(nc.vector.tensor_scalar(z, smax[0:P], NEVER / 2, None, ALU.is_ge))
                wl(nc.vector.tensor_tensor(smax[0:P], smax[0:P], z, ALU.mult))
                wl(nc.vector.tensor_tensor(z, td, smax[0:P], ALU.add))
                wl(nc.vector.scalar_tensor_tensor(out=lz, in0=z, scalar=SLOPE, in1=z, op0=ALU.mult, op1=ALU.max))
                wl(nc.vector.tensor_tensor(ab[0:P, 0], td, lz, ALU.subtract))
                nc.vector.scalar_tensor_tensor(out=ab[0:P, 1], in0=td, scalar=SLOPE, in1=lz, op0=ALU.mult,
                                               op1=ALU.subtract).then_inc(s_ab, 1)

            def add_head(h, fl):
                for i, (a, b) in enumerate(HALVES):
                    dve.wait_ge(s_nut, 2 * h + i + 1)
                    fl(nc.vector.tensor_scalar(den[0:P, a:b], nups[i][0:P, 0:b - a, DH], 1e-30, None, ALU.max))
                    fl(nc.vector.reciprocal(den[0:P, a:b], den[0:P, a:b]))
                    fl(nc.vector.tensor_tensor(share[0:P, 0:b - a, :], nups[i][0:P, 0:b - a, 0:DH],
                                               den[0:P, a:b].unsqueeze(2).broadcast_to([P, b - a, DH]), ALU.mult))
                    to = X[0:P, a:b, DH * h:DH * h + DH]
                    ins = nc.vector.tensor_tensor(to, to, share[0:P, 0:b - a, :], ALU.add)
                    ins.then_inc(s_xh, 1)
                    dve.wait_ge(s_xh, 2 * h + i + 1)

            def weigh(j, s, to, counts_scalar, op, high, gl):
                k = j % T
                ins = nc.vector.scalar_tensor_tensor(out=to, in0=s, scalar=counts_scalar, in1=AT[0:P, k, :], op0=op, op1=ALU.mult)
                if high:
                    gl(ins)
                    gl(nc.vector.scalar_tensor_tensor(out=s, in0=s, scalar=counts_scalar, in1=AH[0:P, k, :], op0=op, op1=ALU.mult))
                    ins = nc.vector.tensor_tensor(to, to, s, ALU.add)
                ins.then_inc(s_p, 1)

            def edge_weights_factored(high):
                gl = Chain(dve, g_dve, T).link
                fl = Chain(dve, s_fin).link
                for j in range(HEADS * T):
                    h, k = divmod(j, T)
                    dve.wait_ge(s_r, j + 1)
                    if j >= 2:
                        dve.wait_ge(s_pu, j - 1)
                    weigh(j, slots[0:P, j % 4, :], slots[0:P, 4 + j % 2, :], fac[0:P, 4, k, h:h + 1], ALU.add, high, gl)
                    if k == T - 1 and h > 0:
                        add_head(h - 1, fl)
                add_head(HEADS - 1, fl)

            def edge_weights_wide(high, wl):
                gl = Chain(dve, g_dve, T).link

                def exponent(j):
                    h, k = divmod(j, T)
                    dve.wait_ge(s_lin, j + 1)
                    s = slots[0:P, j % 4, :]
                    nc.vector.scalar_tensor_tensor(out=s, in0=rows[0:P, 0, :], scalar=tds[0:P, 1, k, h:h + 1], in1=s,
                                                   op0=ALU.add, op1=ALU.max).then_inc(s_q, 1)

                def edge_weights(j):
                    dve.wait_ge(s_e, j + 1)
                    if j >= 2:
                        dve.wait_ge(s_pu, j - 1)
                    weigh(j, slots[0:P, j % 4, :], slots[0:P, 4 + j % 2, :], 1.0, ALU.min, high, gl)

                for h in range(HEADS):
                    dve.wait_ge(s_ev, 2 * h + 2)
                    for j in range(T * h, T * h + T):
                        exponent(j)
                        if j > T * h:
                            edge_weights(j - 1)
                    edge_weights(T * h + T - 1)
                    add_head(h, wl)

            for e in STAGES[1:]:
                if e == GAT_E:
                    square_norms(e)
                    set_scales(e)
                    low_weights(e, 0)
                    scores()
                    wide = dve.value_load(wflag[0:1, 0:1], min_val=0, max_val=1)
                    with dve.If(wide != 0):
                        with dve.If(general != 0):
                            wl = Chain(dve, s_wide).link
                            maxima(True, wl)
                            edge_weights_wide(True, wl)
                        with dve.Else():
                            wl = Chain(dve, s_wide).link
                            maxima(False, wl)
                            edge_weights_wide(False, wl)
                    with dve.Else():
                        dve.wait_ge(s_fac, 2)
                        with dve.If(general != 0):
                            edge_weights_factored(True)
                        with dve.Else():
                            edge_weights_factored(False)
                else:
                    for i in range(3 * KT):
                        mean(e, i)
                        low_mean(e, i)
                        if i == 1:
                            square_norms(e)
                            set_scales(e)
                        if i in (2, 4):
                            low_weights(e, i // 2 - 1)
                if e != GAT_E:
                    dve.wait_ge(s_b, b_after[e])
                if LAYERNORM[e] or e == 8:
                    for m in range(T):
                        tile_begin(e, m, m % 2)
                        if e < 8:
                            tile_end(e, m, m % 2)
                else:
                    with dve.Fori(0, T // 2) as i:
                        for u in range(2):
                            tile_begin(e, 2 * i + u, u)
                            tile_end(e, 2 * i + u, u)

        @block.tensor
        def _(pe):
            pe.wait_ge(s_const, 1)
            pe.wait_ge(s_cnt, 1)
            nc.tensor.matmul(rst[0:1, 0, 0:T], ones[0:P, 0:1], cnt[0:P, :], start=True, stop=True).then_inc(s_startps, 1)

            def count(t, g):
                if g == 0 and t >= 2:
                    pe.wait_ge(s_cint, t - 1)
                pe.wait_ge(s_ohr, 4 * t + g + 1)
                for c in range(GROUPS[g]):
                    ins = nc.tensor.matmul(agg[0:P, t % 2, 0:R3], ringd[:, g % 2, :, c], rings[:, g % 2, c, 0:R3],
                                           start=(g == 0 and c == 0), stop=(g == 3 and c == GROUPS[g] - 1))
                ins.then_inc(s_ohu, 1)

            def transpose_counts(t):
                pe.wait_ge(s_dm, t + 1)
                pe.wait_ge(s_starts, 1)
                if t > 0:
                    pe.wait_ge(s_at, t)
                for k in range(T):
                    ins = nc.tensor.transpose(aps[0:P, k // 5, k % 5], DM[0:P, P * k:P * k + P], ident16[0:P, 0:P])
                ins.then_inc(s_tp, 1)

            def transpose_features(e, m, u):
                n = T * e + m
                pe.wait_ge(s_hp, n + 1)
                if n >= 2:
                    pe.wait_ge(s_ht, n - 1)
                for w in range(2):
                    for f in range(KT):
                        ins = nc.tensor.transpose(hps[u][:, w, f], HP[0:P, m, w, 128 * f:128 * f + 128], identh[0:P, 0:P])
                ins.then_inc(s_tr, 1)

            pe.wait_ge(s_const, 2)
            for t in range(T):
                count(t, 0)
                if t > 0:
                    transpose_counts(t - 1)
                count(t, 1)
                count(t, 2)
                transpose_features(0, t, t % 2)
                count(t, 3)
            transpose_counts(T - 1)

            pe.wait_ge(s_deg, 1)
            pe.wait_ge(s_at, T)
            nc.tensor.matmul(rst[:, 0, 0:2 * T], ones[0:P, :], degov[0:P, :, :].rearrange("p s t -> p (s t)"),
                             start=True, stop=True).then_inc(s_degs, 1)
            pe.wait_ge(s_flag, 1)
            general = pe.value_load(flag[0:1, 0:1], min_val=0, max_val=1)

            with pe.If(general != 0):
                with pe.Fori(0, T) as t:
                    for a, b in COLS:
                        nc.tensor.matmul(agg[0:P, 0, a:b], zeros16[0:P, 0:P], iota[0:P, a:b], start=True, stop=False)
                    with pe.Fori(0, EC) as c:
                        pe.wait_ge(g_ready, EC * t + c + 1)
                        for a, b in COLS:
                            ins = nc.tensor.matmul(agg[0:P, 0, a:b], goh[0:P, 0:P], goh[0:P, 126 + a:126 + b],
                                                   start=False, stop=False)
                        ins.then_inc(g_used, 1)
                    for a, b in COLS:
                        ins = nc.tensor.matmul(agg[0:P, 0, a:b], zeros16[0:P, 0:P], iota[0:P, a:b], start=False, stop=True)
                    ins.then_inc(g_tile, 1)
                    pe.wait_ge(g_dm, t + 1)
                    for w in range(2):
                        for k in range(T):
                            ins = nc.tensor.transpose(aps[0:P, k // 5, k % 5], gdm[0:P, w, P * k:P * k + P], ident16[0:P, 0:P])
                        ins.then_inc(g_tp, 1)
                        pe.wait_ge(g_ev, 2 * t + w + 1)
            pe.wait_ge(s_invc, 1)
            for t in range(T):
                ins = nc.tensor.transpose(rowv[:, 0, t], invc[0:P, t:t + 1].broadcast_to([P, 128]), ident[0:P, 0:P])
            ins.then_inc(s_invr, 1)
            pe.wait_ge(s_inv, 1)

            def norm_products(e):
                pe.wait_ge(s_norm, e)
                nc.tensor.matmul(rst[:, 0, 0:mats[e]], ones[:, :], norms[:, 0:mats[e]], start=True, stop=True).then_inc(s_normps, 1)

            def sum_neighbours(e):
                a = averaging(e)

                def products(f, k, i, counts, start, stop):
                    lo, hi = THIRDS[i]
                    for w in range(2):
                        ins = nc.tensor.matmul(agg[:, 0, 512 * i:512 * i + hi - lo], HP[0:P, k, w, bass.ds(128 * f, 128)],
                                               counts[0:P, k, lo:hi], start=(start and w == 0), stop=(stop and w == 1))
                    return ins

                def block_of_features(f, opening):
                    for i in range(3):
                        if opening and i == 0:
                            pe.wait_ge(s_hp, T * (e - 1) + 1)
                        if not opening:
                            pe.wait_ge(s_mean, 3 * (KT * a + f - 1) + i + 1)
                        products(f, 0, i, AT, True, False)
                        for k in range(1, T):
                            if opening and i == 0:
                                pe.wait_ge(s_hp, T * (e - 1) + k + 1)
                            if k == T - 1:
                                with pe.If(general != 0):
                                    for kh in range(T):
                                        products(f, kh, i, AH, False, False)
                            ins = products(f, k, i, AT, False, k == T - 1)
                        ins.then_inc(s_agg, 1)
                        if opening and i == 0 and e > 1:
                            transpose_features(e - 1, T - 1, 1)
                        if opening and i == 1:
                            norm_products(e)

                block_of_features(0, True)
                with pe.Fori(1, KT) as f:
                    block_of_features(f, False)

            def layer_products(out_ap, m, sides):
                pairs = [(s, w, v, k) for s in range(len(sides)) for w, v in ((0, 0), (1, 0), (0, 1)) for k in range(KT)]
                for i, (s, w, v, k) in enumerate(pairs):
                    ins = nc.tensor.matmul(out_ap, sides[s][:, w, k, bass.ds(P * m, P)], W16[:, s, v, k, :],
                                           start=(i == 0), stop=(i == len(pairs) - 1))
                return ins

            def layer_tile(e, m, u):
                n = first(e, HAS_RST) + m
                if not isinstance(n, int) or n >= 2:
                    pe.wait_ge(s_v, n - 1)
                layer_products(rst[0:P, u, :], m, (HT, NT)).then_inc(s_rst, 1)

            def project():
                transpose_features(6, T - 1, 1)
                norm_products(GAT_E)
                pe.wait_ge(s_sq2, GAT_E)
                pe.wait_ge(s_wlo, sum(mats[:GAT_E + 1]))
                pe.wait_ge(s_ht, T * GAT_E)
                for m in range(T):
                    if m >= 2:
                        pe.wait_ge(s_wxv, m - 1)
                    layer_products(rst[0:P, m % 2, :], m, (HT,)).then_inc(s_wx, 1)

            def source_rows(high):
                turns = 2 if high else 1
                pe.wait_ge(s_sc, 1)
                for h in range(HEADS):
                    if h >= 2:
                        pe.wait_ge(s_mx, T * (h - 1))
                    for t in range(T):
                        ins = nc.tensor.transpose(rowv[:, h % 2, t], tds[0:P, 1, t, h:h + 1].broadcast_to([P, 128]), ident[0:P, 0:P])
                    ins.then_inc(s_tsr, 1)
                    for t in range(T):
                        for w in range(turns):
                            n = turns * (T * h + t) + w
                            if n > 0:
                                pe.wait_ge(s_mk, n)
                            for k in range(T):
                                ins = nc.tensor.transpose(aps[0:P, k // 5, k % 5], (AH if w else AT)[0:P, k, P * t:P * t + P],
                                                          ident16[0:P, 0:P])
                            ins.then_inc(s_ct, 1)

            def sum_head(h, k, o):
                j = T * h + k
                pe.wait_ge(s_p, j + 1)
                for a, b in COLS:
                    ins = nc.tensor.matmul(agg[0:DH + 1, o, a:b], WX[0:P, k, h, :], slots[0:P, 4 + j % 2, a:b],
                                           start=(k == 0), stop=(k == T - 1))
                ins.then_inc(s_pu, 1)

            def turn_sums(h, i):
                a, b = HALVES[i]
                pe.wait_ge(s_nu, h + 1)
                if h > 0:
                    pe.wait_ge(s_xh, 2 * h - 1 + i)
                for t in range(a, b):
                    ins = nc.tensor.transpose(nups[i][0:P, t - a, :], NU[0:DH + 1, P * t:P * t + P], ident[0:DH + 1, 0:DH + 1])
                ins.then_inc(s_nut, 1)

            def attend():
                def ratio_row(h, i):
                    if i == 2:
                        pe.wait_ge(s_re, 3 * h + 1)
                    elif h >= 3:
                        pe.wait_ge(s_xh, 2 * (h - 2) - i)
                    elif h >= 1:
                        pe.wait_ge(s_re, 3 * h - i)
                    for t in range(4 * i, min(4 * i + 4, T)):
                        ins = nc.tensor.transpose(rhop[i % 2][:, t - 4 * i], fac[0:P, 2, t, h:h + 1].broadcast_to([P, 128]), ident[0:P, 0:P])
                    ins.then_inc(s_rho, 1)

                pe.wait_ge(s_fac, 2)
                for i in range(3):
                    ratio_row(0, i)
                for h in range(HEADS):
                    if h > 1:
                        pe.wait_ge(s_nu, h - 1)
                    for k in range(T):
                        sum_head(h, k, h % 2)
                        if h + 1 < HEADS and k in (3, 6):
                            for i in ((0, 1) if k == 3 else (2,)):
                                ratio_row(h + 1, i)
                        if h > 0 and k == 7:
                            pe.wait_ge(s_re, min(3 * (h + 1) + 2, 3 * HEADS))
                            turn_sums(h - 1, 0)
                        if h > 0 and k == 8:
                            pe.wait_ge(s_re, min(3 * (h + 1) + 3, 3 * HEADS))
                            turn_sums(h - 1, 1)
                for i in range(2):
                    turn_sums(HEADS - 1, i)

            def attend_wide():
                def score_rows(h, s):
                    if 2 * h + s > 0:
                        pe.wait_ge(s_ev, 2 * h + s)
                    for t in range(T):
                        ins = nc.tensor.transpose(rowv[:, 0, t], ab[0:P, s, t, h:h + 1].broadcast_to([P, 128]), ident[0:P, 0:P])
                    ins.then_inc(s_row, 1)

                pe.wait_ge(s_ab, 1)
                for h in range(HEADS):
                    for s in range(2):
                        score_rows(h, s)
                    if h > 0:
                        pe.wait_ge(s_nu, h)
                    for k in range(T):
                        sum_head(h, k, 1)
                    for i in range(2):
                        turn_sums(h, i)

            for e in STAGES[1:]:
                if e == GAT_E:
                    project()
                    pe.wait_ge(s_one, 1)
                    pe.wait_ge(s_dif, 1)
                    wide = pe.value_load(wflag[0:1, 0:1], min_val=0, max_val=1)
                    with pe.If(wide != 0):
                        with pe.If(general != 0):
                            source_rows(True)
                        with pe.Else():
                            source_rows(False)
                        attend_wide()
                    with pe.Else():
                        attend()
                    for m in range(T - 1):
                        transpose_features(e, m, m % 2)
                    continue
                sum_neighbours(e)
                pe.wait_ge(s_wlo, sum(mats[:e + 1]))
                pe.wait_ge(s_ht, T * e)
                pe.wait_ge(s_nt, 3 * KT * (averaging(e) + 1))
                for m in range(T):
                    layer_tile(e, m, m % 2)
                    if m > 0 and e < 8:
                        transpose_features(e, m - 1, (m - 1) % 2)


def kernel(x, src, dst, L0_gnn_Ws_self, L0_gnn_Ws_neigh, L0_gnn_bs, L1_gnn_W_self, L1_gnn_W_neigh, L1_gnn_b,
           L2_gnn_Ws, L2_gnn_Wb, L2_gnn_a_w, L2_gnn_a_b, L3_gnn_W_self, L3_gnn_W_neigh, L3_gnn_b):
    import numpy as np
    import concourse.bacc as bacc
    from concourse.bass_utils import run_bass_kernel_spmd

    def rows_first(w):
        return np.asarray(w).reshape(KT, 128, D).transpose(1, 0, 2).reshape(128, KT * D)

    mats = []
    for selfs, neighs in ((L0_gnn_Ws_self, L0_gnn_Ws_neigh), (L1_gnn_W_self, L1_gnn_W_neigh)):
        for l in range(3):
            mats += [rows_first(selfs[l]), rows_first(neighs[l])]
    mats.append(rows_first(np.asarray(L2_gnn_Ws).transpose(1, 0, 2).reshape(D, D)))
    mats += [rows_first(np.asarray(L3_gnn_W_self).T), rows_first(np.asarray(L3_gnn_W_neigh).T)]
    a_w = np.asarray(L2_gnn_a_w)
    arrays = {
        "x": np.ascontiguousarray(x),
        "src": np.ascontiguousarray(src),
        "dst": np.ascontiguousarray(dst),
        "weights": np.ascontiguousarray(np.stack(mats)),
        "biases": np.concatenate([np.asarray(L0_gnn_bs), np.asarray(L1_gnn_b), np.asarray(L2_gnn_Wb).reshape(1, D),
                                  np.asarray(L3_gnn_b).reshape(1, D)]),
        "attn": np.stack([np.ascontiguousarray(a_w[:, :DH]).reshape(D), np.ascontiguousarray(a_w[:, DH:]).reshape(D)]),
        "attn_b": np.ascontiguousarray(L2_gnn_a_b).reshape(1, HEADS),
    }
    nc = bacc.Bacc("TRN2", target_bir_lowering=False, num_devices=1)
    args = [nc.dram_tensor(k, a.shape, mybir.dt.from_np(a.dtype), kind="ExternalInput").ap() for k, a in arrays.items()]
    out = nc.dram_tensor("out", (N, D), F32, kind="ExternalOutput").ap()
    gnn_kernel(nc, *args, out)
    r = run_bass_kernel_spmd(nc, [arrays], core_ids=[0])
    return r.results[0]["out"]
```

```python
import concourse.bass as bass
from concourse import mybir
from concourse.alu_op_type import AluOpType as ALU
from contextlib import ExitStack

F32 = mybir.dt.float32
BF16 = mybir.dt.bfloat16
F16 = mybir.dt.float16
I32 = mybir.dt.int32
U8 = mybir.dt.uint8
ACT = mybir.ActivationFunctionType
AX = mybir.AxisListType.X
MAX = bass.bass_isa.ReduceOp.max

N, D, E = 1250, 512, 40000
P = 125
T = N // P
KT = D // 128
HEADS, DH = 8, 64
EC = E // P
GROUPS = [10, 8, 8, 8]
GMAX = max(GROUPS)
CH = sum(GROUPS)
CAP = CH * 128
SHARED = [0, 0, 2, 2]
EARLY = 3
R3 = 417
LN_EPS, NORM_EPS = 1e-5, 1e-12
NEVER = -3e38
SLOPE = 0.2
WIDE = 40.0
RATIO_MAX = 50.0
COLS = [(0, 512), (512, 1024), (1024, N)]
THIRDS = [(0, 417), (417, 834), (834, N)]
HALVES = [(0, 7), (7, T)]

LN_SCALE, UNIT_SCALE = 1024.0, 32768.0
LN_NORM2 = 520.0
EXPONENT = 0x7F800000

STAGES = range(9)
GAT_E = 7
HAS_RST = [e not in (0, GAT_E) for e in STAGES]
L2NORM = [e in (4, 5, 6) for e in STAGES]
LAYERNORM = [e in (0, 3, 6, 7) for e in STAGES]
DYNAMIC = [e in (1, 2) for e in STAGES]
OUT_SCALE = [LN_SCALE if LAYERNORM[e] else UNIT_SCALE for e in STAGES]


def first(e, table):
    return T * sum(table[:e])


def averaging(e):
    return e - 1 if e < 8 else 6


def steps(e):
    return (e == 3) + 5 * L2NORM[e] + (e == 6) + 7 * LAYERNORM[e]


LN_BASE = [T * sum(steps(i) for i in range(e)) for e in STAGES]


def late(e):
    return 0 if e == 0 else T if e == GAT_E else 2 if LAYERNORM[e] or L2NORM[e] else 1


class Chain:

    def __init__(self, eng, sem, n=0):
        self.eng, self.sem, self.n = eng, sem, n

    def link(self, ins):
        self.n = self.n + 1
        ins.then_inc(self.sem, 1)
        self.eng.wait_ge(self.sem, self.n)


def gnn_kernel(nc, x, src, dst, weights, biases, attn, attn_b, out):
    with ExitStack() as ctx:
        def sb(name, shape, dt):
            return ctx.enter_context(nc.sbuf_tensor(name, shape, dt))

        def sem(name):
            return ctx.enter_context(nc.semaphore(name))

        X = sb("X", [128, T, D], F32)
        AT = sb("AT", [128, T, N], BF16)
        AH = sb("AH", [128, T, N], BF16)
        INV = sb("INV", [128, N], F32)
        BB = sb("BB", [128, D], F32)
        RW = sb("RW", [128, 2, KT * D], F32)
        WG = RW[:, 1, :].bitcast(F16).rearrange("p (w k n) -> p w k n", w=2, k=KT)
        iota = sb("iota", [128, N], F16)
        iotac = sb("iotac", [128, P, GMAX], F16)
        bounds = sb("bounds", [128, T], F32)
        ident = sb("ident", [128, 128], F32)
        ident16 = sb("ident16", [128, 128], BF16)
        identh = sb("identh", [128, 128], F16)
        ones = sb("ones", [128, 128], F32)
        zeros16 = sb("zeros16", [128, 128], BF16)
        small = sb("small", [128, 2, 16], F32)
        stat = sb("stat", [128, 2, 6], F32)
        stats = sb("stats", [128, T, 6], F32)
        moments = sb("moments", [128, T, 4], F32)
        cnt = sb("cnt", [128, T], F32)
        starts = sb("starts", [1, T], I32)
        deg3 = sb("deg3", [128, 3, T], F32)
        degov = sb("degov", [128, 2, T], F32)
        invc = sb("invc", [128, T], F32)
        flagf = sb("flagf", [128, 4], F32)
        flag = sb("flag", [1, 1], I32)
        norms = sb("norms", [128, 3], F32)
        roots = sb("roots", [128, 2, 2], F32)
        bound4 = sb("bound4", [128, 3], F32)
        scale_w = sb("scale_w", [128, 9], F32)
        scale_o = sb("scale_o", [128, 9], F32)
        unscale = sb("unscale", [128, 9], F32)
        tds = sb("tds", [128, 2, T, HEADS], F32)
        tsl = sb("tsl", [128, T, HEADS], F32)
        smax = sb("smax", [128, T, HEADS], F32)
        ab = sb("ab", [128, 3, T, HEADS], F32)
        abias = sb("abias", [128, HEADS], F32)
        ext = sb("ext", [128, 2, HEADS], F32)
        extall = sb("extall", [128, 2, HEADS], F32)
        flag8 = sb("flag8", [128, HEADS], F32)
        wflag = sb("wflag", [1, 1], I32)
        fac = sb("fac", [128, 5, T, HEADS], F32)
        den = sb("den", [128, T], F32)
        WV = sb("WV", [128, 6 * N], F32)
        W16 = WV[:, 0:4096].bitcast(F16).rearrange("p (s w k n) -> p s w k n", s=2, w=2, k=KT)
        Vb = WV[:, 4096:5120].rearrange("p (u n) -> p u n", u=2)
        Rb = WV[:, 5120:6144].rearrange("p (u n) -> p u n", u=2)
        NB = WV[:, 6144:6144 + 2 * R3].rearrange("p (u n) -> p u n", u=2)
        HN = sb("HN", [128, 10624], F32)
        HP = HN[:, 0:5120].bitcast(F16).rearrange("p (t w n) -> p t w n", t=T, w=2)
        NT = HN[:, 5120:10120].bitcast(F16).rearrange("p (w k n) -> p w k n", w=2, k=KT)
        HTf = sb("HT", [128, KT * N], F32)
        HT = HTf[:, :].bitcast(F16).rearrange("p (w k n) -> p w k n", w=2, k=KT)

        ringd = HN[:, 5120:5120 + P * GMAX].bitcast(BF16).rearrange("p (u n c) -> p u n c", u=2, c=GMAX)
        rings = HN[:, 6400:6400 + 2 * GMAX * 209].bitcast(BF16).rearrange("p (u c n) -> p u c n", u=2, c=GMAX)
        ew = INV[:, 0:2 * T * CH].bitcast(I32).rearrange("p (s t c) -> p s t c", s=2, t=T)
        es = WV[:, 0:2 * T * CH].rearrange("p (s t c) -> p s t c", s=2, t=T)
        esn = WV[:, 680:680 + T * CH].rearrange("p (t c) -> p t c", t=T)
        esm = WV[:, 1020:1020 + T * CH].rearrange("p (t c) -> p t c", t=T)
        esd = WV[:, 1360:1360 + T * CH // 2].bitcast(F16).rearrange("p (t c) -> p t c", t=T)
        eall = WV[:, 1800:1800 + 2 * EC].bitcast(I32).rearrange("p (s n) -> p s n", s=2)
        eallf = WV[:, 2440:2440 + 2 * EC].rearrange("p (s n) -> p s n", s=2)
        DM = WV[:, 3080:3080 + 626].bitcast(BF16)
        cint = WV[:, 7000:7000 + R3].bitcast(I32)
        less = WV[:, 4096:4096 + 1600].bitcast(BF16).rearrange("p (t n) -> p t n", t=T)
        tmpe = WV[:, 6144:6144 + 2 * T * CH].rearrange("p (s n) -> p s n", s=2)
        dist = WV[:, 6144:6144 + 2 * 209].bitcast(BF16).rearrange("p (c n) -> p c n", c=2)
        junk8 = WV[:, 3706:3706 + 210].bitcast(BF16)
        gint = HN[:, 6400:6400 + N].bitcast(I32)
        goh = HN[:, 8500:8500 + 700].bitcast(BF16)
        gdm = HN[:, 5120:5120 + 1252].bitcast(BF16).rearrange("p (w n) -> p w n", w=2)

        WX = HN[:, 0:T * HEADS * 65].rearrange("p (t h n) -> p t h n", t=T, h=HEADS)
        rows = HN[:, 5200:5200 + 2 * N].rearrange("p (s n) -> p s n", s=2)
        NU = HN[:, 7700:7700 + N]
        attn_s = HN[:, 8950:8950 + 2 * D].rearrange("p (s n) -> p s n", s=2)
        slots = WV[:, 0:6 * N].rearrange("p (s n) -> p s n", s=6)
        share = BB[:, 0:7 * DH].rearrange("p (t n) -> p t n", n=DH)

        agg = ctx.enter_context(nc.psum_tensor("agg", [128, 2, 1536], F32))
        rst = ctx.enter_context(nc.psum_tensor("rst", [128, 2, 512], F32))
        hps = [agg[:, 1, 512 * (1 + u):512 * (2 + u)].bitcast(F16)[:, 0:8 * 126]
               .rearrange("p (w k n) -> p w k n", w=2, k=KT)[:, :, :, 0:P] for u in range(2)]
        rowv = agg[:, :, 0:128 * T].rearrange("p s (t n) -> p s t n", t=T)[:, :, :, 0:P]
        aps = rst[:, :, :].bitcast(BF16)[:, :, 0:5 * 126].rearrange("p s (k n) -> p s k n", k=5)[:, :, :, 0:P]
        rhop = [rst[:, i, :].rearrange("p (t n) -> p t n", t=4)[:, :, 0:P] for i in range(2)]
        nups = [rst[:, 1 - i, 0:65 * 7].rearrange("p (t n) -> p t n", n=65) for i in range(2)]

        s_const = sem("constants_made")
        s_idx = sem("edge_lists_loaded")
        s_x = sem("x_loaded")
        s_w = sem("weights_loaded")
        s_b = sem("bias_loaded")
        s_ew = sem("destination_windows_loaded")
        s_ews = sem("source_windows_loaded")
        s_cnt = sem("edges_below_bounds_counted")
        s_startps = sem("window_starts_summed")
        s_starts = sem("window_starts_ready")
        s_esc = sem("edge_scalars_ready")
        s_ohr = sem("one_hots_ready")
        s_oha = sem("scalar_engines_one_hots_ready")
        s_sqd = sem("squared_distances_ready")
        s_ohu = sem("one_hots_used")
        s_cint = sem("packed_counts_read")
        s_dm = sem("counts_unpacked")
        s_tp = sem("counts_transposed")
        s_at = sem("counts_stored")
        s_deg = sem("degrees_ready")
        s_degs = sem("edges_summed")
        s_flag = sem("flag_ready")
        s_invc = sem("inverse_degrees_ready")
        s_invr = sem("inverse_degree_rows_in_psum")
        s_inv = sem("inverse_degree_rows_ready")
        g_ready = sem("general_one_hots_ready")
        g_used = sem("general_one_hots_used")
        g_tile = sem("general_tile_counted")
        g_dm = sem("general_counts_unpacked")
        g_tp = sem("general_counts_transposed")
        g_ev = sem("general_counts_stored")
        g_dve = sem("general_vector_step_done")
        s_dve = sem("vector_step_done")
        s_wide = sem("wide_vector_step_done")
        s_pool = sem("pool_step_done")
        s_ln = sem("statistics_step_done")
        s_norm = sem("squares_of_weights_summed")
        s_normps = sem("squared_norms_ready")
        s_sq2 = sem("squared_norms_stored")
        s_roots = sem("norms_ready")
        s_scale = sem("scales_ready")
        s_whi = sem("weights_high_parts_ready")
        s_wlo = sem("weights_low_parts_ready")
        s_agg = sem("neighbour_sums_ready")
        s_mean = sem("neighbour_means_ready")
        s_nhi = sem("means_high_parts_ready")
        s_nt = sem("means_parts_ready")
        s_rst = sem("layer_tile_ready")
        s_v = sem("layer_tile_read")
        s_relu = sem("rectified")
        s_sum = sem("squares_summed")
        s_sq = sem("row_norms_ready")
        s_root = sem("deviations_ready")
        s_var = sem("all_variances_ready")
        s_dev = sem("all_deviations_ready")
        s_pre = sem("normalised_before_relu")
        s_hi = sem("high_parts_ready")
        s_hp = sem("feature_parts_ready")
        s_tr = sem("features_transposed")
        s_ht = sem("transposed_features_stored")
        s_wx = sem("projection_ready")
        s_wxv = sem("projection_stored")
        s_one = sem("ones_beside_projections")
        s_sc = sem("scores_ready")
        s_tsr = sem("source_score_rows_in_psum")
        s_ct = sem("counts_turned")
        s_mk = sem("mask_made")
        s_mx = sem("maxima_done")
        s_ab = sem("score_terms_ready")
        s_row = sem("score_rows_in_psum")
        s_ev = sem("score_rows_stored")
        s_ext = sem("partition_extremes_ready")
        s_all = sem("score_extremes_ready")
        s_dif = sem("exponents_of_factors_ready")
        s_fac = sem("factors_ready")
        s_rho = sem("ratio_rows_in_psum")
        s_re = sem("ratio_rows_stored")
        s_r = sem("excess_ready")
        s_lin = sem("flat_branch_ready")
        s_q = sem("exponents_ready")
        s_e = sem("exponentials_ready")
        s_p = sem("edge_weights_ready")
        s_pu = sem("edge_weights_used")
        s_nu = sem("head_sums_stored")
        s_nut = sem("head_sums_transposed")
        s_xh = sem("head_added")
        s_fin = sem("head_step_done")
        s_out = sem("output_rows_ready")
        s_st = sem("output_stored")

        b_after = [16 * sum(0 if i == 0 else 4 if i == GAT_E else 1 for i in range(e + 1)) for e in STAGES]
        w_after = [16 * sum(0 if i == 0 else 1 if i == GAT_E else 2 for i in range(e + 1)) for e in STAGES]
        mats = [0 if e == 0 else 1 if e == GAT_E else 2 for e in STAGES]
        chunks = [sum(GROUPS[:g]) for g in range(5)]

        def squares(e):
            return agg[:, 0, 0:2] if e == GAT_E else rst[:, 0, 0:2]

        def parts(e, s, w):
            return (WG[:, w] if e == GAT_E else W16[:, s, w]).rearrange("p k n -> p (k n)")

        block = ctx.enter_context(nc.Block())

        @block.sync
        def _(sp):
            sp.dma_start(eall[0:P, 0, :], dst.rearrange("(p c) -> p c", p=P)).then_inc(s_idx, 16)
            sp.dma_start(eall[0:P, 1, :], src.rearrange("(p c) -> p c", p=P)).then_inc(s_idx, 16)
            xv = x.rearrange("(t p) n -> p t n", p=P)
            sp.dma_start(X[0:P, :, :], xv).then_inc(s_x, 16)

            sp.wait_ge(s_starts, 1)
            for t in range(T):
                at = sp.value_load(starts[0:1, t:t + 1], min_val=0, max_val=E - CAP)
                sp.dma_start(ew[:, 0, t, :], dst[bass.ds(at, CAP)].rearrange("(p c) -> p c", p=128)).then_inc(s_ew, 16)

            n = 0
            for e in STAGES[1:]:
                if e > 1:
                    sp.wait_ge(s_wlo, sum(mats[:e]))
                if e == 8:
                    sp.wait_ge(s_wx, T)
                for s in range(mats[e]):
                    sp.dma_start(RW[:, s, :], weights[n]).then_inc(s_w, 16)
                    n += 1
                if e > 1:
                    sp.wait_ge(s_hp, T * e)
                sp.dma_start(BB[0:P, :], biases[e - 1:e, :].broadcast_to([P, D])).then_inc(s_b, 16)
                if e == GAT_E:
                    for s in range(2):
                        sp.dma_start(attn_s[0:P, s, :], attn[s:s + 1, :].broadcast_to([P, D])).then_inc(s_b, 16)
                    sp.dma_start(abias[0:P, :], attn_b[0:1, :].broadcast_to([P, HEADS])).then_inc(s_b, 16)

            outv = out.rearrange("(t p) n -> p t n", p=P)
            for m in range(T):
                sp.wait_ge(s_out, m + 1)
                sp.dma_start(outv[:, m, :], X[0:P, m, :]).then_inc(s_st, 16)
            sp.wait_ge(s_st, 16 * T)

        @block.gpsimd
        def _(pool):
            chain = Chain(pool, s_pool)
            nc.gpsimd.iota(bounds[:, :], [[P, T]], base=0, channel_multiplier=0, allow_small_or_imprecise_dtypes=True)
            nc.gpsimd.memset(ones[:, :], 1.0)
            nc.gpsimd.iota(iota[:, :], [[1, N]], base=0, channel_multiplier=0, allow_small_or_imprecise_dtypes=True)
            nc.gpsimd.iota(iotac[:, :, :], [[1, P], [0, GMAX]], base=0, channel_multiplier=0,
                           allow_small_or_imprecise_dtypes=True).then_inc(s_const, 1)
            nc.gpsimd.memset(zeros16[:, :], 0.0)
            nc.gpsimd.memset(ext[:, :, :], NEVER)
            nc.gpsimd.memset(roots[:, :, :], 1.0)
            nc.gpsimd.memset(bound4[:, 0:1], 4.0 * LN_NORM2)
            chain.link(nc.gpsimd.memset(ident[:, :], 0.0))
            chain.link(nc.gpsimd.affine_select(out=ident[:, :], in_=ident[:, :], compare_op=ALU.not_equal, fill=1.0,
                                               base=0, pattern=[[-1, 128]], channel_multiplier=1))
            nc.gpsimd.tensor_copy(ident16[:, :], ident[:, :])
            nc.gpsimd.tensor_copy(identh[:, :], ident[:, :]).then_inc(s_const, 1)

            pool.wait_ge(s_starts, 1)
            for t in range(T):
                at = pool.value_load(starts[0:1, t:t + 1], min_val=0, max_val=E - CAP)
                nc.gpsimd.dma_start(ew[:, 1, t, :], src[bass.ds(at, CAP)].rearrange("(p c) -> p c", p=128)).then_inc(s_ews, 16)

            pool.wait_ge(s_tr, T * GAT_E)
            nc.gpsimd.memset(WX[0:P, :, :, DH:DH + 1], 1.0).then_inc(s_one, 1)
            pool.wait_ge(s_ext, 1)
            nc.gpsimd.partition_all_reduce(extall[:, :, :].rearrange("p s h -> p (s h)"),
                                           ext[:, :, :].rearrange("p s h -> p (s h)"), 128, MAX).then_inc(s_all, 1)

        @block.scalar
        def _(act):
            def store_counts(t):
                act.wait_ge(s_tp, t + 1)
                for j in range(2):
                    ins = nc.scalar.copy(AT[0:P, 5 * j:5 * j + 5, P * t:P * t + P], aps[0:P, j])
                ins.then_inc(s_at, 1)

            def unpack(t):
                act.wait_ge(s_ohu, 4 * t + 4)
                nc.scalar.copy(cint[0:P, 0:R3], agg[0:P, t % 2, 0:R3]).then_inc(s_cint, 1)
                act.wait_ge(s_cint, t + 1)
                if t > 0:
                    store_counts(t - 1)
                b = cint[0:P, 0:R3].bitcast(U8).rearrange("p (n b) -> p n b", b=4)
                for q in range(3):
                    w = min(R3, N - R3 * q)
                    nc.scalar.activation(DM[0:P, R3 * q:R3 * q + w], b[:, 0:w, q], ACT.Copy,
                                         accum_out=deg3[0:P, q, t:t + 1])
                nc.scalar.activation(junk8[0:P, 0:R3], b[:, :, 3], ACT.Copy,
                                     accum_out=degov[0:P, 1, t:t + 1]).then_inc(s_dm, 1)
                act.wait_ge(s_dm, t + 1)

            def norms_of_rows(e, m, u):
                act.wait_ge(s_v, first(e, HAS_RST) + m + 1)
                nc.scalar.activation(Rb[0:P, u, :], Vb[0:P, u, :], ACT.Relu).then_inc(s_relu, 1)
                act.wait_ge(s_relu, first(e, L2NORM) + m + 1)
                nc.scalar.activation(Vb[0:P, u, :], Rb[0:P, u, :], ACT.Square,
                                     accum_out=small[0:P, u, 0:1]).then_inc(s_sum, 1)
                act.wait_ge(s_sum, first(e, L2NORM) + m + 1)
                nc.scalar.activation(small[0:P, u, 1:2], small[0:P, u, 0:1], ACT.Sqrt).then_inc(s_sq, 1)

            def deviation(e, m, u):
                act.wait_ge(s_ln, LN_BASE[e] + steps(e) * (m + 1) - 4)
                nc.scalar.activation(small[0:P, u, 6:7], small[0:P, u, 5:6], ACT.Sqrt).then_inc(s_root, 1)

            def high_part(e, m, u):
                if LAYERNORM[e]:
                    act.wait_ge(s_pre, first(e, LAYERNORM) + m + 1)
                    nc.scalar.activation(HP[0:P, m, 0, :], Vb[0:P, u, :], ACT.Relu).then_inc(s_hi, 1)
                elif L2NORM[e]:
                    act.wait_ge(s_ln, LN_BASE[e] + steps(e) * (m + 1))
                    nc.scalar.mul(HP[0:P, m, 0, :], Rb[0:P, u, :], small[0:P, u, 1:2]).then_inc(s_hi, 1)
                else:
                    act.wait_ge(s_v, first(e, HAS_RST) + m + 1)
                    nc.scalar.activation(HP[0:P, m, 0, :], Vb[0:P, u, :], ACT.Relu).then_inc(s_hi, 1)

            def store_features(e, m, u):
                act.wait_ge(s_tr, T * e + m + 1)
                nc.scalar.copy(HT[:, :, :, bass.ds(P * m, P)], hps[u]).then_inc(s_ht, 1)

            act.wait_ge(s_const, 2)
            for m in range(EARLY):
                deviation(0, m, m % 2)
                high_part(0, m, m % 2)
                if m > 0:
                    store_features(0, m - 1, (m - 1) % 2)
            def one_hots(t, g):
                if t == 0 and g == 2:
                    act.wait_ge(s_esc, 1)
                act.wait_ge(s_ohu, 4 * t + g - 1)
                n = 2 * t + g - 2
                if n > 0:
                    act.wait_ge(s_oha, n)
                for i in range(SHARED[g]):
                    c = chunks[g] + GROUPS[g] - SHARED[g] + i
                    ins = nc.scalar.activation(dist[:, i, 0:R3], iota[:, 0:R3], ACT.Square, bias=esn[:, t, c:c + 1])
                ins.then_inc(s_sqd, 1)
                act.wait_ge(s_sqd, n + 1)
                for i in range(SHARED[g]):
                    c = chunks[g] + GROUPS[g] - SHARED[g] + i
                    ins = nc.scalar.activation(rings[:, g % 2, c - chunks[g], 0:R3], dist[:, i, 0:R3], ACT.Relu,
                                               bias=es[:, 1, t, c:c + 1], scale=esm[:, t, c:c + 1])
                ins.then_inc(s_oha, 1)

            for t in range(T):
                m = t + EARLY
                if m < T:
                    deviation(0, m, m % 2)
                one_hots(t, 2)
                if m < T:
                    high_part(0, m, m % 2)
                one_hots(t, 3)
                if m <= T:
                    store_features(0, m - 1, (m - 1) % 2)
                unpack(t)
            store_counts(T - 1)

            def sum_squares(e):
                act.wait_ge(s_w, w_after[e])
                if e == GAT_E:
                    act.wait_ge(s_wlo, sum(mats[:e]))
                elif e > 1:
                    act.wait_ge(s_hp, T * e)
                else:
                    act.wait_ge(s_invc, 1)
                for s in range(mats[e]):
                    ins = nc.scalar.activation(parts(e, s, 0), RW[:, s, :], ACT.Square,
                                               scale=2.0 ** -20, accum_out=norms[:, s:s + 1])
                if DYNAMIC[e]:
                    act.wait_ge(s_b, b_after[e])
                    ins = nc.scalar.activation(W16[0:P, 0, 1, 0, :], BB[0:P, :], ACT.Square, accum_out=norms[0:P, 2:3])
                ins.then_inc(s_norm, 1)

            def take_roots(e):
                act.wait_ge(s_sq2, e)
                c = 2 if DYNAMIC[e] else 1
                nc.scalar.activation(roots[:, 1, 0:c], roots[:, 0, 0:c], ACT.Sqrt).then_inc(s_roots, 1)

            def high_weights(e, s):
                if s == 0:
                    act.wait_ge(s_scale, e)
                nc.scalar.mul(parts(e, s, 0), RW[:, s, :],
                              scale_w[:, e:e + 1]).then_inc(s_whi, 1)

            def high_means(e, i):
                n = 3 * KT * averaging(e) + i
                f, (lo, hi) = i // 3, THIRDS[i % 3]
                act.wait_ge(s_mean, n + 1)
                nc.scalar.copy(NT[:, 0, f, lo:hi], NB[:, i % 2, 0:hi - lo]).then_inc(s_nhi, 1)

            def factors():
                act.wait_ge(s_dif, 1)
                nc.scalar.activation(fac[0:P, 1], fac[0:P, 0], ACT.Exp, scale=SLOPE)
                nc.scalar.activation(fac[0:P, 2], fac[0:P, 2], ACT.Exp)
                nc.scalar.activation(fac[0:P, 4], fac[0:P, 0], ACT.Exp).then_inc(s_fac, 1)
                act.wait_ge(s_fac, 1)
                nc.scalar.mul(fac[0:P, 3], fac[0:P, 4], -1.0).then_inc(s_fac, 1)
                act.wait_ge(s_fac, 2)

            def store_sums(h, o):
                act.wait_ge(s_pu, T * (h + 1))
                if h > 0:
                    act.wait_ge(s_nut, 2 * h)
                nc.scalar.copy(NU[0:DH + 1, :], agg[0:DH + 1, o, 0:N]).then_inc(s_nu, 1)

            def attention():
                def store_row(h, i):
                    a, b = 4 * P * i, min(4 * P * i + 4 * P, N)
                    act.wait_ge(s_rho, 3 * h + i + 1)
                    if h >= 2:
                        act.wait_ge(s_r, T * (h - 1))
                    nc.scalar.copy(rows[0:P, h % 2, a:b].rearrange("p (t n) -> p t n", n=P),
                                   rhop[i % 2][0:P, 0:(b - a) // P]).then_inc(s_re, 1)

                for i in range(3):
                    store_row(0, i)
                for h in range(HEADS):
                    act.wait_ge(s_re, 3 * h + 3)
                    for k in range(T):
                        j = T * h + k
                        if h > 0 and k == 7:
                            store_sums(h - 1, (h - 1) % 2)
                        if h + 1 < HEADS and k in (6, 9):
                            for i in ((0, 1) if k == 6 else (2,)):
                                store_row(h + 1, i)
                        if j >= 4:
                            act.wait_ge(s_p, j - 3)
                        nc.scalar.activation(slots[0:P, j % 4, :], rows[0:P, h % 2, :], ACT.Relu, bias=fac[0:P, 3, k, h:h + 1],
                                             scale=fac[0:P, 1, k, h:h + 1]).then_inc(s_r, 1)
                store_sums(HEADS - 1, 1)

            def wide_attention():
                def flat(h, k):
                    j = T * h + k
                    if j >= 4:
                        act.wait_ge(s_p, j - 3)
                    nc.scalar.activation(slots[0:P, j % 4, :], rows[0:P, 1, :], ACT.Identity,
                                         bias=tsl[0:P, k, h:h + 1]).then_inc(s_lin, 1)

                def exponential(j):
                    act.wait_ge(s_q, j + 1)
                    nc.scalar.activation(slots[0:P, j % 4, :], slots[0:P, j % 4, :], ACT.Exp).then_inc(s_e, 1)

                act.wait_ge(s_ab, 1)
                for h in range(HEADS):
                    for s in range(2):
                        act.wait_ge(s_row, 2 * h + s + 1)
                        if s == 0 and h > 0:
                            act.wait_ge(s_q, T * h)
                        nc.scalar.copy(rows[:, s, :].rearrange("p (t n) -> p t n", t=T), rowv[:, 0]).then_inc(s_ev, 1)
                    act.wait_ge(s_ev, 2 * h + 2)
                    for k in range(T):
                        flat(h, k)
                        if k > 0:
                            exponential(T * h + k - 1)
                    exponential(T * h + T - 1)
                    store_sums(h, 1)

            for e in STAGES[1:]:
                if e == GAT_E:
                    factors()
                    wide = act.value_load(wflag[0:1, 0:1], min_val=0, max_val=1)
                    with act.If(wide != 0):
                        wide_attention()
                    with act.Else():
                        attention()
                else:
                    for i in range(3 * KT):
                        high_means(e, i)
                        if i == 2:
                            sum_squares(e)
                        if i == 5:
                            take_roots(e)
                        if i in (6, 8):
                            high_weights(e, i // 2 - 3)
                if e == GAT_E:
                    act.wait_ge(s_var, 1)
                    nc.scalar.activation(moments[0:P, :, 2], moments[0:P, :, 1], ACT.Sqrt).then_inc(s_dev, 1)
                    for m in range(T):
                        high_part(e, m, m % 2)
                        if m > 0:
                            store_features(e, m - 1, (m - 1) % 2)
                    store_features(e, T - 1, 1)
                elif LAYERNORM[e]:
                    if L2NORM[e]:
                        norms_of_rows(e, 0, 0)
                    if e + 1 == GAT_E:
                        sum_squares(GAT_E)
                    for m in range(T):
                        deviation(e, m, m % 2)
                        if L2NORM[e] and m + 1 < T:
                            norms_of_rows(e, m + 1, (m + 1) % 2)
                        if m > 0:
                            store_features(e, m - 1, (m - 1) % 2)
                        high_part(e, m, m % 2)
                        if e + 1 == GAT_E and m == 3:
                            take_roots(GAT_E)
                        if e + 1 == GAT_E and m == 5:
                            high_weights(GAT_E, 0)
                    store_features(e, T - 1, 1)
                elif L2NORM[e]:
                    for m in range(2):
                        norms_of_rows(e, m, m)
                        high_part(e, m, m)
                    with act.Fori(1, T // 2) as i:
                        for u in range(2):
                            norms_of_rows(e, 2 * i + u, u)
                            store_features(e, 2 * i + u - 2, u)
                            high_part(e, 2 * i + u, u)
                    for m in range(T - 2, T):
                        store_features(e, m, m % 2)
                elif e < 8:
                    with act.Fori(0, T // 2) as i:
                        for u in range(2):
                            high_part(e, 2 * i + u, u)
                            store_features(e, 2 * i + u, u)

        @block.vector
        def _(dve):
            chain = Chain(dve, s_dve)
            link = chain.link

            dve.wait_ge(s_const, 1)
            dve.wait_ge(s_idx, 32)
            link(nc.vector.tensor_copy(eallf[0:P], eall[0:P]))
            link(nc.vector.tensor_tensor(less[0:P], eallf[0:P, 0:1, :].broadcast_to([P, T, EC]),
                                         bounds[0:P, :].unsqueeze(2).broadcast_to([P, T, EC]), ALU.is_lt))
            nc.vector.reduce_sum(cnt[0:P, :], less[0:P], AX).then_inc(s_cnt, 1)
            dve.wait_ge(s_startps, 1)
            nc.vector.tensor_scalar(starts[0:1, :], rst[0:1, 0, 0:T], float(E - CAP), None, ALU.min).then_inc(s_starts, 1)

            class Steps:

                def __init__(self, base):
                    self.n = base

                def link(self, ins):
                    self.n = self.n + 1
                    ins.then_inc(s_ln, 1)
                    dve.wait_ge(s_ln, self.n)

            def invert_root(st, v, root, q, least, scale):
                st.link(nc.vector.reciprocal(q, root))
                st.link(nc.vector.tensor_scalar(q, v, q, root, ALU.mult, ALU.add))
                st.link(nc.vector.tensor_scalar(root, q, 0.5 / scale, least / scale, ALU.mult, ALU.max))
                st.link(nc.vector.reciprocal(root, root))

            def read_tile(e, m, u):
                r = first(e, HAS_RST) + m + 1
                if e < 8:
                    dve.wait_ge(s_hp, T * e + m - 1)
                elif m >= 2:
                    dve.wait_ge(s_out, m - 1)
                dve.wait_ge(s_rst, r)
                nc.vector.scalar_tensor_tensor(out=Vb[0:P, u, :], in0=rst[0:P, u, :], scalar=unscale[0:P, e:e + 1],
                                               in1=BB[0:P, :], op0=ALU.mult, op1=ALU.add).then_inc(s_v, 1)

            def add_and_measure(st, e, m, u):
                if HAS_RST[e]:
                    dve.wait_ge(s_v, first(e, HAS_RST) + m + 1)
                if e == 3:
                    st.link(nc.vector.tensor_tensor(X[0:P, m, :], X[0:P, m, :], Vb[0:P, u, :], ALU.add))
                if L2NORM[e]:
                    dve.wait_ge(s_sq, first(e, L2NORM) + m + 1)
                    sq, root, q = (small[0:P, u, i:i + 1] for i in range(3))
                    st.link(nc.vector.tensor_scalar(root, root, NORM_EPS, None, ALU.max))
                    invert_root(st, sq, root, q, NORM_EPS, 1.0 if e == 6 else UNIT_SCALE)
                    if e == 6:
                        st.link(nc.vector.scalar_tensor_tensor(out=X[0:P, m, :], in0=Rb[0:P, u, :], scalar=root,
                                                               in1=X[0:P, m, :], op0=ALU.mult, op1=ALU.add))
                if LAYERNORM[e]:
                    st.link(nc.vector.bn_stats(stat[0:P, u, :], X[0:P, m, :]))
                    st.link(nc.vector.bn_aggr(small[0:P, u, 4:6], stat[0:P, u, :]))
                    var = small[0:P, u, 5:6]
                    st.link(nc.vector.tensor_scalar(var, var, LN_EPS, None, ALU.add))

            def normalise(st, e, m, u):
                mean, var, root, q = (small[0:P, u, i:i + 1] for i in range(4, 8))
                dve.wait_ge(s_root, first(e, LAYERNORM) + m + 1)
                invert_root(st, var, root, q, NORM_EPS, LN_SCALE)
                if T * e + m >= 2:
                    dve.wait_ge(s_hp, T * e + m - 1)
                nc.vector.tensor_scalar(Vb[0:P, u, :], X[0:P, m, :], mean, root,
                                        ALU.subtract, ALU.mult).then_inc(s_pre, 1)

            def low_part(e, m, u):
                n = T * e + m
                dve.wait_ge(s_hi, n + 1)
                if e in (4, 5):
                    f, scalar, op = Rb, small[0:P, u, 1:2], ALU.mult
                else:
                    f, scalar, op = Vb, 0.0, ALU.max
                    if LAYERNORM[e]:
                        dve.wait_ge(s_pre, first(e, LAYERNORM) + m + 1)
                nc.vector.scalar_tensor_tensor(out=HP[0:P, m, 1, :], in0=f[0:P, u, :], scalar=scalar, in1=HP[0:P, m, 0, :],
                                               op0=op, op1=ALU.subtract).then_inc(s_hp, 1)

            dve.wait_ge(s_x, 16)
            st = Steps(0)
            for m in range(EARLY):
                add_and_measure(st, 0, m, m % 2)
                if m > 0:
                    low_part(0, m - 1, (m - 1) % 2)
                normalise(st, 0, m, m % 2)
            low_part(0, EARLY - 1, (EARLY - 1) % 2)

            dve.wait_ge(s_ew, 16 * T)
            dve.wait_ge(s_ews, 16 * T)
            s_in = ew[:, 1].rearrange("p t c -> p (t c)")
            es_r, es_v = (es[:, i].rearrange("p t c -> p (t c)") for i in range(2))
            link(nc.vector.tensor_tensor(esd[:, :, :], ew[:, 0], bounds[:, :].unsqueeze(2).broadcast_to([128, T, CH]),
                                         ALU.subtract))
            link(nc.vector.tensor_scalar(tmpe[:, 0, :], s_in, float(R3), float(R3), ALU.is_ge, ALU.mult))
            link(nc.vector.tensor_scalar(tmpe[:, 1, :], s_in, float(2 * R3), float(R3), ALU.is_ge, ALU.mult))
            link(nc.vector.tensor_tensor(tmpe[:, 0, :], tmpe[:, 0, :], tmpe[:, 1, :], ALU.add))
            link(nc.vector.tensor_tensor(es_r, s_in, tmpe[:, 0, :], ALU.subtract))
            link(nc.vector.tensor_scalar(tmpe[:, 0, :], s_in, float(R3), 255.0, ALU.is_ge, ALU.mult))
            link(nc.vector.tensor_scalar(tmpe[:, 1, :], s_in, float(2 * R3), 65280.0, ALU.is_ge, ALU.mult))
            link(nc.vector.scalar_tensor_tensor(out=es_v, in0=tmpe[:, 0, :], scalar=1.0, in1=tmpe[:, 1, :],
                                                op0=ALU.add, op1=ALU.add))
            nc.vector.tensor_scalar(WV[:, 2 * T * CH:4 * T * CH], WV[:, 0:2 * T * CH], -1.0, None, ALU.mult).then_inc(s_esc, 1)

            def one_hots(t, g):
                if 4 * t + g >= 2:
                    dve.wait_ge(s_ohu, 4 * t + g - 1)
                c0, n = chunks[g], GROUPS[g]
                nc.vector.tensor_tensor(ringd[:, g % 2, :, 0:n], iotac[:, :, 0:n],
                                        esd[:, t:t + 1, c0:c0 + n].broadcast_to([128, P, n]), ALU.is_equal)
                for c in range(n - SHARED[g]):
                    ins = nc.vector.tensor_scalar(rings[:, g % 2, c, 0:R3], iota[:, 0:R3], es[:, 0, t, c0 + c:c0 + c + 1],
                                                  es[:, 1, t, c0 + c:c0 + c + 1], ALU.is_equal, ALU.mult)
                ins.then_inc(s_ohr, 1)

            for t in range(T):
                m = t + EARLY
                one_hots(t, 0)
                if m < T:
                    add_and_measure(st, 0, m, m % 2)
                one_hots(t, 1)
                if m < T:
                    normalise(st, 0, m, m % 2)
                one_hots(t, 2)
                if m < T:
                    low_part(0, m, m % 2)
                one_hots(t, 3)

            dve.wait_ge(s_dm, T)
            nc.vector.reduce_sum(degov[0:P, 0, :], deg3[0:P].rearrange("p q t -> p t q"), AX).then_inc(s_deg, 1)
            dve.wait_ge(s_degs, 1)
            nc.vector.reduce_sum(flagf[:, 0:1], rst[:, 0, 0:T], AX)
            link(nc.vector.reduce_sum(flagf[:, 1:2], rst[:, 0, T:2 * T], AX))
            link(nc.vector.tensor_scalar(flagf[:, 2:3], flagf[:, 0:1], float(E), None, ALU.not_equal))
            link(nc.vector.tensor_tensor(flagf[:, 3:4], flagf[:, 2:3], flagf[:, 1:2], ALU.add))
            link(nc.vector.tensor_scalar(flag[0:1, :], flagf[0:1, 3:4], 1.0, None, ALU.min))
            nc.vector.tensor_copy(flagf[:, 0:1], flagf[:, 3:4]).then_inc(s_flag, 1)
            general = dve.value_load(flag[0:1, 0:1], min_val=0, max_val=1)

            with dve.If(general != 0):
                dve.wait_ge(s_at, T)
                with dve.Fori(0, T) as t:
                    with dve.Fori(0, EC) as c:
                        nc.vector.tensor_scalar(goh[0:P, 0:P], iota[0:P, 0:P], eallf[0:P, 0, bass.ds(c, 1)], None, ALU.is_equal)
                        nc.vector.tensor_scalar(goh[0:P, 126:126 + N], iota[0:P, :], eallf[0:P, 1, bass.ds(c, 1)], None,
                                                ALU.is_equal).then_inc(g_ready, 1)
                        dve.wait_ge(g_used, EC * t + c + 1)
                    dve.wait_ge(g_tile, t + 1)
                    nc.vector.tensor_copy(gint[0:P, :], agg[0:P, 0, 0:N])
                    nc.vector.reduce_sum(degov[0:P, 0, bass.ds(t, 1)], agg[0:P, 0, 0:N], AX)
                    nc.vector.tensor_scalar(eallf[0:P, 0, :], eallf[0:P, 0, :], -float(P), None, ALU.add).then_inc(g_dve, 1)
                    dve.wait_ge(g_dve, t + 1)
                    b = gint[0:P, :].bitcast(U8).rearrange("p (n b) -> p n b", b=4)
                    nc.vector.tensor_copy(gdm[0:P, 0, 0:N], b[:, :, 0])
                    nc.vector.tensor_scalar(gdm[0:P, 1, 0:N], b[:, :, 1], 256.0, None, ALU.mult).then_inc(g_dm, 1)
                    for w in range(2):
                        dve.wait_ge(g_tp, 2 * t + w + 1)
                        to = AT if w == 0 else AH
                        for j in range(2):
                            ins = nc.vector.tensor_copy(to[0:P, 5 * j:5 * j + 5, bass.ds(P * t, P)], aps[0:P, j])
                        ins.then_inc(g_ev, 1)

            link(nc.vector.tensor_scalar(invc[0:P, :], degov[0:P, 0, :], 1.0, None, ALU.max))
            nc.vector.reciprocal(invc[0:P, :], invc[0:P, :]).then_inc(s_invc, 1)
            dve.wait_ge(s_invr, 1)
            nc.vector.tensor_copy(INV[:, :].rearrange("p (t n) -> p t n", t=T), rowv[:, 1]).then_inc(s_inv, 1)
            dve.wait_ge(s_inv, 1)

            def mean(e, i):
                n = 3 * KT * averaging(e) + i
                f, (lo, hi) = i // 3, THIRDS[i % 3]
                w = hi - lo
                dve.wait_ge(s_agg, n + 1)
                if n >= 2:
                    dve.wait_ge(s_nt, n - 1)
                nc.vector.tensor_tensor(NB[:, i % 2, 0:w], agg[:, 0, 512 * (i % 3):512 * (i % 3) + w], INV[:, lo:hi],
                                        ALU.mult).then_inc(s_mean, 1)

            def low_mean(e, i):
                n = 3 * KT * averaging(e) + i
                f, (lo, hi) = i // 3, THIRDS[i % 3]
                dve.wait_ge(s_nhi, n + 1)
                dve.wait_ge(s_mean, n + 1)
                nc.vector.tensor_tensor(NT[:, 1, f, lo:hi], NB[:, i % 2, 0:hi - lo], NT[:, 0, f, lo:hi],
                                        ALU.subtract).then_inc(s_nt, 1)

            def square_norms(e):
                dve.wait_ge(s_normps, e)
                f = roots[:, 0, 0:1]
                if mats[e] == 2:
                    link(nc.vector.tensor_copy(flagf[:, 0:2], squares(e)))
                    ins = nc.vector.tensor_scalar(f, flagf[:, 0:1], flagf[:, 1:2], 1e-24, ALU.add, ALU.max)
                else:
                    ins = nc.vector.tensor_scalar(f, squares(e)[:, 0:1], 1e-24, None, ALU.max)
                if DYNAMIC[e]:
                    link(ins)
                    link(nc.vector.tensor_scalar(flagf[0:P, 2:3], norms[0:P, 2:3], 2.0, None, ALU.mult))
                    link(nc.vector.tensor_scalar(flagf[0:P, 3:4], f[0:P], bound4[0:P, e - 1:e], 2.0 ** 40, ALU.mult, ALU.mult))
                    link(nc.vector.tensor_tensor(roots[0:P, 0, 1:2], flagf[0:P, 3:4], flagf[0:P, 2:3], ALU.add))
                    ins = nc.vector.tensor_scalar(bound4[0:P, e:e + 1], roots[0:P, 0, 1:2], 4.0, None, ALU.mult)
                ins.then_inc(s_sq2, 1)

            def set_scales(e):
                dve.wait_ge(s_roots, e)
                bits = roots[:, 1, :].bitcast(I32)
                c = 2 if DYNAMIC[e] else 1
                link(nc.vector.tensor_scalar(bits[:, 0:c], bits[:, 0:c], EXPONENT, EXPONENT, ALU.bitwise_and, ALU.bitwise_xor))
                link(nc.vector.tensor_scalar(scale_w[:, e:e + 1], roots[:, 1, 0:1], 2.0 ** (13 - 20), None, ALU.mult))
                if DYNAMIC[e]:
                    link(nc.vector.tensor_scalar(scale_o[0:P, e:e + 1], roots[0:P, 1, 1:2], 2.0 ** 13, None, ALU.mult))
                    link(nc.vector.tensor_scalar(BB[0:P, :], BB[0:P, :], scale_o[0:P, e:e + 1], None, ALU.mult))
                before = scale_o[0:P, e - 1:e] if DYNAMIC[e - 1] else OUT_SCALE[e - 1]
                u = unscale[0:P, e:e + 1]
                link(nc.vector.tensor_scalar(u, scale_w[0:P, e:e + 1], before, None, ALU.mult))
                ui = u.bitcast(I32)
                link(nc.vector.tensor_scalar(ui, ui, EXPONENT, EXPONENT, ALU.bitwise_and, ALU.bitwise_xor))
                after = scale_o[0:P, e:e + 1] if DYNAMIC[e] else 1.0
                link(nc.vector.tensor_scalar(u, u, 0.5, after, ALU.mult, ALU.mult))
                nc.vector.tensor_copy(flagf[:, 0:1], scale_w[:, e:e + 1]).then_inc(s_scale, 1)

            def low_weights(e, s):
                dve.wait_ge(s_whi, sum(mats[:e]) + s + 1)
                nc.vector.scalar_tensor_tensor(out=parts(e, s, 1), in0=RW[:, s, :], scalar=scale_w[:, e:e + 1], in1=parts(e, s, 0),
                                               op0=ALU.mult, op1=ALU.subtract).then_inc(s_wlo, 1)

            def scores():
                dve.wait_ge(s_b, b_after[GAT_E])
                def project_tile(m):
                    dve.wait_ge(s_wx, m + 1)
                    nc.vector.scalar_tensor_tensor(out=WX[0:P, m, :, 0:DH], in0=rst[0:P, m % 2, :].rearrange("p (h n) -> p h n", h=HEADS),
                                                   scalar=unscale[0:P, GAT_E:GAT_E + 1],
                                                   in1=BB[0:P, :].rearrange("p (h n) -> p h n", h=HEADS),
                                                   op0=ALU.mult, op1=ALU.add).then_inc(s_wxv, 1)

                dve.wait_ge(s_tr, T * GAT_E)
                project_tile(0)
                for m in range(T):
                    both = WV[0:P, 4096 + 2 * D * (m % 2):4096 + 2 * D * (m % 2 + 1)].rearrange("p (s h n) -> p s h n", s=2, h=HEADS)
                    dve.wait_ge(s_wxv, m + 1)
                    for s in range(2):
                        ins = nc.vector.tensor_tensor(both[:, s], WX[0:P, m, :, 0:DH],
                                                      attn_s[0:P, s, :].rearrange("p (h n) -> p h n", h=HEADS), ALU.mult)
                    chain.n += 1
                    ins.then_inc(s_dve, 1)
                    if m + 1 < T:
                        project_tile(m + 1)
                    dve.wait_ge(s_dve, chain.n)
                    link(nc.vector.reduce_sum(tds[0:P, :, m, :], both, AX))
                td, ts = tds[0:P, 0], tds[0:P, 1]
                link(nc.vector.tensor_tensor(td, td, abias[0:P, :].unsqueeze(1).broadcast_to([P, T, HEADS]), ALU.add))
                nc.vector.tensor_scalar(tsl[0:P], ts, SLOPE, None, ALU.mult).then_inc(s_sc, 1)
                link(nc.vector.tensor_scalar(fac[0:P, 0], ts, -1.0, None, ALU.mult))
                nc.vector.tensor_reduce(ext[0:P, 0, :], ts.rearrange("p t h -> p h t"), AX, ALU.max)
                nc.vector.tensor_reduce(ext[0:P, 1, :], fac[0:P, 0].rearrange("p t h -> p h t"), AX, ALU.max).then_inc(s_ext, 1)
                dve.wait_ge(s_all, 1)
                most = extall[0:P, 0:1, :].broadcast_to([P, T, HEADS])
                link(nc.vector.tensor_tensor(flag8[:, :], extall[:, 0, :], extall[:, 1, :], ALU.add))
                link(nc.vector.tensor_reduce(flagf[:, 0:1], flag8[:, :], AX, ALU.max))
                link(nc.vector.tensor_scalar(wflag[0:1, :], flagf[0:1, 0:1], WIDE, None, ALU.is_ge))
                link(nc.vector.tensor_tensor(fac[0:P, 2], td, most, ALU.add))
                link(nc.vector.tensor_scalar(fac[0:P, 2], fac[0:P, 2], SLOPE - 1.0, RATIO_MAX, ALU.mult, ALU.min))
                nc.vector.tensor_tensor(fac[0:P, 0], ts, most, ALU.subtract).then_inc(s_dif, 1)
                dve.wait_ge(s_dif, 1)

            def maxima(high, wl):
                td = tds[0:P, 0]
                mask = slots[0:P, 2, 0:625].bitcast(BF16).rearrange("p (t n) -> p t n", t=T)
                mask2 = slots[0:P, 3, 0:625].bitcast(BF16).rearrange("p (t n) -> p t n", t=T)
                turns = 2 if high else 1
                for h in range(HEADS):
                    dve.wait_ge(s_tsr, h + 1)
                    for t in range(T):
                        for w in range(turns):
                            dve.wait_ge(s_ct, turns * (T * h + t) + w + 1)
                            for j in range(2):
                                ins = nc.vector.tensor_scalar((mask2 if w else mask)[:, 5 * j:5 * j + 5], aps[0:P, j], 0.0, NEVER,
                                                              ALU.is_equal, ALU.mult)
                            ins.then_inc(s_mk, 1)
                            dve.wait_ge(s_mk, turns * (T * h + t) + w + 1)
                        if high:
                            wl(nc.vector.tensor_tensor(mask, mask, mask2, ALU.max))
                        nc.vector.tensor_tensor_reduce(slots[0:P, 0, :].rearrange("p (t n) -> p t n", t=T), mask, rowv[0:P, h % 2],
                                                       1.0, NEVER, ALU.add, ALU.max, smax[0:P, t, h:h + 1]).then_inc(s_mx, 1)
                        dve.wait_ge(s_mx, T * h + t + 1)
                z, lz = ab[0:P, 0], ab[0:P, 2]
                wl(nc.vector.tensor_scalar(z, smax[0:P], NEVER / 2, None, ALU.is_ge))
                wl(nc.vector.tensor_tensor(smax[0:P], smax[0:P], z, ALU.mult))
                wl(nc.vector.tensor_tensor(z, td, smax[0:P], ALU.add))
                wl(nc.vector.scalar_tensor_tensor(out=lz, in0=z, scalar=SLOPE, in1=z, op0=ALU.mult, op1=ALU.max))
                wl(nc.vector.tensor_tensor(ab[0:P, 0], td, lz, ALU.subtract))
                nc.vector.scalar_tensor_tensor(out=ab[0:P, 1], in0=td, scalar=SLOPE, in1=lz, op0=ALU.mult,
                                               op1=ALU.subtract).then_inc(s_ab, 1)

            def add_sums(h, i, fl):
                a, b = HALVES[i]
                dve.wait_ge(s_nut, 2 * h + i + 1)
                fl(nc.vector.tensor_scalar(den[0:P, a:b], nups[i][0:P, 0:b - a, DH], 1e-30, None, ALU.max))
                fl(nc.vector.reciprocal(den[0:P, a:b], den[0:P, a:b]))
                fl(nc.vector.tensor_tensor(share[0:P, 0:b - a, :], nups[i][0:P, 0:b - a, 0:DH],
                                           den[0:P, a:b].unsqueeze(2).broadcast_to([P, b - a, DH]), ALU.mult))
                to = X[0:P, a:b, DH * h:DH * h + DH]
                nc.vector.tensor_tensor(to, to, share[0:P, 0:b - a, :], ALU.add).then_inc(s_xh, 1)
                dve.wait_ge(s_xh, 2 * h + i + 1)

            def weigh(j, s, to, counts_scalar, op, high, gl):
                k = j % T
                ins = nc.vector.scalar_tensor_tensor(out=to, in0=s, scalar=counts_scalar, in1=AT[0:P, k, :], op0=op, op1=ALU.mult)
                if high:
                    gl(ins)
                    gl(nc.vector.scalar_tensor_tensor(out=s, in0=s, scalar=counts_scalar, in1=AH[0:P, k, :], op0=op, op1=ALU.mult))
                    ins = nc.vector.tensor_tensor(to, to, s, ALU.add)
                ins.then_inc(s_p, 1)

            def edge_weights_factored(high):
                gl = Chain(dve, g_dve, T).link
                fl = Chain(dve, s_fin).link
                for j in range(HEADS * T):
                    h, k = divmod(j, T)
                    dve.wait_ge(s_r, j + 1)
                    if j >= 2:
                        dve.wait_ge(s_pu, j - 1)
                    weigh(j, slots[0:P, j % 4, :], slots[0:P, 4 + j % 2, :], fac[0:P, 4, k, h:h + 1], ALU.add, high, gl)
                    if h > 0 and k in (7, 9):
                        add_sums(h - 1, (k - 7) // 2, fl)
                for i in range(2):
                    add_sums(HEADS - 1, i, fl)

            def edge_weights_wide(high, wl):
                gl = Chain(dve, g_dve, T).link

                def exponent(j):
                    h, k = divmod(j, T)
                    dve.wait_ge(s_lin, j + 1)
                    s = slots[0:P, j % 4, :]
                    nc.vector.scalar_tensor_tensor(out=s, in0=rows[0:P, 0, :], scalar=tds[0:P, 1, k, h:h + 1], in1=s,
                                                   op0=ALU.add, op1=ALU.max).then_inc(s_q, 1)

                def edge_weights(j):
                    dve.wait_ge(s_e, j + 1)
                    if j >= 2:
                        dve.wait_ge(s_pu, j - 1)
                    weigh(j, slots[0:P, j % 4, :], slots[0:P, 4 + j % 2, :], 1.0, ALU.min, high, gl)

                for h in range(HEADS):
                    dve.wait_ge(s_ev, 2 * h + 2)
                    for j in range(T * h, T * h + T):
                        exponent(j)
                        if j > T * h:
                            edge_weights(j - 1)
                    edge_weights(T * h + T - 1)
                    for i in range(2):
                        add_sums(h, i, wl)

            for e in STAGES[1:]:
                if e == GAT_E:
                    scores()
                    wide = dve.value_load(wflag[0:1, 0:1], min_val=0, max_val=1)
                    with dve.If(wide != 0):
                        with dve.If(general != 0):
                            wl = Chain(dve, s_wide).link
                            maxima(True, wl)
                            edge_weights_wide(True, wl)
                        with dve.Else():
                            wl = Chain(dve, s_wide).link
                            maxima(False, wl)
                            edge_weights_wide(False, wl)
                    with dve.Else():
                        dve.wait_ge(s_fac, 2)
                        with dve.If(general != 0):
                            edge_weights_factored(True)
                        with dve.Else():
                            edge_weights_factored(False)
                else:
                    for i in range(3 * KT):
                        mean(e, i)
                        low_mean(e, i)
                        if i == 5:
                            square_norms(e)
                            set_scales(e)
                        if i in (7, 9):
                            low_weights(e, (i - 7) // 2)
                if e != GAT_E:
                    dve.wait_ge(s_b, b_after[e])
                if e == 8:
                    for m in range(T):
                        read_tile(e, m, m % 2)
                        dve.wait_ge(s_v, first(e, HAS_RST) + m + 1)
                        nc.vector.scalar_tensor_tensor(out=X[0:P, m, :], in0=Vb[0:P, m % 2, :], scalar=0.0, in1=X[0:P, m, :],
                                                       op0=ALU.max, op1=ALU.add).then_inc(s_out, 1)
                elif e == GAT_E:
                    for m in range(T):
                        ins = nc.vector.bn_stats(stats[0:P, m, :], X[0:P, m, :])
                    link(ins)
                    for m in range(T):
                        ins = nc.vector.bn_aggr(moments[0:P, m, 0:2], stats[0:P, m, :])
                    link(ins)
                    var, root, q = (moments[0:P, :, i] for i in range(1, 4))
                    nc.vector.tensor_scalar(var, var, LN_EPS, None, ALU.add).then_inc(s_var, 1)
                    dve.wait_ge(s_dev, 1)
                    link(nc.vector.reciprocal(q, root))
                    link(nc.vector.tensor_tensor(q, q, var, ALU.mult))
                    link(nc.vector.tensor_tensor(root, q, root, ALU.add))
                    link(nc.vector.tensor_scalar(root, root, 0.5 / LN_SCALE, None, ALU.mult))
                    link(nc.vector.reciprocal(root, root))
                    for m in range(T):
                        if m > 1:
                            dve.wait_ge(s_hp, T * e + m - 1)
                        nc.vector.tensor_scalar(Vb[0:P, m % 2, :], X[0:P, m, :], moments[0:P, m, 0:1], moments[0:P, m, 2:3],
                                                ALU.subtract, ALU.mult).then_inc(s_pre, 1)
                        if m > 0:
                            low_part(e, m - 1, (m - 1) % 2)
                    low_part(e, T - 1, 1)
                elif LAYERNORM[e]:
                    st = Steps(LN_BASE[e])
                    read_tile(e, 0, 0)
                    for m in range(T):
                        add_and_measure(st, e, m, m % 2)
                        if m > 0:
                            low_part(e, m - 1, (m - 1) % 2)
                        if m + 1 < T:
                            read_tile(e, m + 1, (m + 1) % 2)
                        normalise(st, e, m, m % 2)
                        if e + 1 == GAT_E and m == 2:
                            square_norms(GAT_E)
                        if e + 1 == GAT_E and m == 4:
                            set_scales(GAT_E)
                        if e + 1 == GAT_E and m == 6:
                            low_weights(GAT_E, 0)
                    low_part(e, T - 1, 1)
                else:
                    with dve.Fori(0, T // 2) as i:
                        for u in range(2):
                            st = Steps(LN_BASE[e] + steps(e) * (2 * i + u))
                            read_tile(e, 2 * i + u, u)
                            add_and_measure(st, e, 2 * i + u, u)
                            low_part(e, 2 * i + u, u)

        @block.tensor
        def _(pe):
            pe.wait_ge(s_const, 1)
            pe.wait_ge(s_cnt, 1)
            nc.tensor.matmul(rst[0:1, 0, 0:T], ones[0:P, 0:1], cnt[0:P, :], start=True, stop=True).then_inc(s_startps, 1)

            def count(t, g):
                if g == 0 and t >= 2:
                    pe.wait_ge(s_cint, t - 1)
                pe.wait_ge(s_ohr, 4 * t + g + 1)
                if SHARED[g]:
                    pe.wait_ge(s_oha, 2 * t + g - 1)
                for c in range(GROUPS[g]):
                    ins = nc.tensor.matmul(agg[0:P, t % 2, 0:R3], ringd[:, g % 2, :, c], rings[:, g % 2, c, 0:R3],
                                           start=(g == 0 and c == 0), stop=(g == 3 and c == GROUPS[g] - 1))
                ins.then_inc(s_ohu, 1)

            def transpose_counts(t):
                pe.wait_ge(s_dm, t + 1)
                pe.wait_ge(s_starts, 1)
                if t > 0:
                    pe.wait_ge(s_at, t)
                for k in range(T):
                    ins = nc.tensor.transpose(aps[0:P, k // 5, k % 5], DM[0:P, P * k:P * k + P], ident16[0:P, 0:P])
                ins.then_inc(s_tp, 1)

            def transpose_features(e, m, u):
                n = T * e + m
                pe.wait_ge(s_hp, n + 1)
                if n >= 2:
                    pe.wait_ge(s_ht, n - 1)
                for w in range(2):
                    for f in range(KT):
                        ins = nc.tensor.transpose(hps[u][:, w, f], HP[0:P, m, w, 128 * f:128 * f + 128], identh[0:P, 0:P])
                ins.then_inc(s_tr, 1)

            pe.wait_ge(s_const, 2)
            for m in range(EARLY):
                transpose_features(0, m, m % 2)
            for t in range(T):
                count(t, 0)
                if t > 0:
                    transpose_counts(t - 1)
                count(t, 1)
                count(t, 2)
                if t + EARLY < T:
                    transpose_features(0, t + EARLY, (t + EARLY) % 2)
                count(t, 3)
            transpose_counts(T - 1)

            pe.wait_ge(s_deg, 1)
            pe.wait_ge(s_at, T)
            nc.tensor.matmul(rst[:, 0, 0:2 * T], ones[0:P, :], degov[0:P, :, :].rearrange("p s t -> p (s t)"),
                             start=True, stop=True).then_inc(s_degs, 1)
            pe.wait_ge(s_flag, 1)
            general = pe.value_load(flag[0:1, 0:1], min_val=0, max_val=1)

            with pe.If(general != 0):
                with pe.Fori(0, T) as t:
                    for a, b in COLS:
                        nc.tensor.matmul(agg[0:P, 0, a:b], zeros16[0:P, 0:P], iota[0:P, a:b], start=True, stop=False)
                    with pe.Fori(0, EC) as c:
                        pe.wait_ge(g_ready, EC * t + c + 1)
                        for a, b in COLS:
                            ins = nc.tensor.matmul(agg[0:P, 0, a:b], goh[0:P, 0:P], goh[0:P, 126 + a:126 + b],
                                                   start=False, stop=False)
                        ins.then_inc(g_used, 1)
                    for a, b in COLS:
                        ins = nc.tensor.matmul(agg[0:P, 0, a:b], zeros16[0:P, 0:P], iota[0:P, a:b], start=False, stop=True)
                    ins.then_inc(g_tile, 1)
                    pe.wait_ge(g_dm, t + 1)
                    for w in range(2):
                        for k in range(T):
                            ins = nc.tensor.transpose(aps[0:P, k // 5, k % 5], gdm[0:P, w, P * k:P * k + P], ident16[0:P, 0:P])
                        ins.then_inc(g_tp, 1)
                        pe.wait_ge(g_ev, 2 * t + w + 1)
            pe.wait_ge(s_invc, 1)
            for t in range(T):
                ins = nc.tensor.transpose(rowv[:, 1, t], invc[0:P, t:t + 1].broadcast_to([P, 128]), ident[0:P, 0:P])
            ins.then_inc(s_invr, 1)

            def norm_products(e):
                pe.wait_ge(s_norm, e)
                nc.tensor.matmul(squares(e)[:, 0:mats[e]], ones[:, :], norms[:, 0:mats[e]], start=True, stop=True).then_inc(s_normps, 1)

            def sum_neighbours(e):
                a = averaging(e)

                def products(f, k, i, counts, start, stop):
                    lo, hi = THIRDS[i]
                    for w in range(2):
                        ins = nc.tensor.matmul(agg[:, 0, 512 * i:512 * i + hi - lo], HP[0:P, k, w, bass.ds(128 * f, 128)],
                                               counts[0:P, k, lo:hi], start=(start and w == 0), stop=(stop and w == 1))
                    return ins

                def last_tile(f, i):
                    with pe.If(general != 0):
                        for k in range(T):
                            products(f, k, i, AH, False, False)
                    products(f, T - 1, i, AT, False, True).then_inc(s_agg, 1)

                for k in range(T):
                    pe.wait_ge(s_hp, T * (e - 1) + k + 1)
                    if k < T - 1:
                        for i in range(3):
                            products(0, k, i, AT, k == 0, False)
                    else:
                        for i in range(3):
                            last_tile(0, i)
                    if k >= T - late(e - 1):
                        transpose_features(e - 1, k, k % 2)

                def block_of_features(f):
                    for i in range(3):
                        pe.wait_ge(s_mean, 3 * (KT * a + f - 1) + i + 1)
                        for k in range(T - 1):
                            products(f, k, i, AT, k == 0, False)
                        last_tile(f, i)

                block_of_features(1)
                norm_products(e)
                with pe.Fori(2, KT) as f:
                    block_of_features(f)

            def layer_products(out_ap, m, sides, weights16, means=None):
                pairs = [(s, w, v, k) for s in range(len(sides)) for w, v in ((0, 0), (1, 0), (0, 1)) for k in range(KT)]
                for i, (s, w, v, k) in enumerate(pairs):
                    if means is not None and i == 3 * KT:
                        pe.wait_ge(s_nt, means)
                    ins = nc.tensor.matmul(out_ap, sides[s][:, w, k, bass.ds(P * m, P)], weights16[s][:, v, k, :],
                                           start=(i == 0), stop=(i == len(pairs) - 1))
                return ins

            def layer_tile(e, m, u):
                n = first(e, HAS_RST) + m
                if not isinstance(n, int) or n >= 2:
                    pe.wait_ge(s_v, n - 1)
                layer_products(rst[0:P, u, :], m, (HT, NT), (W16[:, 0], W16[:, 1]),
                               3 * KT * (averaging(e) + 1) if m == 0 else None).then_inc(s_rst, 1)

            def project():
                transpose_features(6, T - 2, 0)
                pe.wait_ge(s_wlo, sum(mats[:GAT_E + 1]))
                for m in range(T):
                    if m == 2:
                        transpose_features(6, T - 1, 1)
                    pe.wait_ge(s_ht, T * 6 + m + 1)
                    if m >= 2:
                        pe.wait_ge(s_wxv, m - 1)
                    else:
                        pe.wait_ge(s_v, first(GAT_E, HAS_RST) + m - 1)
                    layer_products(rst[0:P, m % 2, :], m, (HT,), (WG,)).then_inc(s_wx, 1)

            def source_rows(high):
                turns = 2 if high else 1
                pe.wait_ge(s_sc, 1)
                for h in range(HEADS):
                    if h >= 2:
                        pe.wait_ge(s_mx, T * (h - 1))
                    for t in range(T):
                        ins = nc.tensor.transpose(rowv[:, h % 2, t], tds[0:P, 1, t, h:h + 1].broadcast_to([P, 128]), ident[0:P, 0:P])
                    ins.then_inc(s_tsr, 1)
                    for t in range(T):
                        for w in range(turns):
                            n = turns * (T * h + t) + w
                            if n > 0:
                                pe.wait_ge(s_mk, n)
                            for k in range(T):
                                ins = nc.tensor.transpose(aps[0:P, k // 5, k % 5], (AH if w else AT)[0:P, k, P * t:P * t + P],
                                                          ident16[0:P, 0:P])
                            ins.then_inc(s_ct, 1)

            def sum_head(h, k, o):
                j = T * h + k
                pe.wait_ge(s_p, j + 1)
                for a, b in COLS:
                    ins = nc.tensor.matmul(agg[0:DH + 1, o, a:b], WX[0:P, k, h, :], slots[0:P, 4 + j % 2, a:b],
                                           start=(k == 0), stop=(k == T - 1))
                ins.then_inc(s_pu, 1)

            def turn_sums(h, i):
                a, b = HALVES[i]
                pe.wait_ge(s_nu, h + 1)
                if h > 0:
                    pe.wait_ge(s_xh, 2 * h - 1 + i)
                for t in range(a, b):
                    ins = nc.tensor.transpose(nups[i][0:P, t - a, :], NU[0:DH + 1, P * t:P * t + P], ident[0:DH + 1, 0:DH + 1])
                ins.then_inc(s_nut, 1)

            def attend():
                def ratio_row(h, i):
                    if i == 2:
                        pe.wait_ge(s_re, 3 * h + 1)
                    elif h >= 3:
                        pe.wait_ge(s_xh, 2 * (h - 2) - i)
                    elif h >= 1:
                        pe.wait_ge(s_re, 3 * h - i)
                    for t in range(4 * i, min(4 * i + 4, T)):
                        ins = nc.tensor.transpose(rhop[i % 2][:, t - 4 * i], fac[0:P, 2, t, h:h + 1].broadcast_to([P, 128]), ident[0:P, 0:P])
                    ins.then_inc(s_rho, 1)

                pe.wait_ge(s_fac, 2)
                for i in range(3):
                    ratio_row(0, i)
                for h in range(HEADS):
                    if h > 1:
                        pe.wait_ge(s_nu, h - 1)
                    for k in range(T):
                        sum_head(h, k, h % 2)
                        if h + 1 < HEADS and k in (0, 3):
                            for i in ((0, 1) if k == 0 else (2,)):
                                ratio_row(h + 1, i)
                        if h > 0 and k == 4:
                            pe.wait_ge(s_re, min(3 * (h + 1) + 2, 3 * HEADS))
                            turn_sums(h - 1, 0)
                        if h > 0 and k == 6:
                            pe.wait_ge(s_re, min(3 * (h + 1) + 3, 3 * HEADS))
                            turn_sums(h - 1, 1)
                for i in range(2):
                    turn_sums(HEADS - 1, i)

            def attend_wide():
                def score_rows(h, s):
                    if 2 * h + s > 0:
                        pe.wait_ge(s_ev, 2 * h + s)
                    for t in range(T):
                        ins = nc.tensor.transpose(rowv[:, 0, t], ab[0:P, s, t, h:h + 1].broadcast_to([P, 128]), ident[0:P, 0:P])
                    ins.then_inc(s_row, 1)

                pe.wait_ge(s_ab, 1)
                for h in range(HEADS):
                    for s in range(2):
                        score_rows(h, s)
                    if h > 0:
                        pe.wait_ge(s_nu, h)
                    for k in range(T):
                        sum_head(h, k, 1)
                    for i in range(2):
                        turn_sums(h, i)

            for e in STAGES[1:]:
                if e == GAT_E:
                    project()
                    pe.wait_ge(s_one, 1)
                    pe.wait_ge(s_dif, 1)
                    wide = pe.value_load(wflag[0:1, 0:1], min_val=0, max_val=1)
                    with pe.If(wide != 0):
                        with pe.If(general != 0):
                            source_rows(True)
                        with pe.Else():
                            source_rows(False)
                        attend_wide()
                    with pe.Else():
                        attend()
                    continue
                sum_neighbours(e)
                pe.wait_ge(s_wlo, sum(mats[:e + 1]))
                pe.wait_ge(s_ht, T * e)
                for m in range(T):
                    layer_tile(e, m, m % 2)
                    if e + 1 == GAT_E and m == 1:
                        norm_products(GAT_E)
                    if m >= late(e) and e < 8:
                        transpose_features(e, m - late(e), (m - late(e)) % 2)


def kernel(x, src, dst, L0_gnn_Ws_self, L0_gnn_Ws_neigh, L0_gnn_bs, L1_gnn_W_self, L1_gnn_W_neigh, L1_gnn_b,
           L2_gnn_Ws, L2_gnn_Wb, L2_gnn_a_w, L2_gnn_a_b, L3_gnn_W_self, L3_gnn_W_neigh, L3_gnn_b):
    import numpy as np
    import concourse.bacc as bacc
    from concourse.bass_utils import run_bass_kernel_spmd

    def rows_first(w):
        return np.asarray(w).reshape(KT, 128, D).transpose(1, 0, 2).reshape(128, KT * D)

    mats = []
    for selfs, neighs in ((L0_gnn_Ws_self, L0_gnn_Ws_neigh), (L1_gnn_W_self, L1_gnn_W_neigh)):
        for l in range(3):
            mats += [rows_first(selfs[l]), rows_first(neighs[l])]
    mats.append(rows_first(np.asarray(L2_gnn_Ws).transpose(1, 0, 2).reshape(D, D)))
    mats += [rows_first(np.asarray(L3_gnn_W_self).T), rows_first(np.asarray(L3_gnn_W_neigh).T)]
    a_w = np.asarray(L2_gnn_a_w)
    arrays = {
        "x": np.ascontiguousarray(x),
        "src": np.ascontiguousarray(src),
        "dst": np.ascontiguousarray(dst),
        "weights": np.ascontiguousarray(np.stack(mats)),
        "biases": np.concatenate([np.asarray(L0_gnn_bs), np.asarray(L1_gnn_b), np.asarray(L2_gnn_Wb).reshape(1, D),
                                  np.asarray(L3_gnn_b).reshape(1, D)]),
        "attn": np.stack([np.ascontiguousarray(a_w[:, :DH]).reshape(D), np.ascontiguousarray(a_w[:, DH:]).reshape(D)]),
        "attn_b": np.ascontiguousarray(L2_gnn_a_b).reshape(1, HEADS),
    }
    nc = bacc.Bacc("TRN2", target_bir_lowering=False, num_devices=1)
    args = [nc.dram_tensor(k, a.shape, mybir.dt.from_np(a.dtype), kind="ExternalInput").ap() for k, a in arrays.items()]
    out = nc.dram_tensor("out", (N, D), F32, kind="ExternalOutput").ap()
    gnn_kernel(nc, *args, out)
    r = run_bass_kernel_spmd(nc, [arrays], core_ids=[0])
    return r.results[0]["out"]
```
